# Optimizing a Trainium2 kernel written in Bass

```python
import numpy as np
import jax
import jax.numpy as jnp

def _softmax(x, axis=-1):
    return jax.nn.softmax(x, axis=axis)

def _gelu(x):
    return jax.nn.gelu(x, approximate=True)

def _silu(x):
    return jax.nn.silu(x)

def _sigmoid(x):
    return jax.nn.sigmoid(x)

def _layernorm(x, axis=-1, eps=1e-05):
    m = jnp.mean(x, axis=axis, keepdims=True)
    v = jnp.var(x, axis=axis, keepdims=True)
    return (x - m) / jnp.sqrt(v + eps)

def _scatter_add(tgt, idx, src, axis=0):
    return tgt.at[idx].add(src)

def _segment_sum(src, seg, n):
    return jax.ops.segment_sum(src, seg, n)
kernel_name = 'mk_decoder_postln_d1_seqx_r4_20afd6'

def setup_inputs(seed: int=0):
    np.random.seed(seed)
    _w = jnp.asarray

    def _rec_inputs():
        import jax
        import jax.numpy as jnp
        _rk = jax.random.key(seed)
        x = -0.0002928 + 1 * jax.random.normal(jax.random.fold_in(_rk, 1), (2, 512, 256), jnp.float32)
        _lenS = 512 - jax.random.randint(jax.random.fold_in(_rk, 7), (2,), 0, max(1, 512 // 4) + 1, jnp.int32)
        _lenS2 = 1024 - jax.random.randint(jax.random.fold_in(_rk, 8), (2,), 0, max(1, 1024 // 4) + 1, jnp.int32)
        _ctx_1024P = jax.random.normal(jax.random.fold_in(_rk, 11), (2, 16, 256), jnp.float32)
        _ctx_1024c = jax.random.dirichlet(jax.random.fold_in(_rk, 511), 0.3 * jnp.ones((16,), jnp.float32), (2, 1024))
        _ctx_1024t = jnp.einsum('bsk,bkd->bsd', _ctx_1024c, _ctx_1024P)
        _ctx_1024t = _ctx_1024t * jax.lax.rsqrt(jnp.mean(jnp.square(_ctx_1024t)) + 1e-12) * 0.953939
        ctx_1024 = -1.39393e-06 + 0.999914 * (_ctx_1024t + 0.3 * jax.random.normal(jax.random.fold_in(_rk, 611), (2, 1024, 256), jnp.float32))
        _validS = jnp.arange(512)[None, :] < _lenS[:, None]
        _validS2 = jnp.arange(1024)[None, :] < _lenS2[:, None]
        _causal = jnp.tril(jnp.ones((512, 512), dtype=bool))
        mask_Bx1xSxS2_bk1 = jnp.broadcast_to(_validS2[:, None, None, :], (2, 1, 512, 1024))
        return (x, ctx_1024, mask_Bx1xSxS2_bk1)
    x, ctx_1024, mask_Bx1xSxS2_bk1 = _rec_inputs()

    def _L0_attn_setup():
        import jax, jax.numpy as jnp
        import numpy as np
        LN_EPS = 1e-05
        DENOM_EPS = 1e-06
        NUM_HEADS = 16

        def _layer_norm(x, gamma, beta):
            mu = jnp.mean(x, axis=-1, keepdims=True)
            var = jnp.mean(jnp.square(x - mu), axis=-1, keepdims=True)
            return (x - mu) * jax.lax.rsqrt(var + LN_EPS) * gamma + beta
        key = jax.random.key(seed)
        k1, k2, k3 = jax.random.split(key, 3)
        B, L, D = (4, 1024, 256)
        x = jax.random.normal(k1, (B, L, D), dtype=jnp.float32)
        gamma = jnp.ones((D,), dtype=jnp.float32)
        beta = jnp.zeros((D,), dtype=jnp.float32)
        Wqkv = jax.random.normal(k2, (D, 3 * D), dtype=jnp.float32) / np.sqrt(D)
        Wout = jax.random.normal(k3, (D, D), dtype=jnp.float32) / np.sqrt(D)
        return {'x': x, 'gamma': gamma, 'beta': beta, 'Wqkv': Wqkv, 'Wout': Wout}
    _L0_attn_all = _L0_attn_setup()
    _L0_attn_in = {k: v for k, v in _L0_attn_all.items() if k in ('gamma', 'beta', 'Wqkv', 'Wout')}
    del _L0_attn_all

    def _L0_xattn_setup():
        import jax, jax.numpy as jnp
        import numpy as np
        B, N, D, H = (2, 512, 256, 16)
        DH = D // H
        SCALE = DH ** (-0.5)

        def _heads(x, W, b):
            Bx, Nx, _ = x.shape
            return (x @ W + b).reshape(Bx, Nx, H, DH).transpose(0, 2, 1, 3)
        key = jax.random.key(seed)
        ks = jax.random.split(key, 12)
        s = 0.02
        q = jax.random.normal(ks[0], (B, N, D), jnp.float32)
        k = jax.random.normal(ks[1], (B, N, D), jnp.float32)
        v = jax.random.normal(ks[2], (B, N, D), jnp.float32)
        attn_mask = jax.random.randint(ks[3], (B, 1, N, N), 0, 2).astype(bool)
        Wq = jax.random.normal(ks[4], (D, D), jnp.float32) * s
        bq = jnp.zeros((D,), jnp.float32)
        Wk = jax.random.normal(ks[5], (D, D), jnp.float32) * s
        bk = jnp.zeros((D,), jnp.float32)
        Wv = jax.random.normal(ks[6], (D, D), jnp.float32) * s
        bv = jnp.zeros((D,), jnp.float32)
        Wp = jax.random.normal(ks[7], (D, D), jnp.float32) * s
        bp = jnp.zeros((D,), jnp.float32)
        return {'q': q, 'k': k, 'v': v, 'attn_mask': attn_mask, 'Wq': Wq, 'bq': bq, 'Wk': Wk, 'bk': bk, 'Wv': Wv, 'bv': bv, 'Wp': Wp, 'bp': bp}
    _L0_xattn_all = _L0_xattn_setup()
    _L0_xattn_in = {k: v for k, v in _L0_xattn_all.items() if k in ('Wq', 'bq', 'Wk', 'bk', 'Wv', 'bv', 'Wp', 'bp')}
    del _L0_xattn_all

    def _L0_ffn_setup():
        import jax, jax.numpy as jnp
        import numpy as np
        N_EMBD = 256
        EXPERT_SIZES = [(4, 256), (4, 512)]
        TOP_K = 2
        B, S = (1, 512)
        WIDTHS = []
        for count, size in EXPERT_SIZES:
            WIDTHS += [size] * count
        OFFSETS = np.concatenate([[0], np.cumsum(WIDTHS)]).astype(np.int64)
        E = len(WIDTHS)
        TOTAL_W = int(OFFSETS[-1])
        MAX_W = max(WIDTHS)

        def _stack_experts(w1, w2):
            W1e, W2e = ([], [])
            for e in range(E):
                off, wd = (int(OFFSETS[e]), WIDTHS[e])
                pad = MAX_W - wd
                W1e.append(jnp.pad(w1[:, off:off + wd], ((0, 0), (0, pad))))
                W2e.append(jnp.pad(w2[off:off + wd, :], ((0, pad), (0, 0))))
            return (jnp.stack(W1e), jnp.stack(W2e))
        key = jax.random.key(seed)
        k1, k2, k3, k4 = jax.random.split(key, 4)
        x = jax.random.normal(k1, (B, S, N_EMBD), jnp.float32)
        router_w = jax.random.normal(k2, (E, N_EMBD), jnp.float32) * 0.02
        w1 = jax.random.truncated_normal(k3, -3.0, 3.0, (N_EMBD, TOTAL_W), jnp.float32) * 0.02
        w2 = jax.random.truncated_normal(k4, -3.0, 3.0, (TOTAL_W, N_EMBD), jnp.float32) * 0.02
        return {'x': x, 'router_w': router_w, 'w1': w1, 'w2': w2}
    _L0_ffn_all = _L0_ffn_setup()
    _L0_ffn_in = {k: v for k, v in _L0_ffn_all.items() if k in ('router_w', 'w1', 'w2')}
    del _L0_ffn_all
    return {'x': x, 'ctx_1024': ctx_1024, 'mask_Bx1xSxS2_bk1': mask_Bx1xSxS2_bk1, 'L0_attn_gamma': _L0_attn_in['gamma'], 'L0_attn_beta': _L0_attn_in['beta'], 'L0_attn_Wqkv': _L0_attn_in['Wqkv'], 'L0_attn_Wout': _L0_attn_in['Wout'], 'L0_xattn_Wq': _L0_xattn_in['Wq'], 'L0_xattn_bq': _L0_xattn_in['bq'], 'L0_xattn_Wk': _L0_xattn_in['Wk'], 'L0_xattn_bk': _L0_xattn_in['bk'], 'L0_xattn_Wv': _L0_xattn_in['Wv'], 'L0_xattn_bv': _L0_xattn_in['bv'], 'L0_xattn_Wp': _L0_xattn_in['Wp'], 'L0_xattn_bp': _L0_xattn_in['bp'], 'L0_ffn_router_w': _L0_ffn_in['router_w'], 'L0_ffn_w1': _L0_ffn_in['w1'], 'L0_ffn_w2': _L0_ffn_in['w2']}

def reference(x, ctx_1024, mask_Bx1xSxS2_bk1, L0_attn_gamma, L0_attn_beta, L0_attn_Wqkv, L0_attn_Wout, L0_xattn_Wq, L0_xattn_bq, L0_xattn_Wk, L0_xattn_bk, L0_xattn_Wv, L0_xattn_bv, L0_xattn_Wp, L0_xattn_bp, L0_ffn_router_w, L0_ffn_w1, L0_ffn_w2):
    import jax
    import jax.numpy as jnp

    def _L0_attn_ref(x, gamma, beta, Wqkv, Wout):
        import jax, jax.numpy as jnp
        import numpy as np
        LN_EPS = 1e-05
        DENOM_EPS = 1e-06
        NUM_HEADS = 16

        def _layer_norm(x, gamma, beta):
            mu = jnp.mean(x, axis=-1, keepdims=True)
            var = jnp.mean(jnp.square(x - mu), axis=-1, keepdims=True)
            return (x - mu) * jax.lax.rsqrt(var + LN_EPS) * gamma + beta
        B, L, D = x.shape
        H = NUM_HEADS
        HD = D // H
        residual = x
        xn = _layer_norm(x, gamma, beta)
        qkv = (xn @ Wqkv).reshape(B, L, 3, H, HD)
        qkv = jnp.transpose(qkv, (2, 0, 3, 1, 4))
        q, k, v = (qkv[0], qkv[1], qkv[2])
        q = jax.nn.elu(q) + 1.0
        k = jax.nn.elu(k) + 1.0
        kv = jnp.einsum('bhld,bhle->bhde', k, v)
        qkv_out = jnp.einsum('bhld,bhde->bhle', q, kv)
        denom = jnp.einsum('bhld,bhd->bhl', q, k.sum(axis=2)) + DENOM_EPS
        out = qkv_out / denom[..., None]
        out = jnp.transpose(out, (0, 2, 1, 3)).reshape(B, L, D)
        return residual + out @ Wout

    def _L0_xattn_ref(q, k, v, attn_mask, Wq, bq, Wk, bk, Wv, bv, Wp, bp):
        import jax, jax.numpy as jnp
        import numpy as np
        B, N, D, H = (2, 512, 256, 16)
        DH = D // H
        SCALE = DH ** (-0.5)

        def _heads(x, W, b):
            Bx, Nx, _ = x.shape
            return (x @ W + b).reshape(Bx, Nx, H, DH).transpose(0, 2, 1, 3)
        qh = _heads(q, Wq, bq)
        kh = _heads(k, Wk, bk)
        vh = _heads(v, Wv, bv)
        attn_raw = jnp.einsum('bhqd,bhkd->bhqk', qh, kh) * SCALE
        attn = jnp.where(attn_mask, -jnp.inf, attn_raw)
        attn = jax.nn.softmax(attn, axis=-1)
        x = jnp.einsum('bhqk,bhkd->bhqd', attn, vh)
        x = x.transpose(0, 2, 1, 3).reshape(q.shape[0], q.shape[1], D)
        return x @ Wp + bp

    def _L0_ffn_ref(x, router_w, w1, w2):
        import jax, jax.numpy as jnp
        import numpy as np
        N_EMBD = 256
        EXPERT_SIZES = [(4, 256), (4, 512)]
        TOP_K = 2
        B, S = (1, 512)
        WIDTHS = []
        for count, size in EXPERT_SIZES:
            WIDTHS += [size] * count
        OFFSETS = np.concatenate([[0], np.cumsum(WIDTHS)]).astype(np.int64)
        E = len(WIDTHS)
        TOTAL_W = int(OFFSETS[-1])
        MAX_W = max(WIDTHS)

        def _stack_experts(w1, w2):
            W1e, W2e = ([], [])
            for e in range(E):
                off, wd = (int(OFFSETS[e]), WIDTHS[e])
                pad = MAX_W - wd
                W1e.append(jnp.pad(w1[:, off:off + wd], ((0, 0), (0, pad))))
                W2e.append(jnp.pad(w2[off:off + wd, :], ((0, pad), (0, 0))))
            return (jnp.stack(W1e), jnp.stack(W2e))
        b, s, d = x.shape
        xf = x.reshape(-1, d)
        logits = xf @ router_w.T
        probs = jax.nn.sigmoid(logits.astype(jnp.float32))
        topw, sel = jax.lax.top_k(probs, TOP_K)
        topw = topw / (topw.sum(-1, keepdims=True) + 1e-20)
        topw = topw.astype(x.dtype)
        onehot = sel[:, :, None] == jnp.arange(E)[None, None, :]
        combine = jnp.sum(topw[:, :, None] * onehot, axis=1)
        W1e, W2e = _stack_experts(w1, w2)
        h = jnp.einsum('td,edw->tew', xf, W1e)
        h = jnp.square(jax.nn.relu(h))
        y = jnp.einsum('tew,ewd->ted', h, W2e)
        out = jnp.einsum('ted,te->td', y, combine)
        return out.reshape(b, s, d)
    x = _layernorm(x + _L0_attn_ref(x, L0_attn_gamma, L0_attn_beta, L0_attn_Wqkv, L0_attn_Wout), axis=-1)
    x = _layernorm(x + _L0_xattn_ref(x, ctx_1024, ctx_1024, mask_Bx1xSxS2_bk1, L0_xattn_Wq, L0_xattn_bq, L0_xattn_Wk, L0_xattn_bk, L0_xattn_Wv, L0_xattn_bv, L0_xattn_Wp, L0_xattn_bp), axis=-1)
    x = _layernorm(x + _L0_ffn_ref(x, L0_ffn_router_w, L0_ffn_w1, L0_ffn_w2), axis=-1)
    return x

_drawn_inputs = setup_inputs


def setup_inputs(seed=0):
    import zlib

    import numpy as np

    out = dict(_drawn_inputs(seed))
    spreads = {'L0_attn_gamma': (1.0, 0.6),
     'L0_attn_beta': (0.0, 0.1),
     'L0_xattn_bq': (0.0, 0.8),
     'L0_xattn_bk': (0.0, 0.8),
     'L0_xattn_bv': (0.0, 0.1),
     'L0_xattn_bp': (0.0, 0.1)}
    factors = {'L0_xattn_Wq': 8.0, 'L0_xattn_Wk': 8.0}
    for name, (base, spread) in spreads.items():
        noise = np.random.default_rng([zlib.crc32(name.encode()), seed]).standard_normal(out[name].shape)
        drawn = base * np.exp(spread * noise) if base else spread * noise
        out[name] = jnp.asarray(drawn.astype(out[name].dtype))
    for name, factor in factors.items():
        out[name] = (out[name] * factor).astype(out[name].dtype)
    return out
```

```python
from contextlib import ExitStack

import numpy as np

import concourse.bass as bass
from concourse import mybir

ALU = mybir.AluOpType
ACT = mybir.ActivationFunctionType
AX = mybir.AxisListType
F32 = mybir.dt.float32
F32R = mybir.dt.float32r
BF16 = mybir.dt.bfloat16
I32 = mybir.dt.int32
U8 = mybir.dt.uint8
U16 = mybir.dt.uint16
U32 = mybir.dt.uint32

P = 128
B, S, D = 2, 512, 256
S2 = 1024
H, HD = 16, 16
NT = S // P
NC = D // P
STK = 64
HH = H // 2
NPR = HH // 2
E_ = 8
WIDTHS = [256] * 4 + [512] * 4
UNITS = [(e, k) for e in range(E_) for k in range(WIDTHS[e] // P)]
NU = len(UNITS)
LAST = {e: WIDTHS[e] // P - 1 for e in range(E_)}
SCALE = float(HD) ** -0.5
LN_EPS = 1e-5
DEN_EPS = 1e-6
ROOT_SEED = float(0x5f3759df)
MASKED = -1e30
NR = 6
NRAW = 3
NW = 3
NP = 8
ALL_KEYS = list(range(S2 // P))
LAST_KEYS = ALL_KEYS[-2:]
SKIPPED = (S2 // P - 2) * P
LAG = 4


def ring_plan(kts):
    order = []

    def put(who, *key):
        order.append((key, who))

    def linear_kv(b):
        for i in range(NT):
            put("dve", "akv", b, i)

    def linear_sums(b):
        for c in range(NC):
            put("dve", "sum", b, c)

    def linear_q(b):
        for c in range(NC):
            put("dve", "aq", b, c)

    def linear_out(b):
        for c in range(NC):
            put("dve", "den", b, c)
            put("dve", "num", b, c)

    def transposed(name, b):
        for c in range(NC):
            put("act", name, b, c)

    transposed("xnT", 0)
    transposed("xnT", 1)
    linear_kv(0)
    linear_sums(0)
    linear_q(0)
    linear_kv(1)
    linear_out(0)
    linear_sums(1)
    linear_q(1)
    linear_out(1)
    for b in range(B):
        for i in range(NT):
            put("dve", "ao", b, i)
    transposed("x1T", 0)
    transposed("x1T", 1)
    for b in range(B):
        for k in range(len(kts) // 2):
            put("dve", "mT", b, k)
        for f in range(2):
            j = 2 * b + f
            put("act", "cT", j, 0)
            for k in range(len(kts)):
                if k % 2 == 0 and k + 2 < len(kts):
                    put("act", "cT", j, k // 2 + 1)
                put("dve", "kv", j, k)
                if k:
                    put("act", "kT", j, k - 1)
            put("act", "kT", j, len(kts) - 1)
            for i in range(NT):
                put("dve", "q", j, i)
                if i:
                    put("act", "qT", j, i - 1)
            put("act", "qT", j, NT - 1)
            for i in range(NT):
                for h in range(HH):
                    for s in range(-(-len(kts) // 4)):
                        put("dve", "smax", j, i, h, s)
            for i in range(NT):
                put("act", "qT2", j, i)
            for g in range(2):
                for k in range(len(kts)):
                    for h in range(4):
                        put("act", "st", j, g, k, h)
                    if g and k == min(1, len(kts) - 1):
                        put("dve", "dn", j, 0)
            put("dve", "dn", j, 1)
        for i in range(NT):
            put("dve", "p", b, i)
        transposed("x2T", b)
    put("act", "route")
    first_h = len(order)
    for u in range(NU):
        for b in range(B):
            put("act", "h", u, b)
    tiles, readers, holds, counts = {}, {}, {}, {"act": 0, "dve": 0}
    for n, (key, who) in enumerate(order):
        bank = n % NR if n < first_h else (n - first_h) % 4
        tiles[key] = (bank, n + 1, holds.get(bank))
        holds[bank] = key
        counts[who] += 1
        readers[key] = (who, counts[who])
        if n == first_h - 1:
            before_y = {k: holds[k] for k in (4, 5)}
    return tiles, readers, before_y


def decoder_layer(nc, x, ctx, mask, gamma, beta, Wqkv, Wout, Wq, bq, Wk, bk, Wv, bv, Wp, bp,
                  router_w, w1, w2, out):
    with ExitStack() as stack:
        def sb(name, shape, dt=F32):
            return stack.enter_context(nc.sbuf_tensor(name, shape, dt))

        def sem(name):
            return stack.enter_context(nc.semaphore(name))

        m = {}
        m["ident"] = sb("ident", [P, P])
        m["identb"] = sb("identb", [P, P], BF16)
        m["blocks"] = sb("blocks", [P, P])
        m["spread"] = sb("spread", [P, P])
        m["iota8"] = sb("iota8", [P, E_])
        m["gam"] = sb("gam", [P, NC])
        m["bet"] = sb("bet", [P, NC])
        m["bq"] = sb("bqB", [P, D])
        m["bk"] = sb("bkB", [P, D])
        m["bv"] = sb("bvB", [P, D])
        m["rw"] = sb("rw", [P, NC, E_])
        for s in "HL":
            m["wqkv" + s] = sb("wqkv" + s, [P, NC, 3 * D], F32R)
            m["wout" + s] = sb("wout" + s, [P, NC, D], F32R)
            m["wq" + s] = sb("wq" + s, [P, NC, D], F32R)
            m["wkv" + s] = sb("wkv" + s, [P, NC, 2, 2, P], F32R)
            m["wp" + s] = sb("wp" + s, [P, H // 4, D], F32R)
            m["we" + s] = sb("we" + s, [P, NW, 2 * D], F32R)
        m["raw"] = sb("raw", [P, NRAW, 2 * D])
        m["xr"] = sb("xr", [P, B * NT, D])
        m["xtf"] = sb("xtf", [P, B, NC, S])
        m["xtH"] = sb("xtH", [P, B, NC, S], F32R)
        m["xtL"] = sb("xtL", [P, B, NC, S], F32R)
        m["kt"] = sb("kt", [P, NPR, S2], F32R)
        m["vx"] = sb("vx", [P, S2 // P, HH, 32])
        m["mk"] = sb("mk", [P, 2, HH, STK], F32R)
        m["mq"] = sb("mq", [P, NT, HH, STK], F32R)
        m["qt"] = sb("qt", [P, NPR, S], F32R)
        m["mu"] = sb("mu", [P, 2, S2], U8)
        m["share"] = sb("share", [P, 4096])
        m["pr"] = sb("pr", [P, NP, S])
        m["oxH"] = sb("oxH", [P, 4, S], F32R)
        m["oxL"] = sb("oxL", [P, 4, S], F32R)
        m["tmp"] = sb("tmp", [P, 4, S])
        m["kf"] = sb("kf", [P, 4, P])
        m["cx"] = sb("cx", [P, 2, 2, D])
        m["ctf"] = sb("ctf", [P, NC * 2 * P])
        m["cH"] = sb("cH", [P, NC, 2 * P], F32R)
        m["cL"] = sb("cL", [P, NC, 2 * P], F32R)
        m["st"] = sb("st", [P, NT, 6])
        m["mv"] = sb("mv", [P, NT, 2])
        m["rv"] = sb("rv", [P, 3, NT])
        m["mx"] = sb("mx", [P, NT, HH, 2])
        m["nm"] = sb("nm", [P, HH])
        m["big"] = sb("big", [P, HH])
        m["re"] = sb("re", [P, B * NT, E_])
        m["flag"] = sb("flag", [1, 1], I32)
        m["least"] = sb("least", [P, 2])
        m["top"] = sb("top", [P, B * NT, E_])
        m["idx"] = sb("idx", [P, B * NT, E_], U32)
        m["idxf"] = sb("idxf", [P, B * NT, E_])
        m["wsum"] = sb("wsum", [P, B * NT])
        m["hot"] = sb("hot", [P, E_])
        m["comb"] = sb("comb", [P, B * NT, E_])
        banks = [stack.enter_context(nc.psum_tensor(f"bank{i}", [P, 512], F32)) for i in range(8)]

        sems = {}
        for name in ("consts", "small", "w_split", "filled", "act_emptied", "dve_emptied",
                     "xn_ready", "xt_split", "k_exp", "q_exp", "ks_ready", "ot_split", "x1_ready",
                     "mb_ready", "ctx_split", "k_dup", "k_stacked", "q_stacked", "max_ready",
                     "pv_done", "pv_emptied", "ox_split", "x2_ready", "h_high", "h_split",
                     "y_step", "y_emptied", "out_ready", "stored", "dve_step", "pool_step",
                     "act_step", "biases", "rw_loaded", "wp_loaded", "wp_zero", "q_dup", "route_ready", "mask_loaded", "mask_least", "least_turned", "flag_ready"):
            sems[name] = sem(name)
        for name, n in (("x_loaded", B * NT), ("w_loaded", NRAW), ("mu_loaded", 2), ("cx_loaded", 2)):
            sems[name] = [sem(f"{name}{i}") for i in range(n)]

        io = dict(x=x, ctx=ctx, mask=mask, gamma=gamma, beta=beta, Wqkv=Wqkv, Wout=Wout, Wq=Wq, bq=bq,
                  Wk=Wk, bk=bk, Wv=Wv, bv=bv, Wp=Wp, bp=bp, router_w=router_w, w1=w1, w2=w2, out=out)
        emit(nc, io, m, banks, sems)


def emit(nc, io, m, banks, s):
    kts = K = KG = NS = SN = tiles = readers = before_y = None

    def attend_to(key_tiles):
        nonlocal kts, K, KG, NS, SN, tiles, readers, before_y
        kts = key_tiles
        K = len(kts)
        KG = K // 2
        NS = -(-K // 4)
        SN = min(K, 4) * P
        tiles, readers, before_y = ring_plan(kts)

    attend_to(ALL_KEYS)

    def either(eng, rest, *counters):
        eng.wait_ge(s["flag_ready"], 1)
        flag = eng.value_load(m["flag"][0:1, 0:1], min_val=0, max_val=1)
        start = [c[0] for c in counters]
        with eng.If(flag == 1):
            attend_to(LAST_KEYS)
            rest()
        for c, v in zip(counters, start):
            c[0] = v
        with eng.Else():
            attend_to(ALL_KEYS)
            rest()

    def bank(*key):
        return banks[tiles[key][0]]

    def filled(eng, *key):
        eng.wait_ge(s["filled"], tiles[key][1])

    def emptied(eng, *key):
        who, count = readers[key]
        eng.wait_ge(s[who + "_emptied"], count)

    pieces = ["wqkv0", "wqkv1", "wqkv2", "wout", "wq", "wkv0", "wkv1", "wp0", "wp1"]
    PIECE = {name: n + 1 for n, name in enumerate(pieces)}
    NSM = len(pieces)
    raw_jobs = pieces[:7] + [("unit", u) for u in range(NU)]

    def raw_slot(n):
        return n % NRAW, 16 * (n // NRAW + 1)

    share = m["share"]
    KA = share[:, 0:NT * D].rearrange("p (i d) -> p i d", i=NT)
    V1 = share[:, 1024:1024 + NT * NC * 130].rearrange("p (i c v) -> p i c v", i=NT, c=NC)
    QA = share[:, 2064:2064 + NC * S].rearrange("p (c t) -> p c t", c=NC)
    MB = share[:, 0:2048].bitcast(BF16).rearrange("p (i k) -> p i k", i=NT)
    MALL = share[:, 0:SKIPPED * B * S // P // 4].bitcast(U8)
    MBT = share[:, 2048:4096].bitcast(BF16).rearrange("p (k t) -> p k t", t=S)
    prf = m["pr"][:, :, :].rearrange("p a b -> p (a b)")
    XN = prf[:, 0:2048].rearrange("p (t d) -> p t d", t=B * NT)
    EK = prf[:, 2048:2560].rearrange("p (r d) -> p r d", r=2)
    EQ = prf[:, 2560:3584].rearrange("p (r t) -> p r t", r=2)
    KVM = prf[:, 3584:3840].rearrange("p (c v) -> p c v", c=NC)
    KSM = prf[:, 3840:4096].rearrange("p (c v) -> p c v", c=NC)
    qtf = m["qt"][:, :, :].rearrange("p a b -> p (a b)")
    HHI = qtf[:, 0:1024].rearrange("p (r t) -> p r t", r=2)
    HLO = qtf[:, 1024:2048].rearrange("p (r t) -> p r t", r=2)
    wpraw = m["tmp"][:, 0:2, :].rearrange("p a (q d) -> p (a q) d", q=2)

    def xt(part, b, c):
        return m["xt" + part][:, b, c, :]

    block = nc.Block()
    with block:
        @block.sync
        def _(sp):
            def load_raw(n):
                job = raw_jobs[n]
                slot, _ = raw_slot(n)
                done = s["w_loaded"][slot]
                if n >= NRAW:
                    k = n - NRAW
                    sp.wait_ge(s["w_split"], k + 1 if k < 7 else k + 3)
                dst = m["raw"][:, slot, :]
                if isinstance(job, tuple):
                    u = job[1]
                    sp.dma_start(dst[:, 0:D].rearrange("p (c n) -> p c n", c=NC),
                                 io["w1"][:, u * P:(u + 1) * P].rearrange("(c p) n -> p c n", p=P)).then_inc(done, 16)
                    sp.dma_start(dst[:, D:2 * D], io["w2"][u * P:(u + 1) * P, :]).then_inc(done, 16)
                elif job.startswith("wqkv"):
                    q = int(job[4])
                    sp.dma_start(dst.rearrange("p (c n) -> p c n", c=NC),
                                 io["Wqkv"][:, q * D:(q + 1) * D].rearrange("(c p) n -> p c n", p=P)).then_inc(done, 16)
                elif job in ("wout", "wq"):
                    w = io["Wout"] if job == "wout" else io["Wq"]
                    sp.dma_start(dst.rearrange("p (c n) -> p c n", c=NC),
                                 w.rearrange("(c p) n -> p c n", p=P)).then_inc(done, 16)
                else:
                    c = int(job[3])
                    for a, w in enumerate((io["Wk"], io["Wv"])):
                        sp.dma_start(dst.rearrange("p (f a n) -> p f a n", f=2, a=2)[:, :, a, :],
                                     w[c * P:(c + 1) * P, :].rearrange("p (f n) -> p f n", f=2)).then_inc(done, 16)

            sp.dma_start(MALL.rearrange("p (r k) -> p r k", k=SKIPPED),
                         io["mask"].rearrange("b o (p r) k -> (b o p) r k", r=B * S // P)[:, :, 0:SKIPPED]
                         ).then_inc(s["mask_loaded"], 16)
            for t in range(NT):
                sp.dma_start(m["xr"][:, t, :], io["x"][0, t * P:(t + 1) * P, :]).then_inc(s["x_loaded"][t], 16)
            with nc.allow_non_contiguous_dma("256 elements each, once"):
                for name in ("gamma", "beta"):
                    sp.dma_start(m[name[:3]][:, :], io[name].rearrange("(c p) -> p c", p=P)).then_inc(s["small"], 16)
            for n in range(NRAW):
                load_raw(n)
            for t in range(NT, B * NT):
                sp.dma_start(m["xr"][:, t, :],
                             io["x"][1, (t - NT) * P:(t - NT + 1) * P, :]).then_inc(s["x_loaded"][t], 16)
            sp.wait_ge(s["wp_zero"], 1)
            for a in range(4):
                sp.dma_start(wpraw[32 * a:32 * a + HD, :, :],
                             io["Wp"].rearrange("(q a e) d -> a e q d", a=4, e=HD)[a]).then_inc(s["wp_loaded"], 16)
            sp.dma_start(wpraw[HD:HD + 1, 0, :], io["bp"].rearrange("(a d) -> a d", a=1)).then_inc(s["wp_loaded"], 16)
            for n in range(NRAW, 7):
                load_raw(n)
            for name in ("bq", "bk", "bv"):
                sp.dma_start(m[name][:, :], io[name].rearrange("(a d) -> a d", a=1).broadcast_to([P, D])
                             ).then_inc(s["biases"], 16)
            with nc.allow_non_contiguous_dma("2048 elements, once"):
                for c in range(NC):
                    sp.dma_start(m["rw"][:, c, :], io["router_w"][:, c * P:(c + 1) * P].rearrange("e p -> p e")
                                 ).then_inc(s["rw_loaded"], 16)

            def load_ctx(n):
                j, g = n // KG, n % KG
                if n >= 2:
                    filled(sp, "cT", (n - 2) // KG, (n - 2) % KG)
                k0 = kts[2 * g]
                sp.dma_start(m["cx"][:, n % 2, :, :],
                             io["ctx"][j // 2, k0 * P:(k0 + 2) * P, :].rearrange("(k p) d -> p k d", p=P)
                             ).then_inc(s["cx_loaded"][n % 2], 16)

            def load_mask(n):
                b, i = n // NT, n % NT
                if n >= 2:
                    sp.wait_ge(s["mb_ready"], n - 1)
                sp.dma_start(m["mu"][:, n % 2, 0:K * P],
                             io["mask"][b, 0, i * P:(i + 1) * P, kts[0] * P:(kts[-1] + 1) * P]
                             ).then_inc(s["mu_loaded"][n % 2], 16)

            def rest():
                for b in range(B):
                    for i in range(NT):
                        load_mask(NT * b + i)
                    for n in range(2 * KG):
                        load_ctx(2 * KG * b + n)
                for n in range(7, 7 + NU):
                    load_raw(n)
                for t in range(B * NT):
                    sp.wait_ge(s["out_ready"], t + 1)
                    sp.dma_start(io["out"][t // NT, (t % NT) * P:(t % NT + 1) * P, :],
                                 m["xr"][:, t, :]).then_inc(s["stored"], 16)
                sp.wait_ge(s["stored"], 16 * B * NT)

            either(sp, rest)

        @block.gpsimd
        def _(pool):
            pool.memset(m["tmp"][:, 0:2, :], 0.0).then_inc(s["wp_zero"], 1)
            pool.memset(m["ident"][:, :], 0.0).then_inc(s["pool_step"], 1)
            pool.memset(m["blocks"][:, :], 1.0).then_inc(s["pool_step"], 1)
            pool.memset(m["spread"][:, :], 0.0).then_inc(s["pool_step"], 1)
            pool.wait_ge(s["pool_step"], 3)
            pool.affine_select(out=m["ident"][:, :], in_=m["ident"][:, :], compare_op=ALU.not_equal, fill=1.0,
                               base=0, pattern=[[-1, P]], channel_multiplier=1).then_inc(s["pool_step"], 1)
            v = m["blocks"][:, :].rearrange("p (a e) -> p a e", e=HD)
            pool.affine_select(out=v, in_=v, compare_op=ALU.is_ge, fill=0.0, base=0,
                               pattern=[[-HD, P // HD], [0, HD]], channel_multiplier=1).then_inc(s["pool_step"], 1)
            v = m["spread"][:, :].rearrange("p (a e) -> p a e", e=32)
            pool.affine_select(out=v, in_=v, compare_op=ALU.not_equal, fill=1.0, base=-HD,
                               pattern=[[-32, 4], [0, 32]], channel_multiplier=1).then_inc(s["pool_step"], 1)
            pool.wait_ge(s["pool_step"], 6)
            v = m["blocks"][:, :].rearrange("p (a e) -> p a e", e=HD)
            pool.affine_select(out=v, in_=v, compare_op=ALU.is_ge, fill=0.0, base=HD - 1,
                               pattern=[[HD, P // HD], [0, HD]], channel_multiplier=-1).then_inc(s["consts"], 1)
            pool.tensor_copy(m["identb"][:, :], m["ident"][:, :]).then_inc(s["consts"], 1)
            pool.iota(m["iota8"][:, :], pattern=[[1, E_]], base=0, channel_multiplier=0,
                      allow_small_or_imprecise_dtypes=True).then_inc(s["consts"], 1)
            pool.memset(m["vx"][:, :, :, HD:32], 0.0).then_inc(s["pool_step"], 1)
            pool.wait_ge(s["pool_step"], 7)
            pool.memset(m["vx"][:, :, :, HD:HD + 1], 1.0).then_inc(s["consts"], 1)

            splits = [0]

            def split(src, high, low):
                pool.tensor_copy(high, src).then_inc(s["pool_step"], 1)
                splits[0] += 1
                pool.wait_ge(s["pool_step"], 7 + splits[0])
                pool.tensor_tensor(low, src, high.bitcast(F32), ALU.subtract).then_inc(s["w_split"], 1)

            def split_raw(n):
                slot, count = raw_slot(n)
                two = sum(1 + (isinstance(j, tuple) or j.startswith("wkv")) for j in raw_jobs[slot:n + 1:NRAW])
                pool.wait_ge(s["w_loaded"][slot], 16 * two)
                src = m["raw"][:, slot, :]
                job = raw_jobs[n]
                if isinstance(job, tuple):
                    u = job[1]
                    if u >= NW:
                        pool.wait_ge(s["y_step"], B * (u - NW + 1))
                    split(src, m["weH"][:, u % NW, :], m["weL"][:, u % NW, :])
                elif job.startswith("wqkv"):
                    q = int(job[4])
                    split(src.rearrange("p (c n) -> p c n", c=NC), m["wqkvH"][:, :, q * D:(q + 1) * D],
                          m["wqkvL"][:, :, q * D:(q + 1) * D])
                elif job in ("wout", "wq"):
                    split(src.rearrange("p (c n) -> p c n", c=NC), m[job + "H"][:, :, :], m[job + "L"][:, :, :])
                else:
                    c = int(job[3])
                    v = src.rearrange("p (f a n) -> p f a n", f=2, a=2)
                    split(v, m["wkvH"][:, c, :, :, :], m["wkvL"][:, c, :, :, :])

            for n in range(7):
                split_raw(n)
            pool.wait_ge(s["wp_loaded"], 16 * 5)
            for a in range(2):
                split(wpraw[:, 2 * a:2 * a + 2, :], m["wpH"][:, 2 * a:2 * a + 2, :], m["wpL"][:, 2 * a:2 * a + 2, :])

            def mask_terms(n):
                b, i = n // NT, n % NT
                if n == 0:
                    filled(pool, "num", 1, 1)
                if n == NT:
                    pool.wait_ge(s["max_ready"], 2 * NT)
                pool.wait_ge(s["mu_loaded"][n % 2], 16 * (n // 2 + 1))
                pool.tensor_scalar(MB[:, i, 0:K * P], m["mu"][:, n % 2, 0:K * P], MASKED, None,
                                   ALU.mult).then_inc(s["mb_ready"], 1)

            def rest():
                for n in range(B * NT):
                    mask_terms(n)
                for n in range(7, 7 + NU):
                    split_raw(n)

            either(pool, rest, splits)

        @block.scalar
        def _(act):
            def evacuate(name, b, scale=None):
                for c in range(NC):
                    filled(act, name, b, c)
                    if scale:
                        act.activation(xt("f", b, c), bank(name, b, c)[:, :], ACT.Identity, bias=m["bet"][:, c:c + 1],
                                       scale=m["gam"][:, c:c + 1]).then_inc(s["act_emptied"], 1)
                    else:
                        act.activation(xt("f", b, c), bank(name, b, c)[:, :], ACT.Copy).then_inc(s["act_emptied"], 1)

            def linear_kv(b):
                for i in range(NT):
                    filled(act, "akv", b, i)
                    n = NT * b + i
                    if n >= 2:
                        emptied(act, "akv", (n - 2) // NT, (n - 2) % NT)
                    if b and i == 0:
                        filled(act, "sum", 0, NC - 1)
                    pt = bank("akv", b, i)
                    act.activation(EK[:, n % 2, :], pt[:, 0:D], ACT.Exp)
                    act.activation(V1[:, i, :, 0:P], pt[:, D:2 * D].rearrange("p (c v) -> p c v", c=NC),
                                   ACT.Copy).then_inc(s["k_exp"], 1)

            def linear_q(b):
                for c in range(NC):
                    filled(act, "aq", b, c)
                    if b:
                        emptied(act, "aq", 0, c)
                    act.activation(EQ[:, c, :], bank("aq", b, c)[:, :], ACT.Exp).then_inc(s["q_exp"], 1)

            act.wait_ge(s["small"], 32)
            evacuate("xnT", 0, True)
            evacuate("xnT", 1, True)
            linear_kv(0)
            linear_q(0)
            linear_kv(1)
            linear_q(1)
            evacuate("x1T", 0)
            evacuate("x1T", 1)

            def rest():
                units = [0]

                def attention(j):
                    def context(g):
                        filled(act, "cT", j, g)
                        n = KG * j + g
                        if n:
                            act.wait_ge(s["ctx_split"], n)
                        act.activation(m["ctf"][:, :], bank("cT", j, g)[:, :], ACT.Copy).then_inc(s["act_emptied"], 1)

                    def key_stack(k):
                        filled(act, "kT", j, k)
                        act.activation(m["kt"][:, :, k * P:(k + 1) * P],
                                       bank("kT", j, k)[:, :].rearrange("p (r k) -> p r k", r=NPR),
                                       ACT.Copy).then_inc(s["act_emptied"], 1)

                    def query_stack(name, i):
                        filled(act, name, j, i)
                        act.activation(m["qt"][:, :, i * P:(i + 1) * P],
                                       bank(name, j, i)[:, :].rearrange("p (r k) -> p r k", r=NPR),
                                       ACT.Copy).then_inc(s["act_emptied"], 1)

                    context(0)
                    for k in range(K):
                        if k % 2 == 0 and k + 2 < K:
                            context(k // 2 + 1)
                        if k:
                            key_stack(k - 1)
                    key_stack(K - 1)
                    for i in range(NT):
                        query_stack("qT", i)
                    for i in range(NT):
                        query_stack("qT2", i)

                    def gathered(g):
                        n = 2 * j + g
                        act.wait_ge(s["pv_done"], 4 * K * (n + 1))
                        if n >= 2:
                            act.wait_ge(s["ox_split"], n - 1)
                        act.activation(m["tmp"][:, n % 2, :], banks[6 + g][:, :], ACT.Copy).then_inc(s["pv_emptied"], 1)

                    for g in range(2):
                        for k in range(K):
                            for h in range(4):
                                filled(act, "st", j, g, k, h)
                                u = units[0]
                                if u >= NP:
                                    act.wait_ge(s["pv_done"], u - NP + 1)
                                act.activation(m["pr"][:, u % NP, :], bank("st", j, g, k, h)[:, :], ACT.Exp,
                                               scale=SCALE).then_inc(s["act_emptied"], 1)
                                units[0] += 1
                            if g and k == 0:
                                gathered(0)
                    gathered(1)

                for b in range(B):
                    attention(2 * b)
                    attention(2 * b + 1)
                    evacuate("x2T", b)

                filled(act, "route")
                act.activation(m["re"][:, :, :].rearrange("p t e -> p (t e)"), bank("route")[:, 0:B * NT * E_],
                               ACT.Exp, scale=-1.0).then_inc(s["act_emptied"], 1)
                for n in range(NU * B):
                    u, b = n // B, n % B
                    filled(act, "h", u, b)
                    if n >= 4:
                        act.wait_ge(s["h_split"], n - 3)
                    act.activation(m["pr"][:, n % 4, :], bank("h", u, b)[:, :], ACT.Relu).then_inc(s["act_emptied"], 1)
                    emptied(act, "h", u, b)
                    if n >= 2:
                        act.wait_ge(s["y_step"], n - 1)
                    act.activation(HHI[:, n % 2, :], m["pr"][:, n % 4, :], ACT.Square).then_inc(s["h_high"], 1)

            either(act, rest)

        @block.vector
        def _(dve):
            steps = [0]

            def chain(ins):
                steps[0] += 1
                ins.then_inc(s["dve_step"], 1)
                dve.wait_ge(s["dve_step"], steps[0])

            def statistics(i, src):
                chain(dve.bn_stats(m["st"][:, i, :], src))
                chain(dve.bn_aggr(m["mv"][:, i, :], m["st"][:, i, :]))

            def normalise_rows(src, dst, b, ready):
                v, y, a = m["rv"][:, 0, :], m["rv"][:, 1, :], m["rv"][:, 2, :]
                chain(dve.tensor_scalar(v, m["mv"][:, :, 1], LN_EPS, None, ALU.add))
                chain(dve.tensor_scalar(y.bitcast(I32), v.bitcast(I32), -0.5, ROOT_SEED, ALU.mult, ALU.add))
                for _ in range(3):
                    chain(dve.tensor_tensor(a, y, y, ALU.mult))
                    chain(dve.scalar_tensor_tensor(out=a, in0=a, scalar=-0.5, in1=v, op0=ALU.mult, op1=ALU.mult))
                    chain(dve.scalar_tensor_tensor(out=y, in0=a, scalar=1.5, in1=y, op0=ALU.add, op1=ALU.mult))
                for i in range(NT):
                    t = NT * b + i
                    dve.tensor_scalar(dst[:, t, :], src[:, t, :], m["mv"][:, i, 0:1], m["rv"][:, 1, i:i + 1],
                                      ALU.subtract, ALU.mult).then_inc(ready, 1)

            def split_rows(name, b):
                for c in range(NC):
                    emptied(dve, name, b, c)
                    chain(dve.tensor_copy(xt("H", b, c), xt("f", b, c)))
                    dve.tensor_tensor(xt("L", b, c), xt("f", b, c), xt("H", b, c).bitcast(F32),
                                      ALU.subtract).then_inc(s["xt_split"], 1)

            def linear_kv(b):
                for i in range(NT):
                    n = NT * b + i
                    dve.wait_ge(s["k_exp"], n + 1)
                    chain(dve.tensor_scalar(EK[:, n % 2, :], EK[:, n % 2, :], 1.0, None, ALU.min))
                    dve.scalar_tensor_tensor(out=KA[:, i, :], in0=bank("akv", b, i)[:, 0:D], scalar=0.0,
                                             in1=EK[:, n % 2, :], op0=ALU.max, op1=ALU.add
                                             ).then_inc(s["dve_emptied"], 1)

            def linear_sums(b):
                for c in range(NC):
                    filled(dve, "sum", b, c)
                    pt = bank("sum", b, c)
                    chain(dve.tensor_tensor(KVM[:, c, :], pt[:, 0:P], m["blocks"][:, :], ALU.mult))
                    dve.tensor_scalar(KSM[:, c, :], m["blocks"][:, :], pt[:, P:P + 1], None,
                                      ALU.mult).then_inc(s["dve_emptied"], 1)

            def linear_q(b):
                for c in range(NC):
                    dve.wait_ge(s["q_exp"], NC * b + c + 1)
                    chain(dve.tensor_scalar(EQ[:, c, :], EQ[:, c, :], 1.0, None, ALU.min))
                    dve.scalar_tensor_tensor(out=QA[:, c, :], in0=bank("aq", b, c)[:, :], scalar=0.0,
                                             in1=EQ[:, c, :], op0=ALU.max, op1=ALU.add
                                             ).then_inc(s["dve_emptied"], 1)

            def linear_out(b):
                for c in range(NC):
                    filled(dve, "den", b, c)
                    d, o = m["tmp"][:, 2, :], m["tmp"][:, 3, :]
                    ins = dve.tensor_scalar(d, bank("den", b, c)[:, :], DEN_EPS, None, ALU.add)
                    ins.then_inc(s["dve_emptied"], 1)
                    emptied(dve, "den", b, c)
                    chain(dve.reciprocal(d, d))
                    filled(dve, "num", b, c)
                    dve.tensor_tensor(o, bank("num", b, c)[:, :], d, ALU.mult).then_inc(s["dve_emptied"], 1)
                    emptied(dve, "num", b, c)
                    chain(dve.tensor_copy(m["oxH"][:, 2 * b + c, :], o))
                    dve.tensor_tensor(m["oxL"][:, 2 * b + c, :], o, m["oxH"][:, 2 * b + c, :].bitcast(F32),
                                      ALU.subtract).then_inc(s["ot_split"], 1)

            dve.wait_ge(s["mask_loaded"], 16)
            dve.tensor_reduce(m["least"][:, 0:1], MALL.bitcast(U16), AX.X, ALU.min).then_inc(s["mask_least"], 1)
            dve.wait_ge(s["least_turned"], 1)
            chain(dve.tensor_reduce(m["least"][0:1, 0:1], banks[7][0:1, 0:P], AX.X, ALU.min))
            dve.tensor_scalar(m["flag"][0:1, 0:1], m["least"][0:1, 0:1], 257.0, None,
                              ALU.is_equal).then_inc(s["flag_ready"], 1)
            dve.memset(V1[:, :, :, P:P + 1], 1.0).then_inc(s["ks_ready"], 1)
            dve.memset(m["mk"][:, :, :, 3 * HD:STK].bitcast(F32), 0.0)
            chain(dve.memset(m["mq"][:, :, :, 3 * HD:STK].bitcast(F32), 0.0))
            chain(dve.memset(m["mk"][:, :, :, 3 * HD:3 * HD + 2].bitcast(F32), 1.0))
            for b in range(B):
                for i in range(NT):
                    dve.wait_ge(s["x_loaded"][NT * b + i], 16)
                    statistics(i, m["xr"][:, NT * b + i, :])
                normalise_rows(m["xr"], XN, b, s["xn_ready"])
            split_rows("xnT", 0)
            split_rows("xnT", 1)
            dve.wait_ge(s["consts"], 4)
            linear_kv(0)
            linear_sums(0)
            linear_q(0)
            linear_kv(1)
            dve.wait_ge(s["w_split"], PIECE["wp1"])
            linear_out(0)
            linear_sums(1)
            linear_q(1)
            linear_out(1)
            for t in range(B * NT):
                filled(dve, "ao", t // NT, t % NT)
                ins = dve.scalar_tensor_tensor(out=m["xr"][:, t, :], in0=m["xr"][:, t, :], scalar=2.0,
                                               in1=bank("ao", t // NT, t % NT)[:, 0:D], op0=ALU.mult, op1=ALU.add)
                ins.then_inc(s["dve_emptied"], 1)
                emptied(dve, "ao", t // NT, t % NT)
                statistics(t % NT, m["xr"][:, t, :])
                if t % NT == NT - 1:
                    normalise_rows(m["xr"], m["xr"], t // NT, s["x1_ready"])
            split_rows("x1T", 0)
            split_rows("x1T", 1)
            dve.wait_ge(s["biases"], 48)

            def rest():
                kvs = [0]

                def attention(j):
                    b, f = j // 2, j % 2
                    cols = slice(f * P, (f + 1) * P)
                    for g in range(KG):
                        n = KG * j + g
                        emptied(dve, "cT", j, g)
                        if n:
                            filled(dve, "kv", (n - 1) // KG, 2 * ((n - 1) % KG) + 1)
                        chain(dve.tensor_copy(m["cH"][:, :, :].rearrange("p c k -> p (c k)"), m["ctf"][:, :]))
                        dve.tensor_tensor(m["cL"][:, :, :].rearrange("p c k -> p (c k)"), m["ctf"][:, :],
                                          m["cH"][:, :, :].rearrange("p c k -> p (c k)").bitcast(F32),
                                          ALU.subtract).then_inc(s["ctx_split"], 1)
                        for k in (2 * g, 2 * g + 1):
                            filled(dve, "kv", j, k)
                            pt = bank("kv", j, k)
                            kf = m["kf"][:, kvs[0] % 2, :]
                            if kvs[0] >= 2:
                                dve.wait_ge(s["k_stacked"], kvs[0] - 1)
                            dve.tensor_tensor(kf, pt[:, 0:P], m["bk"][:, cols], ALU.add)
                            dve.tensor_tensor(m["vx"][:, k, :, 0:HD], pt[:, P:2 * P].rearrange("p (h e) -> p h e", e=HD),
                                              m["bv"][:, cols].rearrange("p (h e) -> p h e", e=HD),
                                              ALU.add).then_inc(s["dve_emptied"], 1)
                            emptied(dve, "kv", j, k)
                            r = kvs[0] % 2
                            mk = m["mk"][:, r, :, :]
                            if kvs[0] >= 2:
                                n2 = kvs[0] - 2
                                filled(dve, "kT", n2 // K, n2 % K)
                            kv3 = kf.rearrange("p (h e) -> p h e", e=HD)
                            chain(dve.tensor_copy(mk[:, :, 0:HD], kv3))
                            dve.tensor_copy(mk[:, :, 2 * HD:3 * HD], kv3)
                            dve.tensor_tensor(mk[:, :, HD:2 * HD], kv3, mk[:, :, 0:HD].bitcast(F32),
                                              ALU.subtract).then_inc(s["k_stacked"], 1)
                            kvs[0] += 1
                    for i in range(NT):
                        filled(dve, "q", j, i)
                        qf = m["kf"][:, 2 + i % 2, :]
                        if NT * j + i >= 2:
                            dve.wait_ge(s["q_stacked"], NT * j + i - 1)
                        dve.tensor_tensor(qf, bank("q", j, i)[:, 0:P], m["bq"][:, cols],
                                          ALU.add).then_inc(s["dve_emptied"], 1)
                        emptied(dve, "q", j, i)
                        q3 = qf.rearrange("p (h e) -> p h e", e=HD)
                        mq = m["mq"][:, i, :, :]
                        if j:
                            filled(dve, "qT2", j - 1, i)
                        chain(dve.tensor_copy(mq[:, :, 0:HD], q3))
                        dve.tensor_copy(mq[:, :, HD:2 * HD], q3)
                        dve.tensor_tensor(mq[:, :, 2 * HD:3 * HD], q3, mq[:, :, 0:HD].bitcast(F32),
                                          ALU.subtract).then_inc(s["q_stacked"], 1)
                    dve.wait_ge(s["mb_ready"], NT * (b + 1))
                    for i in range(NT):
                        for h in range(HH):
                            for c in range(NS):
                                filled(dve, "smax", j, i, h, c)
                                pt = bank("smax", j, i, h, c)[:, 0:SN]
                                dve.tensor_tensor_reduce(pt, pt,
                                                         MB[:, i, c * SN:(c + 1) * SN], 1.0, -3e38, ALU.add, ALU.max,
                                                         m["mx"][:, i, h, c:c + 1]).then_inc(s["dve_emptied"], 1)
                        emptied(dve, "smax", j, i, HH - 1, NS - 1)
                        mx = m["mx"][:, i, :, 0]
                        if NS > 1:
                            chain(dve.tensor_tensor(mx, mx, m["mx"][:, i, :, 1], ALU.max))
                        chain(dve.tensor_scalar(m["big"][:, :], mx, MASKED / 2, 3e38, ALU.is_lt, ALU.mult))
                        chain(dve.scalar_tensor_tensor(out=m["nm"][:, :], in0=mx, scalar=-1.0, in1=m["big"][:, :],
                                                       op0=ALU.mult, op1=ALU.add))
                        mq = m["mq"][:, i, :, :]
                        chain(dve.tensor_copy(mq[:, :, 3 * HD], m["nm"][:, :]))
                        dve.tensor_tensor(mq[:, :, 3 * HD + 1], m["nm"][:, :], mq[:, :, 3 * HD].bitcast(F32),
                                          ALU.subtract).then_inc(s["max_ready"], 1)

                    def normalise(g):
                        n = 2 * j + g
                        filled(dve, "dn", j, g)
                        d, o = m["tmp"][:, 2, :], m["tmp"][:, 3, :]
                        dve.reciprocal(d, bank("dn", j, g)[:, :]).then_inc(s["dve_emptied"], 1)
                        emptied(dve, "dn", j, g)
                        chain(dve.tensor_tensor(o, m["tmp"][:, n % 2, :], d, ALU.mult))
                        if f == 0 and g == 0 and b:
                            filled(dve, "p", 0, NT - 1)
                        q = 2 * f + g
                        chain(dve.tensor_copy(m["oxH"][:, q, :], o))
                        dve.tensor_tensor(m["oxL"][:, q, :], o, m["oxH"][:, q, :].bitcast(F32),
                                          ALU.subtract).then_inc(s["ox_split"], 1)

                    normalise(0)
                    normalise(1)

                def mask_transposed(b):
                    for k in range(KG):
                        filled(dve, "mT", b, k)
                        dve.tensor_copy(MBT[:, 2 * k:2 * k + 2, :].rearrange("p k t -> p (k t)"),
                                        bank("mT", b, k)[:, :].bitcast(BF16)).then_inc(s["dve_emptied"], 1)

                for b in range(B):
                    mask_transposed(b)
                    attention(2 * b)
                    attention(2 * b + 1)
                    for i in range(NT):
                        t = NT * b + i
                        filled(dve, "p", b, i)
                        dve.tensor_tensor(m["xr"][:, t, :], m["xr"][:, t, :], bank("p", b, i)[:, 0:D],
                                          ALU.add).then_inc(s["dve_emptied"], 1)
                        emptied(dve, "p", b, i)
                        statistics(i, m["xr"][:, t, :])
                    normalise_rows(m["xr"], m["xr"], b, s["x2_ready"])
                    split_rows("x2T", b)

                emptied(dve, "route")
                chain(dve.tensor_scalar(m["re"][:, :, :], m["re"][:, :, :], 1.0, None, ALU.add))
                chain(dve.reciprocal(m["re"][:, :, :], m["re"][:, :, :]))
                for t in range(B * NT):
                    chain(dve.max(m["top"][:, t, :], m["re"][:, t, :]))
                    dve.max_index(m["idx"][:, t, :], m["top"][:, t, :], m["re"][:, t, :])
                chain(dve.tensor_tensor(m["wsum"][:, :], m["top"][:, :, 0], m["top"][:, :, 1], ALU.add))
                chain(dve.tensor_scalar(m["wsum"][:, :], m["wsum"][:, :], 1e-20, None, ALU.add))
                chain(dve.reciprocal(m["wsum"][:, :], m["wsum"][:, :]))
                chain(dve.tensor_copy(m["idxf"][:, :, :], m["idx"][:, :, :]))
                for k in range(2):
                    chain(dve.tensor_tensor(m["top"][:, :, k], m["top"][:, :, k], m["wsum"][:, :], ALU.mult))
                for t in range(B * NT):
                    chain(dve.tensor_scalar(m["hot"][:, :], m["iota8"][:, :], m["idxf"][:, t, 0:1],
                                            m["top"][:, t, 0:1], ALU.is_equal, ALU.mult))
                    chain(dve.tensor_scalar(m["comb"][:, t, :], m["iota8"][:, :], m["idxf"][:, t, 1:2],
                                            m["top"][:, t, 1:2], ALU.is_equal, ALU.mult))
                    chain(dve.tensor_tensor(m["comb"][:, t, :], m["comb"][:, t, :], m["hot"][:, :], ALU.add))

                def gather(e, b):
                    dve.wait_ge(s["y_step"], B * UNITS.index((e, LAST[e])) + b + 1)
                    for i in range(NT):
                        t = NT * b + i
                        dve.scalar_tensor_tensor(out=m["xr"][:, t, :],
                                                 in0=banks[4 + t // 2][:, (t % 2) * D:(t % 2 + 1) * D],
                                                 scalar=m["comb"][:, t, e:e + 1], in1=m["xr"][:, t, :],
                                                 op0=ALU.mult, op1=ALU.add).then_inc(s["y_emptied"], 1)

                due = []
                for n in range(NU * B):
                    u, b = n // B, n % B
                    low = m["pr"][:, 4 + n % 4, :]
                    emptied(dve, "h", u, b)
                    chain(dve.tensor_tensor(low, m["pr"][:, n % 4, :], m["pr"][:, n % 4, :], ALU.mult))
                    dve.wait_ge(s["h_high"], n + 1)
                    if n >= 2:
                        dve.wait_ge(s["y_step"], n - 1)
                    dve.tensor_tensor(HLO[:, n % 2, :], low, HHI[:, n % 2, :].bitcast(F32),
                                      ALU.subtract).then_inc(s["h_split"], 1)
                    if due and due[0][0] <= n:
                        gather(*due.pop(0)[1])
                    if UNITS[u][1] == LAST[UNITS[u][0]]:
                        due.append((n + 2, (UNITS[u][0], b)))
                for b in range(B):
                    gather(*due.pop(0)[1])
                    for i in range(NT):
                        t = NT * b + i
                        dve.wait_ge(s["y_emptied"], B * NT * (E_ - 1) + t + 1)
                        statistics(i, m["xr"][:, t, :])
                    normalise_rows(m["xr"], m["xr"], b, s["out_ready"])

            either(dve, rest, steps)

        @block.tensor
        def _(pe):
            order = [0]

            def claim(*key):
                bk, n, before = tiles[key]
                order[0] += 1
                assert n == order[0], key
                if before is not None:
                    emptied(pe, *before)
                return banks[bk]

            def three(out, pairs, stop=True, start=True):
                todo = [(a, b, x, y) for a, b in pairs for x, y in (("H", "H"), ("H", "L"), ("L", "H"))]
                for n, (a, b, x, y) in enumerate(todo):
                    ins = pe.matmul(out, a(x), b(y), start=start and n == 0, stop=stop and n == len(todo) - 1)
                return ins

            def transposed(name, b, src, ready, count):
                for c in range(NC):
                    pe.wait_ge(ready, count)
                    pt = claim(name, b, c)
                    for i in range(NT):
                        ins = pe.transpose(pt[:, i * P:(i + 1) * P], src[:, NT * b + i, c * P:(c + 1) * P],
                                           m["ident"][:, :])
                    ins.then_inc(s["filled"], 1)

            def xtile(b, c, i):
                return lambda part: m["xt" + part][:, b, c, i * P:(i + 1) * P]

            def linear_kv(b):
                pe.wait_ge(s["w_split"], PIECE["wqkv2"])
                pe.wait_ge(s["xt_split"], NC * (b + 1))
                for i in range(NT):
                    pt = claim("akv", b, i)
                    three(pt[:, :], [(xtile(b, c, i), lambda p, c=c: m["wqkv" + p][:, c, D:3 * D])
                                     for c in range(NC)]).then_inc(s["filled"], 1)

            def linear_sums(b):
                for i in range(NT):
                    emptied(pe, "akv", b, i)
                pe.wait_ge(s["ks_ready"], 1)
                for c in range(NC):
                    pt = claim("sum", b, c)
                    for i in range(NT):
                        ins = pe.matmul(pt[:, 0:P + 1], KA[:, i, c * P:(c + 1) * P], V1[:, i, c, 0:P + 1],
                                        start=(i == 0), stop=(i == NT - 1))
                    ins.then_inc(s["filled"], 1)

            def linear_q(b):
                for c in range(NC):
                    pt = claim("aq", b, c)
                    three(pt[:, :], [(lambda p, a=a, c=c: m["wqkv" + p][:, a, c * P:(c + 1) * P],
                                      lambda p, a=a: xt(p, b, a)) for a in range(NC)]).then_inc(s["filled"], 1)

            def linear_out(b):
                emptied(pe, "sum", b, NC - 1)
                emptied(pe, "aq", b, NC - 1)
                for c in range(NC):
                    for name, lhs in (("den", KSM), ("num", KVM)):
                        pt = claim(name, b, c)
                        pe.matmul(pt[:, :], lhs[:, c, :], QA[:, c, :], start=True,
                                  stop=True).then_inc(s["filled"], 1)

            pe.wait_ge(s["consts"], 4)
            pe.wait_ge(s["mask_least"], 1)
            pe.transpose(banks[7][0:1, 0:P], m["least"][:, 0:1], m["ident"][:, :]).then_inc(s["least_turned"], 1)
            transposed("xnT", 0, XN, s["xn_ready"], NT)
            transposed("xnT", 1, XN, s["xn_ready"], 2 * NT)
            linear_kv(0)
            linear_sums(0)
            linear_q(0)
            linear_kv(1)
            linear_out(0)
            linear_sums(1)
            linear_q(1)
            linear_out(1)
            pe.wait_ge(s["w_split"], PIECE["wout"])
            for b in range(B):
                pe.wait_ge(s["ot_split"], NC * (b + 1))
                for i in range(NT):
                    pt = claim("ao", b, i)
                    three(pt[:, 0:D], [(lambda p, c=c: m["ox" + p][:, 2 * b + c, i * P:(i + 1) * P],
                                        lambda p, c=c: m["wout" + p][:, c, :]) for c in range(NC)]
                          ).then_inc(s["filled"], 1)
            transposed("x1T", 0, m["xr"], s["x1_ready"], NT)
            transposed("x1T", 1, m["xr"], s["x1_ready"], 2 * NT)

            def rest():
                units = [0]
                waiting = []
                kvs = [0]
                ctxs = [0]

                def mask_transposed(b):
                    pe.wait_ge(s["mb_ready"], NT * (b + 1))
                    for k in range(KG):
                        pt = claim("mT", b, k)[:, :].bitcast(BF16)
                        for a in range(2):
                            for i in range(NT):
                                ins = pe.transpose(pt[:, a * S + i * P:a * S + (i + 1) * P],
                                                   MB[:, i, (2 * k + a) * P:(2 * k + a + 1) * P], m["identb"][:, :])
                        ins.then_inc(s["filled"], 1)

                def attention(j):
                    b, f = j // 2, j % 2
                    def turn_context(g):
                        n = ctxs[0]
                        pe.wait_ge(s["cx_loaded"][n % 2], 16 * (n // 2 + 1))
                        ctxs[0] += 1
                        pt = claim("cT", j, g)
                        for c in range(NC):
                            for k in range(2):
                                ins = pe.transpose(pt[:, (2 * c + k) * P:(2 * c + k + 1) * P],
                                                   m["cx"][:, n % 2, k, c * P:(c + 1) * P], m["ident"][:, :])
                        ins.then_inc(s["filled"], 1)
                    turn_context(0)
                    pe.wait_ge(s["w_split"], PIECE["wkv1"])

                    def turn_keys(k):
                        pe.wait_ge(s["k_stacked"], kvs[0] + 1)
                        pt = claim("kT", j, k)
                        for r in range(NPR):
                            ins = pe.transpose(pt[:, r * P:(r + 1) * P],
                                               m["mk"][:, kvs[0] % 2, 2 * r:2 * r + 2, :].rearrange("p a b -> p (a b)").bitcast(F32),
                                               m["ident"][:, :])
                        ins.then_inc(s["filled"], 1)
                        kvs[0] += 1

                    def turn_queries(name, i):
                        pt = claim(name, j, i)
                        for r in range(NPR):
                            ins = pe.transpose(pt[:, r * P:(r + 1) * P],
                                               m["mq"][:, i, 2 * r:2 * r + 2, :].rearrange("p a b -> p (a b)").bitcast(F32),
                                               m["ident"][:, :])
                        ins.then_inc(s["filled"], 1)

                    for k in range(K):
                        if k % 2 == 0 and k + 2 < K:
                            turn_context(k // 2 + 1)
                        pe.wait_ge(s["ctx_split"], KG * j + k // 2 + 1)
                        pt = claim("kv", j, k)
                        three(pt[:, 0:2 * P], [(lambda p, c=c: m["c" + p][:, c, (k % 2) * P:(k % 2 + 1) * P],
                                                lambda p, c=c: m["wkv" + p][:, c, f, :, :].rearrange("p a n -> p (a n)"))
                                               for c in range(NC)]).then_inc(s["filled"], 1)
                        if k:
                            turn_keys(k - 1)
                    turn_keys(K - 1)
                    pe.wait_ge(s["w_split"], PIECE["wq"])
                    pe.wait_ge(s["xt_split"], 2 * NC + NC * (b + 1) if b else 2 * NC + NC)
                    for i in range(NT):
                        pt = claim("q", j, i)
                        three(pt[:, 0:P], [(xtile(b, c, i), lambda p, c=c: m["wq" + p][:, c, f * P:(f + 1) * P])
                                           for c in range(NC)]).then_inc(s["filled"], 1)
                        if i:
                            pe.wait_ge(s["q_stacked"], NT * j + i)
                            turn_queries("qT", i - 1)
                    pe.wait_ge(s["q_stacked"], NT * (j + 1))
                    turn_queries("qT", NT - 1)
                    emptied(pe, "kT", j, K - 1)
                    for i in range(NT):
                        emptied(pe, "qT", j, i)
                        for h in range(HH):
                            rows = slice(STK * (h % 2), STK * (h % 2) + 3 * HD)
                            for c in range(NS):
                                pt = claim("smax", j, i, h, c)
                                pe.matmul(pt[:, 0:SN], m["qt"][rows, h // 2, i * P:(i + 1) * P],
                                          m["kt"][rows, h // 2, c * SN:(c + 1) * SN], start=True,
                                          stop=True).then_inc(s["filled"], 1)
                    for i in range(NT):
                        pe.wait_ge(s["max_ready"], NT * j + i + 1)
                        turn_queries("qT2", i)
                    emptied(pe, "qT2", j, NT - 1)

                    def gather(u, g, k, h):
                        emptied(pe, "st", j, g, k, h)
                        if k == 0 and h == 0 and 2 * j + g >= 2:
                            pe.wait_ge(s["pv_emptied"], 2 * j + g - 1)
                        ins = pe.matmul(banks[6 + g][32 * h:32 * h + 32, :], m["vx"][:, k, 4 * g + h, :],
                                        m["pr"][:, u % NP, :], start=(k == 0), stop=(k == K - 1))
                        ins.then_inc(s["pv_done"], 1)
                        return ins

                    def spread(g):
                        n = 2 * j + g
                        pe.wait_ge(s["pv_emptied"], n + 1)
                        pt = claim("dn", j, g)
                        pe.matmul(pt[:, :], m["spread"][:, :], m["tmp"][:, n % 2, :], start=True,
                                  stop=True).then_inc(s["filled"], 1)

                    for g in range(2):
                        for k in range(K):
                            for h in range(4):
                                head = 4 * g + h
                                rows = slice(STK * (head % 2), STK * (head % 2) + STK)
                                pt = claim("st", j, g, k, h)
                                pe.matmul(pt[:, :], m["kt"][rows, head // 2, k * P:(k + 1) * P],
                                          m["qt"][rows, head // 2, :], start=True, stop=False)
                                pe.matmul(pt[:, :], m["identb"][:, :], MBT[:, k, :], start=False,
                                          stop=True).then_inc(s["filled"], 1)
                                waiting.append((units[0], g, k, h))
                                units[0] += 1
                            if len(waiting) > LAG:
                                for _ in range(4):
                                    gather(*waiting.pop(0))
                            if g and k == min(1, K - 1):
                                spread(0)
                    while waiting:
                        gather(*waiting.pop(0))
                    spread(1)

                for b in range(B):
                    mask_transposed(b)
                    attention(2 * b)
                    attention(2 * b + 1)
                    pe.wait_ge(s["w_split"], PIECE["wp1"])
                    pe.wait_ge(s["ox_split"], 4 * (b + 1))
                    for i in range(NT):
                        pt = claim("p", b, i)
                        three(pt[:, 0:D], [(lambda p, q=q: m["ox" + p][:, q, i * P:(i + 1) * P],
                                            lambda p, q=q: m["wp" + p][:, q, :]) for q in range(4)]
                              ).then_inc(s["filled"], 1)
                    transposed("x2T", b, m["xr"], s["x2_ready"], NT * (b + 1))

                pe.wait_ge(s["rw_loaded"], 32)
                emptied(pe, "x2T", 1, 1)
                pt = claim("route")
                for b in range(B):
                    for i in range(NT):
                        for c in range(NC):
                            t = NT * b + i
                            ins = pe.matmul(pt[:, t * E_:(t + 1) * E_], m["xtf"][:, b, c, i * P:(i + 1) * P],
                                            m["rw"][:, c, :], start=(c == 0), stop=(c == NC - 1))
                ins.then_inc(s["filled"], 1)

                def expert_in(n):
                    u, b = n // B, n % B
                    pe.wait_ge(s["w_split"], NSM + u + 1)
                    pe.wait_ge(s["xt_split"], 4 * NC + NC * (b + 1))
                    pt = claim("h", u, b)
                    three(pt[:, :], [(lambda p, c=c: m["we" + p][:, u % NW, c * P:(c + 1) * P],
                                      lambda p, c=c: xt(p, b, c)) for c in range(NC)]).then_inc(s["filled"], 1)

                def expert_out(n):
                    u, b = n // B, n % B
                    e, k = UNITS[u]
                    pe.wait_ge(s["h_split"], n + 1)
                    if u == 0 and b == 0:
                        for kk in (4, 5):
                            emptied(pe, *before_y[kk])
                        pe.wait_ge(s["pv_emptied"], 8)
                    for i in range(NT):
                        t = NT * b + i
                        y = banks[4 + t // 2][:, (t % 2) * D:(t % 2 + 1) * D]
                        if k == 0 and e:
                            pe.wait_ge(s["y_emptied"], B * NT * (e - 1) + NT * b + 2 * (i // 2) + 2)
                        for p, (x_, y_) in enumerate((("H", "H"), ("H", "L"), ("L", "H"))):
                            ins = pe.matmul(y, {"H": HHI, "L": HLO}[x_][:, n % 2, i * P:(i + 1) * P],
                                            m["we" + y_][:, u % NW, D:2 * D],
                                            start=(k == 0 and p == 0 and t % 2 == 0), stop=(k == LAST[e] and p == 2),
                                            skip_group_check=True)
                    ins.then_inc(s["y_step"], 1)

                expert_in(0)
                for n in range(NU * B):
                    if n + 1 < NU * B:
                        expert_in(n + 1)
                    expert_out(n)

            either(pe, rest, order)


_INS = ["x", "ctx_1024", "mask_Bx1xSxS2_bk1", "L0_attn_gamma", "L0_attn_beta", "L0_attn_Wqkv", "L0_attn_Wout",
        "L0_xattn_Wq", "L0_xattn_bq", "L0_xattn_Wk", "L0_xattn_bk", "L0_xattn_Wv", "L0_xattn_bv",
        "L0_xattn_Wp", "L0_xattn_bp", "L0_ffn_router_w", "L0_ffn_w1", "L0_ffn_w2"]


def kernel(**inputs):
    import concourse.bacc as _bacc
    from concourse.bass_utils import run_bass_kernel_spmd as _run

    nc = _bacc.Bacc("TRN2", target_bir_lowering=False, num_devices=1)
    arrays, args = {}, []
    for name in _INS:
        a = np.ascontiguousarray(inputs[name])
        arrays[f"in_{name}"] = a
        args.append(nc.dram_tensor(f"in_{name}", a.shape, mybir.dt.from_np(a.dtype), kind="ExternalInput").ap())
    args.append(nc.dram_tensor("out", (B, S, D), F32, kind="ExternalOutput").ap())
    decoder_layer(nc, *args)
    r = _run(nc, [arrays], core_ids=[0])
    return r.results[0]["out"]
```

```python
from contextlib import ExitStack

import numpy as np

import concourse.bass as bass
from concourse import mybir

ALU = mybir.AluOpType
ACT = mybir.ActivationFunctionType
AX = mybir.AxisListType
F32 = mybir.dt.float32
F32R = mybir.dt.float32r
BF16 = mybir.dt.bfloat16
I32 = mybir.dt.int32
U8 = mybir.dt.uint8
U16 = mybir.dt.uint16
U32 = mybir.dt.uint32

P = 128
B, S, D = 2, 512, 256
S2 = 1024
H, HD = 16, 16
NT = S // P
NC = D // P
STK = 64
HH = H // 2
NPR = HH // 2
E_ = 8
WIDTHS = [256] * 4 + [512] * 4
LEAD = 6
UNITS = [(e, k) for e in range(E_) for k in range(WIDTHS[e] // P)]
NU = len(UNITS)
LAST = {e: WIDTHS[e] // P - 1 for e in range(E_)}
TASKS = [(u, 0) for u in range(LEAD)]
for _u in range(NU):
    TASKS += [(_u + LEAD, 0)] if _u + LEAD < NU else []
    TASKS.append((_u, 1))
SCALE = float(HD) ** -0.5
LN_EPS = 1e-5
DEN_EPS = 1e-6
ROOT_SEED = float(0x5f3759df)
MASKED = -1e30
NR = 6
NRAW = 4
NW = 9
NP = 8
ALL_KEYS = list(range(S2 // P))
LAST_KEYS = ALL_KEYS[-2:]
SKIPPED = (S2 // P - 2) * P


def passes(kts, q):
    return [2 * q, 2 * q + 1] if len(kts) == 2 else [q]


def expert_stages():
    out, finish = [("in", 0)], []
    for n, (u, b) in enumerate(TASKS):
        out += [("in", n + 1)] if n + 1 < len(TASKS) else []
        out += [("out", n)] + finish[0:1]
        finish = finish[1:]
        e, k = UNITS[u]
        if k == LAST[e]:
            out.append(("add", e, b))
        if u == NU - 1:
            parts = [("finish", b, part) for part in range(NT + 1)]
            finish = parts if b == 0 else finish + parts
    return out + finish


def schedule(kts):
    groups = [(g, k) for g in range(2) for k in range(len(kts))]

    def gather_pass(j, between):
        out, last = [], None
        for n, (g, k) in enumerate(groups):
            out.append(("probs", j, g, k))
            if last:
                out.append(("values", j, *last))
                if last == (0, len(kts) - 1):
                    out.append(("norm", j, 0))
            for step in between[n:n + 1] if n < len(groups) - 1 else between[n:]:
                out += step
            last = (g, k)
        return out + [("values", j, *last), ("norm", j, 1)]

    def maxima(j):
        return [("maxima", j, i) for i in range(NT)]

    experts = expert_stages()
    if len(kts) > 2:
        plan = [("round", n) for n in range(3, 8)] + [
            ("kv", 0), ("enter", 1), ("turn", "xnT", 1), ("sum", 0), ("q", 0), ("linear", 0), ("kv", 1),
            ("turn", "aoT", 0), ("attended", 0), ("sum", 1), ("q", 1), ("linear", 1), ("turn", "aoT", 1),
            ("attended", 1), ("turn", "x1T", 0), ("turn", "x1T", 1)]
        for j in range(2 * B):
            b = j // 2
            plan += [("mask", b)] if j % 2 == 0 else []
            for k in range(len(kts)):
                plan += [("context", j, k // 2)] if k % 2 == 0 else []
                plan += [("keys", j, k)] + ([("kturn", j, k - 1)] if k else [])
            plan += [("kturn", j, len(kts) - 1), ("queries", j)] + maxima(j) + [("queries2", j)]
            plan += gather_pass(j, [])
            if j % 2:
                plan += [("turn", "oxT", b), ("project", b), ("settle", b), ("turn", "x2T", b), ("route", b),
                         ("shares", b)]
        return plan + experts
    ahead = experts[:experts.index(("in", TASKS.index((0, 1))))]
    later = experts[len(ahead):]
    plan = [("kv", 0), ("q", 0), ("enter", 1), ("sum", 0), ("round", 3), ("turn", "xnT", 1), ("context", 0, 0),
            ("linear", 0), ("round", 4), ("kv", 1), ("turn", "aoT", 0), ("round", 5), ("keys", 0, 0), ("q", 1),
            ("attended", 0), ("kturn", 0, 0), ("sum", 1), ("keys", 0, 1), ("round", 6), ("linear", 1),
            ("turn", "x1T", 0), ("kturn", 0, 1), ("turn", "aoT", 1), ("queries", 0), ("round", 7),
            ("attended", 1), ("mask", 0), ("maxima", 0, 0), ("context", 1, 0), ("maxima", 0, 1),
            ("maxima", 0, 2), ("keys", 1, 0), ("maxima", 0, 3), ("turn", "x1T", 1), ("queries2", 0),
            ("kturn", 1, 0), ("queries", 1), ("keys", 1, 1), ("kturn", 1, 1), ("mask", 1)]
    for j in range(2 * B - 1):
        between = [[x] for x in maxima(j + 1)]
        if j == 2:
            for n, x in enumerate([("turn", "oxT", 0), ("project", 0), ("settle", 0), ("turn", "x2T", 0)]):
                between[n].append(x)
            between[-1] += [("route", 0), ("shares", 0)]
        plan += gather_pass(j, between) + [("queries2", j + 1)]
        plan += [("queries", j + 2)] if j + 2 < 2 * B else []
    cuts = [0, 0, 2, 4, 6, 8, 10, 12, len(ahead)]
    part = [ahead[x:y] for x, y in zip(cuts, cuts[1:])]
    plan += gather_pass(2 * B - 1, part[0:4])
    return plan + part[4] + [("turn", "oxT", 1)] + part[5] + [("project", 1)] + part[6] + [("settle", 1)] + part[
        7] + [("turn", "x2T", 1), ("route", 1)] + later[:1] + [("shares", 1)] + later[1:]


def ring_plan(kts):
    order = [(("xnT", 0, c), "act_emptied") for c in range(NC)]
    first_h = None

    def put(who, *key):
        order.append((key, who))

    for stage, *at in schedule(kts):
        if stage == "kv":
            for i in range(NT):
                put("dve_emptied", "akv", at[0], i)
        elif stage in ("sum", "q"):
            for c in range(NC):
                put("dve_emptied", {"sum": "sum", "q": "aq"}[stage], at[0], c)
        elif stage in ("linear", "attended", "project"):
            for i in range(NT):
                put("dve_emptied", {"linear": "nd", "attended": "ao", "project": "p"}[stage], at[0], i)
        elif stage == "turn":
            for c in range(NC):
                put({"xnT": "act_emptied", "aoT": "ox_split", "oxT": "ox_split"}.get(at[0], "xt_split"), *at, c)
        elif stage == "mask":
            for k in range(len(kts) // 2):
                put("dve_emptied", "mT", at[0], k)
        elif stage == "context":
            put("ctx_split", "cT", *at)
        elif stage == "keys":
            put("dve_emptied", "kv", *at)
        elif stage == "kturn":
            for j in passes(kts, at[0]):
                put("act_emptied", "kT", j, at[1])
        elif stage == "queries":
            for i in range(NT):
                put("dve_emptied", "q", at[0], i)
                if i:
                    put("act_emptied", "qT", at[0], i - 1)
            put("act_emptied", "qT", at[0], NT - 1)
        elif stage == "maxima":
            for h in range(HH):
                for c in range(-(-len(kts) // 4)):
                    put("dve_emptied", "smax", *at, h, c)
        elif stage == "queries2":
            for i in range(NT):
                put("act_emptied", "qT2", at[0], i)
        elif stage == "probs":
            for h in range(4):
                put("act_emptied", "st", *at, h)
        elif stage == "norm":
            put("dve_emptied", "oN", *at)
        elif stage == "route":
            put("act_emptied", "route", at[0])
        elif stage == "in":
            if at[0] == 0:
                first_h = len(order)
            put("act_emptied", "h", at[0])
    tiles, readers, holds = {}, {}, {}
    counts = {"act_emptied": 0, "dve_emptied": 0, "ox_split": 0, "xt_split": B * NC, "ctx_split": 0}
    for n, (key, who) in enumerate(order):
        bank = n % NR if n < first_h else (n - first_h) % 4
        tiles[key] = (bank, n + 1, holds.get(bank))
        holds[bank] = key
        counts[who] += 1
        readers[key] = (who, counts[who])
        if n == first_h - 1:
            before_y = {k: holds[k] for k in (4, 5)}
    return tiles, readers, before_y


def decoder_layer(nc, x, ctx, mask, gamma, beta, Wqkv, Wout, Wq, bq, Wk, bk, Wv, bv, Wp, bp,
                  router_w, w1, w2, out):
    with ExitStack() as stack:
        def sb(name, shape, dt=F32):
            return stack.enter_context(nc.sbuf_tensor(name, shape, dt))

        def sem(name):
            return stack.enter_context(nc.semaphore(name))

        m = {}
        m["ident"] = sb("ident", [P, P])
        m["identb"] = sb("identb", [P, P], BF16)
        m["identr"] = sb("identr", [P, P], F32R)
        m["blocks"] = sb("blocks", [P, P])
        m["iota8"] = sb("iota8", [P, E_])
        m["gam"] = sb("gam", [P, NC])
        m["bet"] = sb("bet", [P, NC])
        m["bq"] = sb("bqB", [P, D])
        m["bk"] = sb("bkB", [P, D])
        m["bv"] = sb("bvB", [P, D])
        m["bp"] = sb("bpB", [P, D])
        m["rw"] = sb("rw", [P, NC, E_])
        lin = sb("lin", [P, 8 * S], F32R)
        for n, s in enumerate("HL"):
            m["wqkv" + s] = lin[:, n * 6 * D:(n + 1) * 6 * D].rearrange("p (c n) -> p c n", c=NC)
            m["wout" + s] = lin[:, (12 + 2 * n) * D:(14 + 2 * n) * D].rearrange("p (c n) -> p c n", c=NC)
        qt = [sb("qt", [P, NPR, S], F32R)[:, :, :], lin[:, 0:4 * S].rearrange("p (r t) -> p r t", r=NPR)]
        mq = [sb("mq", [P, NT, HH, STK], F32R)[:, :, :, :],
              lin[:, 4 * S:8 * S].rearrange("p (i h k) -> p i h k", i=NT, h=HH)]
        m["qt"], m["mq"] = qt, mq
        for s in "HL":
            m["wq" + s] = sb("wq" + s, [P, NC, D], F32R)
            m["wkv" + s] = sb("wkv" + s, [P, NC, 2, 2, P], F32R)
            m["wp" + s] = sb("wp" + s, [P, NC, D], F32R)
            m["we" + s] = sb("we" + s, [P, 3, 2 * D], F32R)
        m["raw"] = sb("raw", [P, NRAW, 2 * D])
        m["xr"] = sb("xr", [P, B * NT, D])
        m["xtf"] = sb("xtf", [P, B, NC, S])
        m["xtH"] = sb("xtH", [P, B, NC, S], F32R)
        m["xtL"] = sb("xtL", [P, B, NC, S], F32R)
        m["kt"] = sb("kt", [P, NPR, S2], F32R)
        m["vx"] = sb("vx", [P, S2 // P, HH, 32])
        m["mk"] = sb("mk", [P, 2, HH, STK], F32R)
        m["mu"] = sb("mu", [P, 2, S2], U8)
        m["share"] = sb("share", [P, 4096])
        m["pr"] = sb("pr", [P, NP, S])
        m["oxH"] = sb("oxH", [P, NC, S], F32R)
        m["oxL"] = sb("oxL", [P, NC, S], F32R)
        m["mterm"] = sb("mterm", [P, 2048])
        m["tmp"] = sb("tmp", [P, 4, S])
        m["kf"] = sb("kf", [P, 4, P])
        m["cx"] = sb("cx", [P, 2, 2, D])
        m["cH"] = sb("cH", [P, NC, 2 * P], F32R)
        m["cL"] = sb("cL", [P, NC, 2 * P], F32R)
        m["st"] = sb("st", [P, NT, 6])
        m["mv"] = sb("mv", [P, NT, 2])
        m["rv"] = sb("rv", [P, 3, NT])
        m["mx"] = sb("mx", [P, NT, HH, 2])
        m["nm"] = sb("nm", [P, HH])
        m["big"] = sb("big", [P, HH])
        m["re"] = sb("re", [P, B * NT, E_])
        m["flag"] = sb("flag", [1, 1], I32)
        m["least"] = sb("least", [P, 2])
        m["top"] = sb("top", [P, B * NT, E_])
        m["idx"] = sb("idx", [P, B * NT, E_], U32)
        m["idxf"] = sb("idxf", [P, B * NT, E_])
        m["wsum"] = sb("wsum", [P, B * NT, 1])
        m["hot"] = sb("hot", [P, NT, E_])
        m["rd"] = sb("rd", [P, 2, H])
        m["comb"] = sb("comb", [P, B * NT, E_])
        banks = [stack.enter_context(nc.psum_tensor(f"bank{i}", [P, 512], F32)) for i in range(8)]

        sems = {}
        for name in ("consts", "small", "w_split", "filled", "act_emptied", "dve_emptied",
                     "xn_ready", "xt_split", "k_exp", "q_exp", "ks_ready", "w_high", "x1_biased", "x1_ready",
                     "mb_ready", "ctx_high", "ctx_split", "xt_high", "x2_copied", "k_stacked", "q_stacked", "max_ready",
                     "pv_done", "pv_emptied", "ox_split", "x2_ready", "h_high", "h_split",
                     "y_step", "y_emptied", "out_ready", "stored", "dve_step", "pool_step",
                     "biases", "rw_loaded", "mask_loaded", "mask_least", "least_turned", "flag_ready"):
            sems[name] = sem(name)
        for name, n in (("x_loaded", B * NT), ("w_loaded", NRAW), ("mu_loaded", 2), ("cx_loaded", 2)):
            sems[name] = [sem(f"{name}{i}") for i in range(n)]

        io = dict(x=x, ctx=ctx, mask=mask, gamma=gamma, beta=beta, Wqkv=Wqkv, Wout=Wout, Wq=Wq, bq=bq,
                  Wk=Wk, bk=bk, Wv=Wv, bv=bv, Wp=Wp, bp=bp, router_w=router_w, w1=w1, w2=w2, out=out)
        emit(nc, io, m, banks, sems)


def emit(nc, io, m, banks, s):
    kts = K = KG = NS = SN = tiles = readers = before_y = None

    def attend_to(key_tiles):
        nonlocal kts, K, KG, NS, SN, tiles, readers, before_y
        kts = key_tiles
        K = len(kts)
        KG = K // 2
        NS = -(-K // 4)
        SN = min(K, 4) * P
        tiles, readers, before_y = ring_plan(kts)

    attend_to(ALL_KEYS)

    def either(eng, rest, *counters):
        eng.wait_ge(s["flag_ready"], 1)
        flag = eng.value_load(m["flag"][0:1, 0:1], min_val=0, max_val=1)
        start = [c[0] for c in counters]
        with eng.If(flag == 1):
            attend_to(LAST_KEYS)
            rest()
        for c, v in zip(counters, start):
            c[0] = v
        with eng.Else():
            attend_to(ALL_KEYS)
            rest()

    def bank(*key):
        return banks[tiles[key][0]]

    def filled(eng, *key):
        eng.wait_ge(s["filled"], tiles[key][1])

    def emptied(eng, *key):
        who, count = readers[key]
        eng.wait_ge(s[who], count)

    pieces = ["wqkv1", "wqkv2", "wqkv0", "wkv0", "wkv1", "wout", "wq", "wp"]
    PIECE = {name: n + 1 for n, name in enumerate(pieces)}
    NSM = len(pieces)
    raw_jobs = pieces + [("unit", u) for u in range(NU)]

    def raw_slot(n):
        slot = n % NRAW
        return slot, 16 * sum(1 + (isinstance(job, tuple) or job.startswith("wkv"))
                              for job in raw_jobs[slot:n + 1:NRAW])

    def piece(part, name):
        if name.startswith("wqkv"):
            q = int(name[4])
            return m["wqkv" + part][:, :, q * D:(q + 1) * D]
        if name.startswith("wkv"):
            return m["wkv" + part][:, int(name[3]), :, :, :].rearrange("p f a n -> p f (a n)")
        return m[name + part][:, :, :]

    share = m["share"]
    KA = share[:, 0:NT * D].rearrange("p (i d) -> p i d", i=NT)
    V1 = share[:, 1024:1024 + NT * NC * 130].rearrange("p (i c v) -> p i c v", i=NT, c=NC)
    QA = share[:, 2064:2064 + NC * S].rearrange("p (c t) -> p c t", c=NC)
    MALL = share[:, 0:SKIPPED * B * S // P // 4].bitcast(U8)
    prf = m["pr"][:, :, :].rearrange("p a b -> p (a b)")
    XN = prf[:, 0:2048].rearrange("p (t d) -> p t d", t=B * NT)
    KVS = share[:, 3088:3088 + NC * 136].rearrange("p (c v) -> p c v", c=NC)
    qtf = m["qt"][0].rearrange("p a b -> p (a b)")
    HHI = qtf[:, 0:1024].rearrange("p (r t) -> p r t", r=2)
    HLO = qtf[:, 1024:2048].rearrange("p (r t) -> p r t", r=2)
    HLOW = m["mterm"][:, 0:2 * S].rearrange("p (r t) -> p r t", r=2)
    HID = m["xtf"][:, 0, :, :]
    RAW = m["tmp"]
    ON = m["tmp"][:, 2:4, :].rearrange("p a (i d) -> p (a i) d", i=2)

    def mask_term(b, i):
        if K > 2:
            return share[:, 0:2048].bitcast(BF16)[:, i * K * P:(i + 1) * K * P]
        return m["mterm"][:, 0:1024].bitcast(BF16)[:, (NT * b + i) * K * P:(NT * b + i + 1) * K * P]

    def mask_term_t(b, k):
        if K > 2:
            return m["mterm"][:, :].bitcast(BF16)[:, k * S:(k + 1) * S]
        return m["mterm"][:, 1024:2048].bitcast(BF16)[:, (K * b + k) * S:(K * b + k + 1) * S]

    def key_cols(j, k0, n=P):
        first = (j * K * P if K == 2 else 0) + k0 * P
        return slice(first, first + n)

    def value_tile(j, k):
        return (j * K if K == 2 else 0) + k

    def qslot(j):
        return j % 2 if K == 2 else 0

    def flat(part, name):
        return {"wkv": lambda a: a.rearrange("p c f a n -> p (c f a n)"),
                "wq": lambda a: a.rearrange("p c n -> p (c n)"),
                "c": lambda a: a.rearrange("p c k -> p (c k)")}[name](
                    m[name + part][:, :, :, :, :] if name == "wkv" else m[name + part][:, :, :])

    def expert_weights(part, u):
        slot = u % NW
        if slot < 3:
            return m["we" + part][:, slot, :]
        if slot == 3:
            return flat(part, "wq")
        if slot == 4:
            return flat(part, "c")
        if slot < 7:
            return flat(part, "wkv")[:, (slot - 5) * 2 * D:(slot - 4) * 2 * D]
        n = 2 * (slot - 7) + "HL".index(part)
        return m["mq"][0].rearrange("p i h k -> p (i h k)")[:, n * 2 * D:(n + 1) * 2 * D]

    def last_use(eng, slot):
        q = B if K == 2 else 2 * B
        if slot in (4, 5, 6):
            filled(eng, "kv", q - 1, K - 1)
        elif slot == 3:
            filled(eng, "q", 2 * B - 1, NT - 1)
        elif slot > 6:
            filled(eng, "qT2", 2 if K == 2 else 2 * B - 1, NT - 1)

    def xt(part, b, c):
        return m["xt" + part][:, b, c, :]

    block = nc.Block()
    with block:
        @block.sync
        def _(sp):
            def load_raw(n):
                job = raw_jobs[n]
                slot, _ = raw_slot(n)
                done = s["w_loaded"][slot]
                if n >= NRAW:
                    sp.wait_ge(s["w_split"], n - NRAW + 1)
                dst = m["raw"][:, slot, :]
                if isinstance(job, tuple):
                    u = job[1]
                    sp.dma_start(dst[:, 0:D].rearrange("p (c n) -> p c n", c=NC),
                                 io["w1"][:, u * P:(u + 1) * P].rearrange("(c p) n -> p c n", p=P)).then_inc(done, 16)
                    sp.dma_start(dst[:, D:2 * D], io["w2"][u * P:(u + 1) * P, :]).then_inc(done, 16)
                elif job.startswith("wqkv"):
                    q = int(job[4])
                    sp.dma_start(dst.rearrange("p (c n) -> p c n", c=NC),
                                 io["Wqkv"][:, q * D:(q + 1) * D].rearrange("(c p) n -> p c n", p=P)).then_inc(done, 16)
                elif job in ("wout", "wq", "wp"):
                    w = {"wout": io["Wout"], "wq": io["Wq"], "wp": io["Wp"]}[job]
                    sp.dma_start(dst.rearrange("p (c n) -> p c n", c=NC),
                                 w.rearrange("(c p) n -> p c n", p=P)).then_inc(done, 16)
                else:
                    c = int(job[3])
                    for a, w in enumerate((io["Wk"], io["Wv"])):
                        sp.dma_start(dst.rearrange("p (f a n) -> p f a n", f=2, a=2)[:, :, a, :],
                                     w[c * P:(c + 1) * P, :].rearrange("p (f n) -> p f n", f=2)).then_inc(done, 16)

            for t in range(NT):
                sp.dma_start(m["xr"][:, t, :], io["x"][0, t * P:(t + 1) * P, :]).then_inc(s["x_loaded"][t], 16)
            sp.dma_start(MALL.rearrange("p (r k) -> p r k", k=SKIPPED),
                         io["mask"].rearrange("b o (p r) k -> (b o p) r k", r=B * S // P)[:, :, 0:SKIPPED]
                         ).then_inc(s["mask_loaded"], 16)
            with nc.allow_non_contiguous_dma("256 elements each, once"):
                for name in ("gamma", "beta"):
                    sp.dma_start(m[name[:3]][:, :], io[name].rearrange("(c p) -> p c", p=P)).then_inc(s["small"], 16)
            for n in range(2):
                load_raw(n)
            for t in range(NT, B * NT):
                sp.dma_start(m["xr"][:, t, :],
                             io["x"][1, (t - NT) * P:(t - NT + 1) * P, :]).then_inc(s["x_loaded"][t], 16)
            for n in range(2, NRAW):
                load_raw(n)
            for name in ("bq", "bk", "bv", "bp"):
                sp.dma_start(m[name][:, :], io[name].rearrange("(a d) -> a d", a=1).broadcast_to([P, D])
                             ).then_inc(s["biases"], 16)
            for n in range(NRAW, NSM):
                load_raw(n)
            with nc.allow_non_contiguous_dma("2048 elements, once"):
                for c in range(NC):
                    sp.dma_start(m["rw"][:, c, :], io["router_w"][:, c * P:(c + 1) * P].rearrange("e p -> p e")
                                 ).then_inc(s["rw_loaded"], 16)

            def load_ctx(n):
                q, g = n // KG, n % KG
                if n >= 2:
                    filled(sp, "cT", (n - 2) // KG, (n - 2) % KG)
                k0 = kts[2 * g]
                sp.dma_start(m["cx"][:, n % 2, :, :],
                             io["ctx"][passes(kts, q)[0] // 2, k0 * P:(k0 + 2) * P, :].rearrange(
                                 "(k p) d -> p k d", p=P)).then_inc(s["cx_loaded"][n % 2], 16)

            def load_mask(n):
                b, i = n // NT, n % NT
                if n >= 2:
                    sp.wait_ge(s["mb_ready"], n - 1)
                sp.dma_start(m["mu"][:, n % 2, 0:K * P],
                             io["mask"][b, 0, i * P:(i + 1) * P, kts[0] * P:(kts[-1] + 1) * P]
                             ).then_inc(s["mu_loaded"][n % 2], 16)

            def rest():
                if K == 2:
                    for n in range(B):
                        load_ctx(n)
                for b in range(B):
                    for i in range(NT):
                        load_mask(NT * b + i)
                    for n in range(2 * KG if K > 2 else 0):
                        load_ctx(2 * KG * b + n)
                for n in range(NSM, NSM + NU):
                    load_raw(n)
                for t in range(B * NT):
                    sp.wait_ge(s["out_ready"], t + 1)
                    sp.dma_start(io["out"][t // NT, (t % NT) * P:(t % NT + 1) * P, :],
                                 m["xr"][:, t, :]).then_inc(s["stored"], 16)
                sp.wait_ge(s["stored"], 16 * B * NT)

            either(sp, rest)

        @block.gpsimd
        def _(pool):
            pool.memset(m["ident"][:, :], 0.0).then_inc(s["pool_step"], 1)
            pool.memset(m["blocks"][:, :], 1.0).then_inc(s["pool_step"], 1)
            pool.wait_ge(s["pool_step"], 2)
            pool.affine_select(out=m["ident"][:, :], in_=m["ident"][:, :], compare_op=ALU.not_equal, fill=1.0,
                               base=0, pattern=[[-1, P]], channel_multiplier=1).then_inc(s["pool_step"], 1)
            v = m["blocks"][:, :].rearrange("p (a e) -> p a e", e=HD)
            pool.affine_select(out=v, in_=v, compare_op=ALU.is_ge, fill=0.0, base=0,
                               pattern=[[-HD, P // HD], [0, HD]], channel_multiplier=1).then_inc(s["pool_step"], 1)
            pool.wait_ge(s["pool_step"], 4)
            v = m["blocks"][:, :].rearrange("p (a e) -> p a e", e=HD)
            pool.affine_select(out=v, in_=v, compare_op=ALU.is_ge, fill=0.0, base=HD - 1,
                               pattern=[[HD, P // HD], [0, HD]], channel_multiplier=-1).then_inc(s["consts"], 1)
            pool.tensor_copy(m["identb"][:, :], m["ident"][:, :]).then_inc(s["consts"], 1)
            pool.tensor_copy(m["identr"][:, :], m["ident"][:, :]).then_inc(s["consts"], 1)
            pool.iota(m["iota8"][:, :], pattern=[[1, E_]], base=0, channel_multiplier=0,
                      allow_small_or_imprecise_dtypes=True).then_inc(s["consts"], 1)
            pool.memset(m["vx"][:, :, :, HD:32], 0.0).then_inc(s["pool_step"], 1)
            pool.wait_ge(s["pool_step"], 5)
            pool.memset(m["vx"][:, :, :, HD:HD + 1], 1.0).then_inc(s["consts"], 1)

            for n, name in enumerate(pieces):
                pool.wait_ge(s["w_high"], n + 1)
                src = m["raw"][:, raw_slot(n)[0], :].rearrange("p (c n) -> p c n", c=2)
                pool.tensor_tensor(piece("L", name), src, piece("H", name).bitcast(F32),
                                   ALU.subtract).then_inc(s["w_split"], 1)

            def split_unit(u):
                slot, count = raw_slot(NSM + u)
                pool.wait_ge(s["w_loaded"][slot], count)
                if u >= NW:
                    pool.wait_ge(s["y_step"], TASKS.index((u - NW, 1)) + 1)
                else:
                    last_use(pool, u)
                src, high = m["raw"][:, slot, :], expert_weights("H", u)
                pool.tensor_copy(high, src).then_inc(s["pool_step"], 1)
                pool.wait_ge(s["pool_step"], 5 + u + 1)
                pool.tensor_tensor(expert_weights("L", u), src, high.bitcast(F32),
                                   ALU.subtract).then_inc(s["w_split"], 1)

            def mask_terms(n):
                b, i = n // NT, n % NT
                if n == 0 and K > 2:
                    filled(pool, "nd", B - 1, NT - 1)
                if n == NT and K > 2:
                    pool.wait_ge(s["max_ready"], 2 * NT)
                pool.wait_ge(s["mu_loaded"][n % 2], 16 * (n // 2 + 1))
                pool.tensor_scalar(mask_term(b, i), m["mu"][:, n % 2, 0:K * P], MASKED, None,
                                   ALU.mult).then_inc(s["mb_ready"], 1)

            def rest():
                for b in range(B):
                    for i in range(NT):
                        mask_terms(NT * b + i)
                    if b == 0:
                        pool.wait_ge(s["biases"], 64)
                        for t in range(B * NT):
                            filled(pool, "x1T", t // NT, NC - 1)
                            pool.tensor_tensor(m["xr"][:, t, :], m["xr"][:, t, :], m["bp"][:, :],
                                               ALU.add).then_inc(s["x1_biased"], 1)
                for u in range(NU):
                    split_unit(u)

            either(pool, rest)

        @block.scalar
        def _(act):
            def evacuate(name, b):
                for c in range(NC):
                    filled(act, name, b, c)
                    pt = bank(name, b, c)[:, :]
                    if name == "xnT":
                        act.activation(xt("f", b, c), pt, ACT.Identity, bias=m["bet"][:, c:c + 1],
                                       scale=m["gam"][:, c:c + 1]).then_inc(s["act_emptied"], 1)
                        continue
                    if name == "x2T":
                        act.activation(xt("f", b, c), pt, ACT.Copy).then_inc(s["x2_copied"], 1)
                    high = xt("H", b, c)
                    if name in ("aoT", "oxT"):
                        high = m["oxH"][:, c, :]
                        before = {("aoT", 1): ("ao", 0), ("oxT", 0): ("ao", 1), ("oxT", 1): ("p", 0)}
                        if (name, b) in before and c == 0:
                            filled(act, *before[name, b], NT - 1)
                    act.activation(high, pt, ACT.Copy).then_inc(s["xt_high"], 1)

            def linear_kv(b):
                for i in range(NT):
                    filled(act, "akv", b, i)
                    n = NT * b + i
                    if b and i == 0:
                        filled(act, "sum", 0, NC - 1)
                    if n == 0:
                        act.wait_ge(s["ks_ready"], 1)
                    pt = bank("akv", b, i)
                    act.activation(KA[:, i, :], pt[:, 0:D], ACT.Exp)
                    act.activation(V1[:, i, :, 0:P], pt[:, D:2 * D].rearrange("p (c v) -> p c v", c=NC),
                                   ACT.Copy).then_inc(s["k_exp"], 1)

            def linear_q(b):
                for c in range(NC):
                    filled(act, "aq", b, c)
                    if b:
                        filled(act, "nd", 0, NT - 1)
                    act.activation(QA[:, c, :], bank("aq", b, c)[:, :], ACT.Exp).then_inc(s["q_exp"], 1)

            def round_piece(n):
                slot, count = raw_slot(n)
                act.wait_ge(s["w_loaded"][slot], count)
                act.activation(piece("H", pieces[n]), m["raw"][:, slot, :].rearrange("p (c n) -> p c n", c=2),
                               ACT.Copy).then_inc(s["w_high"], 1)

            for n in range(2):
                round_piece(n)
            act.wait_ge(s["small"], 32)
            evacuate("xnT", 0)
            round_piece(2)

            def rest():
                units = [0]
                gathered = [0]

                def context(q, g):
                    filled(act, "cT", q, g)
                    n = KG * q + g
                    if n:
                        filled(act, "kv", (n - 1) // KG, 2 * ((n - 1) % KG) + 1)
                    act.activation(flat("H", "c"), bank("cT", q, g)[:, :], ACT.Copy).then_inc(s["ctx_high"], 1)

                def key_stacks(q, k):
                    for j in passes(kts, q):
                        filled(act, "kT", j, k)
                        act.activation(m["kt"][:, :, key_cols(j, k)],
                                       bank("kT", j, k)[:, :].rearrange("p (r k) -> p r k", r=NPR),
                                       ACT.Copy).then_inc(s["act_emptied"], 1)

                def query_stacks(name, j):
                    for i in range(NT):
                        filled(act, name, j, i)
                        act.activation(m["qt"][qslot(j)][:, :, i * P:(i + 1) * P],
                                       bank(name, j, i)[:, :].rearrange("p (r k) -> p r k", r=NPR),
                                       ACT.Copy).then_inc(s["act_emptied"], 1)

                def probs(j, g, k):
                    for h in range(4):
                        filled(act, "st", j, g, k, h)
                        u = units[0]
                        if u >= NP:
                            act.wait_ge(s["pv_done"], u - NP + 1)
                        act.activation(m["pr"][:, u % NP, :], bank("st", j, g, k, h)[:, :], ACT.Exp,
                                       scale=SCALE).then_inc(s["act_emptied"], 1)
                        units[0] += 1

                def norm(j, g):
                    n = gathered[0]
                    act.wait_ge(s["pv_done"], 4 * K * (n + 1))
                    if n >= 2:
                        filled(act, "oN", (n - 2) // 2, (n - 2) % 2)
                    act.activation(RAW[:, n % 2, :], banks[6 + g][:, :], ACT.Copy).then_inc(s["pv_emptied"], 1)
                    gathered[0] += 1

                def round_hidden(n):
                    filled(act, "h", n)
                    if n >= 2:
                        act.wait_ge(s["h_split"], n - 1)
                    act.activation(HID[:, n % 2, :], bank("h", n)[:, :], ACT.Relu).then_inc(s["act_emptied"], 1)
                    emptied(act, "h", n)
                    if n >= 2:
                        act.wait_ge(s["y_step"], n - 1)
                    else:
                        filled(act, "st", 2 if K == 2 else 2 * B - 1, 1, K - 1, 3)
                    act.activation(HHI[:, n % 2, :], HID[:, n % 2, :], ACT.Square).then_inc(s["h_high"], 1)

                def route(b):
                    filled(act, "route", b)
                    act.activation(m["re"][:, NT * b:NT * (b + 1), :].rearrange("p t e -> p (t e)"),
                                   bank("route", b)[:, 0:NT * E_], ACT.Exp, scale=-1.0).then_inc(s["act_emptied"], 1)

                for stage, *at in schedule(kts):
                    if stage == "kv":
                        linear_kv(*at)
                    elif stage == "q":
                        linear_q(*at)
                    elif stage == "turn":
                        evacuate(*at)
                    elif stage == "round":
                        round_piece(*at)
                    elif stage == "context":
                        context(*at)
                    elif stage == "kturn":
                        key_stacks(*at)
                    elif stage == "queries":
                        query_stacks("qT", *at)
                    elif stage == "queries2":
                        query_stacks("qT2", *at)
                    elif stage == "probs":
                        probs(*at)
                    elif stage == "norm":
                        norm(*at)
                    elif stage == "route":
                        route(*at)
                    elif stage == "in":
                        round_hidden(*at)

            either(act, rest)

        @block.vector
        def _(dve):
            steps = [0]
            turns = [0]

            def chain(ins):
                steps[0] += 1
                ins.then_inc(s["dve_step"], 1)
                dve.wait_ge(s["dve_step"], steps[0])

            def statistics(i, src):
                chain(dve.bn_stats(m["st"][:, i, :], src))
                chain(dve.bn_aggr(m["mv"][:, i, :], m["st"][:, i, :]))

            def normalise_rows(src, dst, b, ready):
                v, y, a = m["rv"][:, 0, :], m["rv"][:, 1, :], m["rv"][:, 2, :]
                chain(dve.tensor_scalar(v, m["mv"][:, :, 1], LN_EPS, None, ALU.add))
                chain(dve.tensor_scalar(y.bitcast(I32), v.bitcast(I32), -0.5, ROOT_SEED, ALU.mult, ALU.add))
                for _ in range(3):
                    chain(dve.tensor_tensor(a, y, y, ALU.mult))
                    chain(dve.scalar_tensor_tensor(out=a, in0=a, scalar=-0.5, in1=v, op0=ALU.mult, op1=ALU.mult))
                    chain(dve.scalar_tensor_tensor(out=y, in0=a, scalar=1.5, in1=y, op0=ALU.add, op1=ALU.mult))
                for i in range(NT):
                    t = NT * b + i
                    dve.tensor_scalar(dst[:, t, :], src[:, t, :], m["mv"][:, i, 0:1], m["rv"][:, 1, i:i + 1],
                                      ALU.subtract, ALU.mult).then_inc(ready, 1)

            def split_rows(name, b):
                for c in range(NC):
                    if name == "xnT":
                        emptied(dve, name, b, c)
                        chain(dve.tensor_copy(xt("H", b, c), xt("f", b, c)))
                        dve.tensor_tensor(xt("L", b, c), xt("f", b, c), xt("H", b, c).bitcast(F32),
                                          ALU.subtract).then_inc(s["xt_split"], 1)
                        continue
                    turns[0] += 1
                    dve.wait_ge(s["xt_high"], turns[0])
                    if name in ("aoT", "oxT"):
                        high, low, done = m["oxH"][:, c, :], m["oxL"][:, c, :], s["ox_split"]
                    else:
                        high, low, done = xt("H", b, c), xt("L", b, c), s["xt_split"]
                    dve.tensor_tensor(low, bank(name, b, c)[:, :], high.bitcast(F32), ALU.subtract).then_inc(done, 1)

            def linear_kv(b):
                for i in range(NT):
                    dve.wait_ge(s["k_exp"], NT * b + i + 1)
                    chain(dve.tensor_scalar(KA[:, i, :], KA[:, i, :], 1.0, None, ALU.min))
                    dve.scalar_tensor_tensor(out=KA[:, i, :], in0=bank("akv", b, i)[:, 0:D], scalar=0.0,
                                             in1=KA[:, i, :], op0=ALU.max, op1=ALU.add
                                             ).then_inc(s["dve_emptied"], 1)

            def linear_sums(b):
                if b:
                    filled(dve, "nd", 0, NT - 1)
                for c in range(NC):
                    filled(dve, "sum", b, c)
                    pt = bank("sum", b, c)
                    dve.tensor_tensor(KVS[:, c, 0:P], pt[:, 0:P], m["blocks"][:, :], ALU.mult)
                    dve.tensor_scalar(KVS[:, c, P:P + HH],
                                      m["blocks"][:, :].rearrange("p (h e) -> p h e", e=HD)[:, :, 0],
                                      pt[:, P:P + 1], None, ALU.mult).then_inc(s["dve_emptied"], 1)

            def linear_q(b):
                for c in range(NC):
                    dve.wait_ge(s["q_exp"], NC * b + c + 1)
                    chain(dve.tensor_scalar(QA[:, c, :], QA[:, c, :], 1.0, None, ALU.min))
                    dve.scalar_tensor_tensor(out=QA[:, c, :], in0=bank("aq", b, c)[:, :], scalar=0.0,
                                             in1=QA[:, c, :], op0=ALU.max, op1=ALU.add
                                             ).then_inc(s["dve_emptied"], 1)

            def linear_out(b):
                if b:
                    filled(dve, "aoT", 0, NC - 1)
                for i in range(NT):
                    filled(dve, "nd", b, i)
                    pt = bank("nd", b, i)[:, 0:NC * 136].rearrange("p (c v) -> p c v", c=NC)
                    rd = m["rd"][:, i % 2, :].rearrange("p (c h) -> p c h", c=NC)
                    chain(dve.tensor_scalar(rd, pt[:, :, P:P + HH], DEN_EPS, None, ALU.add))
                    chain(dve.reciprocal(rd, rd))
                    dve.tensor_tensor(ON[:, i, :].rearrange("p (c h e) -> p c h e", c=NC, e=HD),
                                      pt[:, :, 0:P].rearrange("p c (h e) -> p c h e", e=HD),
                                      rd.unsqueeze(3).broadcast_to([P, NC, HH, HD]),
                                      ALU.mult).then_inc(s["dve_emptied"], 1)

            chain(dve.memset(m["mk"][:, :, :, 3 * HD:STK].bitcast(F32), 0.0))
            dve.memset(m["mq"][0][:, :, :, 3 * HD:STK].bitcast(F32), 0.0)
            chain(dve.memset(m["mk"][:, :, :, 3 * HD:3 * HD + 2].bitcast(F32), 1.0))

            def enter(b):
                for i in range(NT):
                    dve.wait_ge(s["x_loaded"][NT * b + i], 16)
                    statistics(i, m["xr"][:, NT * b + i, :])
                normalise_rows(m["xr"], XN, b, s["xn_ready"])

            enter(0)
            dve.wait_ge(s["mask_loaded"], 16)
            dve.tensor_reduce(m["least"][:, 0:1], MALL.bitcast(U16), AX.X, ALU.min).then_inc(s["mask_least"], 1)
            split_rows("xnT", 0)
            dve.wait_ge(s["least_turned"], 1)
            chain(dve.tensor_reduce(m["least"][0:1, 0:1], banks[7][0:1, 0:P], AX.X, ALU.min))
            dve.tensor_scalar(m["flag"][0:1, 0:1], m["least"][0:1, 0:1], 257.0, None,
                              ALU.is_equal).then_inc(s["flag_ready"], 1)
            dve.memset(V1[:, :, :, P:P + 1], 1.0).then_inc(s["ks_ready"], 1)
            dve.wait_ge(s["consts"], 5)

            def attended(b):
                for i in range(NT):
                    t = NT * b + i
                    filled(dve, "ao", b, i)
                    dve.scalar_tensor_tensor(out=m["xr"][:, t, :], in0=m["xr"][:, t, :], scalar=2.0,
                                             in1=bank("ao", b, i)[:, 0:D], op0=ALU.mult, op1=ALU.add
                                             ).then_inc(s["dve_emptied"], 1)
                    emptied(dve, "ao", b, i)
                    statistics(i, m["xr"][:, t, :])
                normalise_rows(m["xr"], m["xr"], b, s["x1_ready"])

            def mask_transposed(b):
                for k in range(KG):
                    filled(dve, "mT", b, k)
                    for a in range(2):
                        ins = dve.tensor_copy(mask_term_t(b, 2 * k + a),
                                              bank("mT", b, k)[:, :].bitcast(BF16)[:, a * S:(a + 1) * S])
                    ins.then_inc(s["dve_emptied"], 1)

            def rest():
                kvs = [0]
                stacks = [(j, x[2]) for x in schedule(kts) if x[0] == "keys" for j in passes(kts, x[1])]

                def context(q, g):
                    dve.wait_ge(s["ctx_high"], KG * q + g + 1)
                    dve.tensor_tensor(flat("L", "c"), bank("cT", q, g)[:, :], flat("H", "c").bitcast(F32),
                                      ALU.subtract).then_inc(s["ctx_split"], 1)

                def keys(q, k):
                    if q == 0 and k == 0:
                        dve.wait_ge(s["biases"], 64)
                    filled(dve, "kv", q, k)
                    for n, j in enumerate(passes(kts, q)):
                        key_stack(j, k, bank("kv", q, k)[:, n * 2 * P:(n + 1) * 2 * P],
                                  j == passes(kts, q)[-1], ("kv", q, k))

                def key_stack(j, k, pt, last, tile):
                    cols = slice((j % 2) * P, (j % 2 + 1) * P)
                    kf = m["kf"][:, kvs[0] % 2, :]
                    if kvs[0] >= 2:
                        dve.wait_ge(s["k_stacked"], kvs[0] - 1)
                    dve.tensor_tensor(kf, pt[:, 0:P], m["bk"][:, cols], ALU.add)
                    values = dve.tensor_tensor(m["vx"][:, value_tile(j, k), :, 0:HD],
                                               pt[:, P:2 * P].rearrange("p (h e) -> p h e", e=HD),
                                               m["bv"][:, cols].rearrange("p (h e) -> p h e", e=HD), ALU.add)
                    if last:
                        values.then_inc(s["dve_emptied"], 1)
                        emptied(dve, *tile)
                    else:
                        chain(values)
                    mk = m["mk"][:, kvs[0] % 2, :, :]
                    if kvs[0] >= 2:
                        filled(dve, "kT", *stacks[kvs[0] - 2])
                    kv3 = kf.rearrange("p (h e) -> p h e", e=HD)
                    chain(dve.tensor_copy(mk[:, :, 0:HD], kv3))
                    dve.tensor_copy(mk[:, :, 2 * HD:3 * HD], kv3)
                    dve.tensor_tensor(mk[:, :, HD:2 * HD], kv3, mk[:, :, 0:HD].bitcast(F32),
                                      ALU.subtract).then_inc(s["k_stacked"], 1)
                    kvs[0] += 1

                def queries(j):
                    cols = slice((j % 2) * P, (j % 2 + 1) * P)
                    if j == 1 and K == 2:
                        filled(dve, "ao", B - 1, NT - 1)
                        chain(dve.memset(m["mq"][1][:, :, :, 3 * HD:STK].bitcast(F32), 0.0))
                    for i in range(NT):
                        filled(dve, "q", j, i)
                        qf = m["kf"][:, 2 + i % 2, :]
                        if NT * j + i >= 2:
                            dve.wait_ge(s["q_stacked"], NT * j + i - 1)
                        dve.tensor_tensor(qf, bank("q", j, i)[:, 0:P], m["bq"][:, cols],
                                          ALU.add).then_inc(s["dve_emptied"], 1)
                        emptied(dve, "q", j, i)
                        q3 = qf.rearrange("p (h e) -> p h e", e=HD)
                        mq = m["mq"][qslot(j)][:, i, :, :]
                        back = 2 if K == 2 else 1
                        if j >= back:
                            filled(dve, "qT2", j - back, i)
                        chain(dve.tensor_copy(mq[:, :, 0:HD], q3))
                        dve.tensor_copy(mq[:, :, HD:2 * HD], q3)
                        dve.tensor_tensor(mq[:, :, 2 * HD:3 * HD], q3, mq[:, :, 0:HD].bitcast(F32),
                                          ALU.subtract).then_inc(s["q_stacked"], 1)

                def maxima(j, i):
                    dve.wait_ge(s["mb_ready"], NT * (j // 2 + 1))
                    for h in range(HH):
                        for c in range(NS):
                            filled(dve, "smax", j, i, h, c)
                            pt = bank("smax", j, i, h, c)[:, 0:SN]
                            dve.tensor_tensor_reduce(pt, pt, mask_term(j // 2, i)[:, c * SN:(c + 1) * SN], 1.0,
                                                     -3e38, ALU.add, ALU.max,
                                                     m["mx"][:, i, h, c:c + 1]).then_inc(s["dve_emptied"], 1)
                    emptied(dve, "smax", j, i, HH - 1, NS - 1)
                    mx = m["mx"][:, i, :, 0]
                    if NS > 1:
                        chain(dve.tensor_tensor(mx, mx, m["mx"][:, i, :, 1], ALU.max))
                    chain(dve.tensor_scalar(m["big"][:, :], mx, MASKED / 2, 3e38, ALU.is_lt, ALU.mult))
                    chain(dve.scalar_tensor_tensor(out=m["nm"][:, :], in0=mx, scalar=-1.0, in1=m["big"][:, :],
                                                   op0=ALU.mult, op1=ALU.add))
                    mq = m["mq"][qslot(j)][:, i, :, :]
                    chain(dve.tensor_copy(mq[:, :, 3 * HD], m["nm"][:, :]))
                    dve.tensor_tensor(mq[:, :, 3 * HD + 1], m["nm"][:, :], mq[:, :, 3 * HD].bitcast(F32),
                                      ALU.subtract).then_inc(s["max_ready"], 1)

                def norm(j, g):
                    filled(dve, "oN", j, g)
                    if g == 0 and j % 2 == 0:
                        filled(dve, *(("oxT", 0) if j else ("aoT", 1)), NC - 1)
                    pt = bank("oN", j, g)[:, :].rearrange("p (i h v) -> p i h v", i=NT, h=4)
                    rd = m["rd"][:, g, :].rearrange("p (i h) -> p i h", i=NT)
                    chain(dve.reciprocal(rd, pt[:, :, :, HD]))
                    q = 2 * (j % 2) + g
                    dve.tensor_tensor(ON[:, :, q * 4 * HD:(q + 1) * 4 * HD].rearrange("p i (h e) -> p i h e", e=HD),
                                      pt[:, :, :, 0:HD], rd.unsqueeze(3).broadcast_to([P, NT, 4, HD]),
                                      ALU.mult).then_inc(s["dve_emptied"], 1)

                def project(b):
                    for i in range(NT):
                        t = NT * b + i
                        filled(dve, "p", b, i)
                        dve.wait_ge(s["x1_biased"], t + 1)
                        dve.tensor_tensor(m["xr"][:, t, :], m["xr"][:, t, :], bank("p", b, i)[:, 0:D],
                                          ALU.add).then_inc(s["dve_emptied"], 1)
                        emptied(dve, "p", b, i)
                        statistics(i, m["xr"][:, t, :])

                def shares(b):
                    rows = slice(NT * b, NT * (b + 1))
                    emptied(dve, "route", b)
                    re, top, idxf, wsum, comb = (m[x][:, rows, :] for x in ("re", "top", "idxf", "wsum", "comb"))
                    chain(dve.tensor_scalar(re, re, 1.0, None, ALU.add))
                    chain(dve.reciprocal(re, re))
                    for t in range(NT * b, NT * (b + 1)):
                        ins = dve.max(m["top"][:, t, :], m["re"][:, t, :])
                    chain(ins)
                    for t in range(NT * b, NT * (b + 1)):
                        ins = dve.max_index(m["idx"][:, t, :], m["top"][:, t, :], m["re"][:, t, :])
                    chain(ins)
                    chain(dve.tensor_copy(idxf, m["idx"][:, rows, :]))
                    chain(dve.tensor_tensor(wsum, top[:, :, 0:1], top[:, :, 1:2], ALU.add))
                    chain(dve.tensor_scalar(wsum, wsum, 1e-20, None, ALU.add))
                    chain(dve.reciprocal(wsum, wsum))
                    chain(dve.tensor_tensor(top[:, :, 0:2], top[:, :, 0:2], wsum.broadcast_to([P, NT, 2]), ALU.mult))
                    places = m["iota8"][:, :].unsqueeze(1).broadcast_to([P, NT, E_])
                    hot = m["hot"][:, :, :]
                    for k, dst in ((0, hot), (1, comb)):
                        chain(dve.tensor_tensor(dst, places, idxf[:, :, k:k + 1].broadcast_to([P, NT, E_]),
                                                ALU.is_equal))
                        chain(dve.tensor_tensor(dst, dst, top[:, :, k:k + 1].broadcast_to([P, NT, E_]), ALU.mult))
                    chain(dve.tensor_tensor(comb, comb, hot, ALU.add))

                def hidden_low(n):
                    emptied(dve, "h", n)
                    chain(dve.tensor_tensor(HLOW[:, n % 2, :], HID[:, n % 2, :], HID[:, n % 2, :], ALU.mult))
                    dve.wait_ge(s["h_high"], n + 1)
                    if n >= 2:
                        dve.wait_ge(s["y_step"], n - 1)
                    dve.tensor_tensor(HLO[:, n % 2, :], HLOW[:, n % 2, :], HHI[:, n % 2, :].bitcast(F32),
                                      ALU.subtract).then_inc(s["h_split"], 1)

                def gather(e, b):
                    dve.wait_ge(s["y_step"], TASKS.index((UNITS.index((e, LAST[e])), b)) + 1)
                    for i in range(NT):
                        t = NT * b + i
                        if gathers[0] >= NT:
                            dve.wait_ge(s["y_emptied"], gathers[0] - NT + 1)
                        gathers[0] += 1
                        y_read[e, t] = gathers[0]
                        dve.scalar_tensor_tensor(out=m["xr"][:, t, :],
                                                 in0=banks[4 + t // 2][:, (t % 2) * D:(t % 2 + 1) * D],
                                                 scalar=m["comb"][:, t, e:e + 1], in1=m["xr"][:, t, :],
                                                 op0=ALU.mult, op1=ALU.add).then_inc(s["y_emptied"], 1)

                def finish(b, part):
                    t = NT * b + part
                    if part < NT:
                        dve.wait_ge(s["y_emptied"], y_read[E_ - 1, t])
                        statistics(part, m["xr"][:, t, :])
                    else:
                        normalise_rows(m["xr"], m["xr"], b, s["out_ready"])

                gathers, y_read = [0], {}
                for stage, *at in schedule(kts):
                    if stage == "kv":
                        linear_kv(*at)
                    elif stage == "sum":
                        linear_sums(*at)
                    elif stage == "q":
                        linear_q(*at)
                    elif stage == "linear":
                        linear_out(*at)
                    elif stage == "turn":
                        split_rows(*at)
                    elif stage == "attended":
                        attended(*at)
                    elif stage == "mask":
                        mask_transposed(*at)
                    elif stage == "enter":
                        enter(*at)
                    elif stage == "context":
                        context(*at)
                    elif stage == "keys":
                        keys(*at)
                    elif stage == "queries":
                        queries(*at)
                    elif stage == "maxima":
                        maxima(*at)
                    elif stage == "norm":
                        norm(*at)
                    elif stage == "project":
                        project(*at)
                    elif stage == "settle":
                        normalise_rows(m["xr"], m["xr"], at[0], s["x2_ready"])
                    elif stage == "shares":
                        shares(*at)
                    elif stage == "in":
                        hidden_low(*at)
                    elif stage == "add":
                        gather(*at)
                    elif stage == "finish":
                        finish(*at)

            either(dve, rest, steps, turns)

        @block.tensor
        def _(pe):
            order = [0]

            def claim(*key):
                bk, n, before = tiles[key]
                order[0] += 1
                assert n == order[0], key
                if before is not None:
                    emptied(pe, *before)
                return banks[bk]

            def three(out, pairs, stop=True, start=True):
                todo = [(a, b, x, y) for a, b in pairs for x, y in (("H", "H"), ("H", "L"), ("L", "H"))]
                for n, (a, b, x, y) in enumerate(todo):
                    ins = pe.matmul(out, a(x), b(y), start=start and n == 0, stop=stop and n == len(todo) - 1)
                return ins

            def transposed(name, b):
                src, ready, count = {"xnT": (XN, "xn_ready", NT * (b + 1)),
                                     "aoT": (ON, None, 0), "x1T": (m["xr"], "x1_ready", NT * (b + 1)),
                                     "oxT": (ON, None, 0), "x2T": (m["xr"], "x2_ready", NT * (b + 1))}[name]
                if ready:
                    pe.wait_ge(s[ready], count)
                elif name == "aoT":
                    emptied(pe, "nd", b, NT - 1)
                else:
                    emptied(pe, "oN", 2 * b + 1, 1)
                for c in range(NC):
                    pt = claim(name, b, c)
                    for i in range(NT):
                        t = i if ready is None else NT * b + i
                        ins = pe.transpose(pt[:, i * P:(i + 1) * P], src[:, t, c * P:(c + 1) * P],
                                           m["ident"][:, :])
                    ins.then_inc(s["filled"], 1)

            def xtile(b, c, i):
                return lambda part: m["xt" + part][:, b, c, i * P:(i + 1) * P]

            def linear_kv(b):
                pe.wait_ge(s["w_split"], PIECE["wqkv2"])
                pe.wait_ge(s["xt_split"], NC * (b + 1))
                for i in range(NT):
                    pt = claim("akv", b, i)
                    three(pt[:, :], [(xtile(b, c, i), lambda p, c=c: m["wqkv" + p][:, c, D:3 * D])
                                     for c in range(NC)]).then_inc(s["filled"], 1)

            def linear_sums(b):
                for i in range(NT):
                    emptied(pe, "akv", b, i)
                pe.wait_ge(s["ks_ready"], 1)
                for c in range(NC):
                    pt = claim("sum", b, c)
                    for i in range(NT):
                        ins = pe.matmul(pt[:, 0:P + 1], KA[:, i, c * P:(c + 1) * P], V1[:, i, c, 0:P + 1],
                                        start=(i == 0), stop=(i == NT - 1))
                    ins.then_inc(s["filled"], 1)

            def linear_q(b):
                pe.wait_ge(s["w_split"], PIECE["wqkv0"])
                for c in range(NC):
                    pt = claim("aq", b, c)
                    three(pt[:, :], [(lambda p, a=a, c=c: m["wqkv" + p][:, a, c * P:(c + 1) * P],
                                      lambda p, a=a: xt(p, b, a)) for a in range(NC)]).then_inc(s["filled"], 1)

            def linear_out(b):
                emptied(pe, "sum", b, NC - 1)
                emptied(pe, "aq", b, NC - 1)
                for i in range(NT):
                    pt = claim("nd", b, i)
                    for c in range(NC):
                        ins = pe.matmul(pt[:, c * 136:(c + 1) * 136], QA[:, c, i * P:(i + 1) * P], KVS[:, c, :],
                                        start=True, stop=True)
                    ins.then_inc(s["filled"], 1)

            def attended(b):
                pe.wait_ge(s["w_split"], PIECE["wout"])
                emptied(pe, "aoT", b, NC - 1)
                for i in range(NT):
                    pt = claim("ao", b, i)
                    three(pt[:, 0:D], [(lambda p, c=c: m["ox" + p][:, c, i * P:(i + 1) * P],
                                        lambda p, c=c: m["wout" + p][:, c, :]) for c in range(NC)]
                          ).then_inc(s["filled"], 1)

            def mask_transposed(b):
                pe.wait_ge(s["mb_ready"], NT * (b + 1))
                for k in range(KG):
                    pt = claim("mT", b, k)[:, :].bitcast(BF16)
                    for a in range(2):
                        for i in range(NT):
                            ins = pe.transpose(pt[:, a * S + i * P:a * S + (i + 1) * P],
                                               mask_term(b, i)[:, (2 * k + a) * P:(2 * k + a + 1) * P],
                                               m["identb"][:, :])
                    ins.then_inc(s["filled"], 1)

            pe.wait_ge(s["consts"], 5)
            transposed("xnT", 0)
            pe.wait_ge(s["mask_least"], 1)
            pe.transpose(banks[7][0:1, 0:P], m["least"][:, 0:1], m["ident"][:, :]).then_inc(s["least_turned"], 1)

            def rest():
                units = [0, 0]
                kvs = [0]
                ctxs = [0]

                def turn_stack(key, stack):
                    pt = claim(*key)
                    for r in range(NPR):
                        ins = pe.transpose(pt[:, r * P:(r + 1) * P].bitcast(F32R),
                                           stack[:, 2 * r:2 * r + 2, :].rearrange("p a b -> p (a b)"),
                                           m["identr"][:, :])
                    ins.then_inc(s["filled"], 1)

                def turn_context(j, g):
                    n = ctxs[0]
                    pe.wait_ge(s["cx_loaded"][n % 2], 16 * (n // 2 + 1))
                    ctxs[0] += 1
                    pt = claim("cT", j, g)
                    for c in range(NC):
                        for k in range(2):
                            ins = pe.transpose(pt[:, (2 * c + k) * P:(2 * c + k + 1) * P],
                                               m["cx"][:, n % 2, k, c * P:(c + 1) * P], m["ident"][:, :])
                    ins.then_inc(s["filled"], 1)

                def turn_keys(q, k):
                    for j in passes(kts, q):
                        pe.wait_ge(s["k_stacked"], kvs[0] + 1)
                        turn_stack(("kT", j, k), m["mk"][:, kvs[0] % 2, :, :])
                        kvs[0] += 1

                def keys(q, k):
                    pe.wait_ge(s["w_split"], PIECE["wkv1"])
                    emptied(pe, "cT", q, k // 2)
                    f, n = passes(kts, q)[0] % 2, len(passes(kts, q))
                    pt = claim("kv", q, k)
                    three(pt[:, 0:2 * P * n], [(lambda p, c=c: m["c" + p][:, c, (k % 2) * P:(k % 2 + 1) * P],
                                                lambda p, c=c: m["wkv" + p][:, c, f:f + n, :, :].rearrange(
                                                    "p f a n -> p (f a n)")) for c in range(NC)]
                          ).then_inc(s["filled"], 1)

                def queries(j):
                    b, f = j // 2, j % 2
                    pe.wait_ge(s["w_split"], PIECE["wq"])
                    emptied(pe, "x1T", b, NC - 1)
                    for i in range(NT):
                        pt = claim("q", j, i)
                        three(pt[:, 0:P], [(xtile(b, c, i), lambda p, c=c: m["wq" + p][:, c, f * P:(f + 1) * P])
                                           for c in range(NC)]).then_inc(s["filled"], 1)
                        if i:
                            pe.wait_ge(s["q_stacked"], NT * j + i)
                            turn_stack(("qT", j, i - 1), m["mq"][qslot(j)][:, i - 1, :, :])
                    pe.wait_ge(s["q_stacked"], NT * (j + 1))
                    turn_stack(("qT", j, NT - 1), m["mq"][qslot(j)][:, NT - 1, :, :])

                def maxima(j, i):
                    emptied(pe, "kT", j, K - 1)
                    emptied(pe, "qT", j, i)
                    for h in range(HH):
                        rows = slice(STK * (h % 2), STK * (h % 2) + 3 * HD)
                        for c in range(NS):
                            pt = claim("smax", j, i, h, c)
                            pe.matmul(pt[:, 0:SN], m["qt"][qslot(j)][rows, h // 2, i * P:(i + 1) * P],
                                      m["kt"][rows, h // 2, key_cols(j, c * SN // P, SN)], start=True,
                                      stop=True).then_inc(s["filled"], 1)

                def queries2(j):
                    for i in range(NT):
                        pe.wait_ge(s["max_ready"], NT * j + i + 1)
                        turn_stack(("qT2", j, i), m["mq"][qslot(j)][:, i, :, :])

                def probs(j, g, k):
                    emptied(pe, "qT2", j, NT - 1)
                    emptied(pe, "mT", j // 2, KG - 1)
                    for h in range(4):
                        head = 4 * g + h
                        rows = slice(STK * (head % 2), STK * (head % 2) + STK)
                        pt = claim("st", j, g, k, h)
                        pe.matmul(pt[:, :], m["kt"][rows, head // 2, key_cols(j, k)],
                                  m["qt"][qslot(j)][rows, head // 2, :], start=True, stop=False)
                        pe.matmul(pt[:, :], m["identb"][:, :], mask_term_t(j // 2, k), start=False,
                                  stop=True).then_inc(s["filled"], 1)

                def values(j, g, k):
                    if k == 0 and 2 * j + g >= 2:
                        pe.wait_ge(s["pv_emptied"], 2 * j + g - 1)
                    for h in range(4):
                        emptied(pe, "st", j, g, k, h)
                        pe.matmul(banks[6 + g][32 * h:32 * h + 32, :], m["vx"][:, value_tile(j, k), 4 * g + h, :],
                                  m["pr"][:, units[0] % NP, :], start=(k == 0),
                                  stop=(k == K - 1)).then_inc(s["pv_done"], 1)
                        units[0] += 1

                def norm(j, g):
                    n = 2 * j + g
                    pe.wait_ge(s["pv_emptied"], n + 1)
                    pt = claim("oN", j, g)
                    for i in range(NT):
                        ins = pe.transpose(pt[:, i * P:(i + 1) * P], RAW[:, n % 2, i * P:(i + 1) * P],
                                           m["ident"][:, :])
                    ins.then_inc(s["filled"], 1)

                def project(b):
                    pe.wait_ge(s["w_split"], PIECE["wp"])
                    emptied(pe, "oxT", b, NC - 1)
                    for i in range(NT):
                        pt = claim("p", b, i)
                        three(pt[:, 0:D], [(lambda p, c=c: m["ox" + p][:, c, i * P:(i + 1) * P],
                                            lambda p, c=c: m["wp" + p][:, c, :]) for c in range(NC)]
                              ).then_inc(s["filled"], 1)

                def route(b):
                    pe.wait_ge(s["rw_loaded"], 32)
                    pe.wait_ge(s["x2_copied"], NC * (b + 1))
                    pt = claim("route", b)
                    for i in range(NT):
                        for c in range(NC):
                            ins = pe.matmul(pt[:, i * E_:(i + 1) * E_], m["xtf"][:, b, c, i * P:(i + 1) * P],
                                            m["rw"][:, c, :], start=(c == 0), stop=(c == NC - 1))
                    ins.then_inc(s["filled"], 1)

                def expert_in(n):
                    u, b = TASKS[n]
                    pe.wait_ge(s["w_split"], NSM + u + 1)
                    emptied(pe, "x2T", b, NC - 1)
                    pt = claim("h", n)
                    three(pt[:, :], [(lambda p, c=c: expert_weights(p, u)[:, c * P:(c + 1) * P],
                                      lambda p, c=c: xt(p, b, c)) for c in range(NC)]).then_inc(s["filled"], 1)

                def expert_out(n):
                    u, b = TASKS[n]
                    e, k = UNITS[u]
                    pe.wait_ge(s["h_split"], n + 1)
                    if u == 0:
                        if b == 0:
                            for kk in (4, 5):
                                emptied(pe, *before_y[kk])
                        else:
                            pe.wait_ge(s["pv_emptied"], 8)
                    for i in range(NT):
                        t = NT * b + i
                        y = banks[4 + t // 2][:, (t % 2) * D:(t % 2 + 1) * D]
                        if k == 0 and e:
                            pe.wait_ge(s["y_emptied"], y_read[e - 1, b] + 2 * (i // 2) + 2)
                        for p, (x_, y_) in enumerate((("H", "H"), ("H", "L"), ("L", "H"))):
                            ins = pe.matmul(y, {"H": HHI, "L": HLO}[x_][:, n % 2, i * P:(i + 1) * P],
                                            expert_weights(y_, u)[:, D:2 * D],
                                            start=(k == 0 and p == 0 and t % 2 == 0),
                                            stop=(k == LAST[e] and p == 2), skip_group_check=True)
                    ins.then_inc(s["y_step"], 1)

                adds = [tuple(x[1:]) for x in schedule(kts) if x[0] == "add"]
                y_read = {x: NT * n for n, x in enumerate(adds)}
                for stage, *at in schedule(kts):
                    if stage == "kv":
                        linear_kv(*at)
                    elif stage == "sum":
                        linear_sums(*at)
                    elif stage == "q":
                        linear_q(*at)
                    elif stage == "linear":
                        linear_out(*at)
                    elif stage == "turn":
                        transposed(*at)
                    elif stage == "attended":
                        attended(*at)
                    elif stage == "mask":
                        mask_transposed(*at)
                    elif stage == "context":
                        turn_context(*at)
                    elif stage == "keys":
                        keys(*at)
                    elif stage == "kturn":
                        turn_keys(*at)
                    elif stage == "queries":
                        queries(*at)
                    elif stage == "maxima":
                        maxima(*at)
                    elif stage == "queries2":
                        queries2(*at)
                    elif stage == "probs":
                        probs(*at)
                    elif stage == "values":
                        values(*at)
                    elif stage == "norm":
                        norm(*at)
                    elif stage == "project":
                        project(*at)
                    elif stage == "route":
                        route(*at)
                    elif stage == "in":
                        expert_in(*at)
                    elif stage == "out":
                        expert_out(*at)

            either(pe, rest, order)


_INS = ["x", "ctx_1024", "mask_Bx1xSxS2_bk1", "L0_attn_gamma", "L0_attn_beta", "L0_attn_Wqkv", "L0_attn_Wout",
        "L0_xattn_Wq", "L0_xattn_bq", "L0_xattn_Wk", "L0_xattn_bk", "L0_xattn_Wv", "L0_xattn_bv",
        "L0_xattn_Wp", "L0_xattn_bp", "L0_ffn_router_w", "L0_ffn_w1", "L0_ffn_w2"]


def kernel(**inputs):
    import concourse.bacc as _bacc
    from concourse.bass_utils import run_bass_kernel_spmd as _run

    nc = _bacc.Bacc("TRN2", target_bir_lowering=False, num_devices=1)
    arrays, args = {}, []
    for name in _INS:
        a = np.ascontiguousarray(inputs[name])
        arrays[f"in_{name}"] = a
        args.append(nc.dram_tensor(f"in_{name}", a.shape, mybir.dt.from_np(a.dtype), kind="ExternalInput").ap())
    args.append(nc.dram_tensor("out", (B, S, D), F32, kind="ExternalOutput").ap())
    decoder_layer(nc, *args)
    r = _run(nc, [arrays], core_ids=[0])
    return r.results[0]["out"]
```

```python
from contextlib import ExitStack

import numpy as np

import concourse.bass as bass
from concourse import mybir

ALU = mybir.AluOpType
ACT = mybir.ActivationFunctionType
AX = mybir.AxisListType
F32 = mybir.dt.float32
F32R = mybir.dt.float32r
BF16 = mybir.dt.bfloat16
I32 = mybir.dt.int32
U8 = mybir.dt.uint8
U16 = mybir.dt.uint16
U32 = mybir.dt.uint32

P = 128
B, S, D = 2, 512, 256
S2 = 1024
H, HD = 16, 16
NT = S // P
NC = D // P
STK = 64
HH = H // 2
NPR = HH // 2
E_ = 8
WIDTHS = [256] * 4 + [512] * 4
LEAD = 9
END_LEAD = 2
UNITS = [(e, k) for e in range(E_) for k in range(WIDTHS[e] // P)]
NU = len(UNITS)
LAST = {e: WIDTHS[e] // P - 1 for e in range(E_)}
TASKS = [(u, 0) for u in range(LEAD)]
while len(TASKS) < B * NU:
    _ahead, _behind = (sum(b == c for _, b in TASKS) for c in range(B))
    if _ahead < NU and (_ahead - _behind < END_LEAD or TASKS[-1][1] == TASKS[-2][1] == 1 or
                        (_ahead - _behind == END_LEAD and TASKS[-1][1] == 1)):
        TASKS.append((_ahead, 0))
    else:
        TASKS.append((_behind, 1))
SCALE = float(HD) ** -0.5
LN_EPS = 1e-5
DEN_EPS = 1e-6
ROOT_SEED = float(0x5f3759df)
MASKED = -1e38
EASED = 1e-8
WARM_UP = (42, 20, 30)
NR = 6
NRAW = 4
NW = 11
NP = 8
ALL_KEYS = list(range(S2 // P))
LAST_KEYS = ALL_KEYS[-2:]
SKIPPED = (S2 // P - 2) * P


FEW_KEYS_ORDER = """
enter 1, kv 0, round 3, q 0, turn xnT 1, round 4, sum 0, context 0 0, linear 0, round 5, kv 1,
turn aoT 0, round 6, q 1, round 7, keys 0 0, sum 1, attended 0, linear 1, kturn 0 0, turn x1T 0, mask 0,
mask 1, keys 0 1, query 0, turn aoT 1, kturn 0 1, context 1 0, qturn 0 0, qturn 0 1, qturn 0 2,
qturn 0 3, maxima 0 0, maxima 0 1, maxima 0 2, maxima 0 3, attended 1, qturn2 0 0, qturn2 0 1,
qturn2 0 2, qturn2 0 3,
probs 0 0 0, query 1, keys 1 0, qturn 1 0, qturn 1 1, qturn 1 2, qturn 1 3, maxima 1 0,
probs 0 0 1, values 0 0 0, maxima 1 1, kturn 1 0, qturn2 1 0,
probs 0 1 0, turn x1T 1, values 0 0 1, maxima 1 2, keys 1 1, qturn2 1 1,
probs 0 1 1, values 0 1 0, maxima 1 3, qturn2 1 2, kturn 1 1, query 2, norm 0 0, values 0 1 1,
qturn2 1 3, qturn 2 0, qturn 2 1, qturn 2 2, qturn 2 3,
probs 1 0 0, maxima 2 0, norm 0 1,
probs 1 0 1, values 1 0 0, maxima 2 1, qturn2 2 0,
probs 1 1 0, values 1 0 1, maxima 2 2, qturn2 2 1,
probs 1 1 1, values 1 1 0, maxima 2 3, qturn2 2 2, query 3, norm 1 0, values 1 1 1, qturn2 2 3,
qturn 3 0, qturn 3 1, qturn 3 2, qturn 3 3,
probs 2 0 0, maxima 3 0, norm 1 1,
probs 2 0 1, maxima 3 1, values 2 0 0, qturn2 3 0, turn oxT 0,
probs 2 1 0, maxima 3 2, values 2 0 1, qturn2 3 1,
probs 2 1 1, maxima 3 3, values 2 1 0, project 0, qturn2 3 2, settle 0, norm 2 0, values 2 1 1,
qturn2 3 3,
probs 3 0 0, norm 2 1,
probs 3 0 1, values 3 0 0, turn x2T 0,
probs 3 1 0, values 3 0 1, route 0, shares 0, experts 1,
probs 3 1 1, values 3 1 0, experts 2, norm 3 0, values 3 1 1, norm 3 1, experts 3, turn oxT 1,
experts 2, project 1, experts 3, settle 1, experts 5, turn x2T 1, experts 2, route 1, experts 4,
shares 1"""


def passes(kts, q):
    return [2 * q, 2 * q + 1] if len(kts) == 2 else [q]


def expert_stages():
    out, finish = [("in", 0)], []
    for n, (u, b) in enumerate(TASKS):
        out += [("in", n + 1)] if n + 1 < len(TASKS) else []
        out += [("out", n)] + finish[0:1]
        finish = finish[1:]
        e, k = UNITS[u]
        if k == LAST[e]:
            out.append(("add", e, b))
        if u == NU - 1:
            parts = [("finish", b, part) for part in range(2)]
            finish = parts if b == 0 else finish + parts
    return out + finish


def schedule(kts):
    def gather_pass(j):
        groups = [(g, k) for g in range(2) for k in range(len(kts))]
        out = []
        for n, (g, k) in enumerate(groups):
            out += [("probs", j, g, k)] + ([("values", j, *groups[n - 1])] if n else [])
            out += [("norm", j, 0)] if n == len(kts) + 1 else []
        return out + [("values", j, *groups[-1]), ("norm", j, 1)]

    def each(stage, j):
        return [(stage, j, i) for i in range(NT)]

    experts = expert_stages()
    if len(kts) > 2:
        plan = [("round", n) for n in range(3, 8)] + [
            ("kv", 0), ("enter", 1), ("turn", "xnT", 1), ("sum", 0), ("q", 0), ("linear", 0), ("kv", 1),
            ("turn", "aoT", 0), ("attended", 0), ("sum", 1), ("q", 1), ("linear", 1), ("turn", "aoT", 1),
            ("attended", 1), ("turn", "x1T", 0), ("turn", "x1T", 1)]
        for j in range(2 * B):
            b = j // 2
            plan += [("mask", b)] if j % 2 == 0 else []
            for k in range(len(kts)):
                plan += [("context", j, k // 2)] if k % 2 == 0 else []
                plan += [("keys", j, k)] + ([("kturn", j, k - 1)] if k else [])
            plan += [("kturn", j, len(kts) - 1)] + [("query", j)] + each("qturn", j)
            plan += each("maxima", j) + each("qturn2", j) + gather_pass(j)
            if j % 2:
                plan += [("turn", "oxT", b), ("project", b), ("settle", b), ("turn", "x2T", b), ("route", b),
                         ("shares", b)]
        return plan + experts
    plan = []
    for step in FEW_KEYS_ORDER.split(","):
        stage, *at = step.split()
        if stage == "experts":
            plan, experts = plan + experts[:int(at[0])], experts[int(at[0]):]
        else:
            plan.append((stage, *(int(a) if a.isdigit() else a for a in at)))
    return plan + experts


def ring_plan(kts):
    order = [(("xnT", 0, c), "act_emptied") for c in range(NC)]
    first_h = None

    def put(who, *key):
        order.append((key, who))

    for stage, *at in schedule(kts):
        if stage == "kv":
            for i in range(NT):
                put("dve_emptied", "akv", at[0], i)
        elif stage in ("sum", "q"):
            for c in range(NC):
                put("dve_emptied", {"sum": "sum", "q": "aq"}[stage], at[0], c)
        elif stage in ("linear", "attended", "project"):
            for i in range(NT):
                put("dve_emptied", {"linear": "nd", "attended": "ao", "project": "p"}[stage], at[0], i)
        elif stage == "turn":
            for c in range(NC):
                put({"xnT": "act_emptied", "aoT": "ox_split", "oxT": "ox_split"}.get(at[0], "xt_split"), *at, c)
        elif stage == "mask":
            for k in range(len(kts) // 2):
                put("act_emptied", "mT", at[0], k)
        elif stage == "context":
            put("ctx_split", "cT", *at)
        elif stage == "keys":
            put("dve_emptied", "kv", *at)
        elif stage == "kturn":
            for j in passes(kts, at[0]):
                put("act_emptied", "kT", j, at[1])
        elif stage == "query":
            put("q_stacked", "q", *at)
        elif stage == "qturn":
            put("act_emptied", "qT", *at)
        elif stage == "maxima":
            for n in range(HH * len(kts) // 4):
                put("dve_emptied", "smax", *at, n)
        elif stage == "qturn2":
            put("act_emptied", "qT2", *at)
        elif stage == "probs":
            for h in range(4):
                put("act_emptied", "st", *at, h)
        elif stage == "norm":
            put("dve_emptied", "oN", *at)
        elif stage == "route":
            put("act_emptied", "route", at[0])
        elif stage == "in":
            if at[0] == 0:
                first_h = len(order)
            put("act_emptied", "h", at[0])
    tiles, readers, holds = {}, {}, {}
    counts = {"act_emptied": 0, "dve_emptied": 0, "ox_split": 0, "q_stacked": 0, "xt_split": B * NC, "ctx_split": 0}
    for n, (key, who) in enumerate(order):
        bank = n % NR if n < first_h else (n - first_h) % 4
        tiles[key] = (bank, n + 1, holds.get(bank))
        holds[bank] = key
        counts[who] += 1
        readers[key] = (who, counts[who])
        if n == first_h - 1:
            before_y = {k: holds[k] for k in (4, 5)}
    return tiles, readers, before_y


def decoder_layer(nc, x, ctx, mask, gamma, beta, Wqkv, Wout, Wq, bq, Wk, bk, Wv, bv, Wp, bp,
                  router_w, w1, w2, out):
    with ExitStack() as stack:
        def sb(name, shape, dt=F32):
            return stack.enter_context(nc.sbuf_tensor(name, shape, dt))

        def sem(name):
            return stack.enter_context(nc.semaphore(name))

        m = {}
        m["ident"] = sb("ident", [P, P])
        m["identb"] = sb("identb", [P, P], BF16)
        m["identr"] = sb("identr", [P, P], F32R)
        m["blocks"] = sb("blocks", [P, P])
        m["iota8"] = sb("iota8", [P, E_])
        m["gam"] = sb("gam", [P, NC])
        m["bet"] = sb("bet", [P, NC])
        m["bq"] = sb("bqB", [P, D])
        m["bk"] = sb("bkB", [P, D])
        m["bv"] = sb("bvB", [P, D])
        m["bp"] = sb("bpB", [P, D])
        m["rw"] = sb("rw", [P, NC, E_])
        lin = sb("lin", [P, 8 * S], F32R)
        for n, s in enumerate("HL"):
            m["wqkv" + s] = lin[:, n * 6 * D:(n + 1) * 6 * D].rearrange("p (c n) -> p c n", c=NC)
            m["wout" + s] = lin[:, (12 + 2 * n) * D:(14 + 2 * n) * D].rearrange("p (c n) -> p c n", c=NC)
        qt = [sb("qt", [P, NPR, S], F32R)[:, :, :], lin[:, 0:4 * S].rearrange("p (r t) -> p r t", r=NPR)]
        mq = [sb("mq", [P, NT, HH, STK], F32R)[:, :, :, :],
              lin[:, 4 * S:8 * S].rearrange("p (i h k) -> p i h k", i=NT, h=HH)]
        m["qt"], m["mq"] = qt, mq
        for s in "HL":
            m["wq" + s] = sb("wq" + s, [P, NC, D], F32R)
            m["wkv" + s] = sb("wkv" + s, [P, NC, 2, 2, P], F32R)
            m["wp" + s] = sb("wp" + s, [P, NC, D], F32R)
            m["we" + s] = sb("we" + s, [P, 5, 2 * D], F32R)
        m["raw"] = sb("raw", [P, NRAW, 2 * D])
        m["xr"] = sb("xr", [P, B * NT, D])
        m["xtf"] = sb("xtf", [P, B, NC, S])
        m["xtH"] = sb("xtH", [P, B, NC, S], F32R)
        m["xtL"] = sb("xtL", [P, B, NC, S], F32R)
        m["kt"] = sb("kt", [P, NPR, S2], F32R)
        m["vx"] = sb("vx", [P, S2 // P, HH, 32])
        m["mk"] = sb("mk", [P, 2, HH, STK], F32R)
        m["mu"] = sb("mu", [P, 2, S2], U8)
        m["share"] = sb("share", [P, 4096])
        m["pr"] = sb("pr", [P, NP // 2, S])
        m["oxH"] = sb("oxH", [P, NC, S], F32R)
        m["oxL"] = sb("oxL", [P, NC, S], F32R)
        m["mterm"] = sb("mterm", [P, 2048])
        m["tmp"] = sb("tmp", [P, 4, S])
        m["kf"] = sb("kf", [P, 2, P])
        m["qf"] = sb("qf", [P, NT, P])
        m["cx"] = sb("cx", [P, 2, 2, D])
        m["cH"] = sb("cH", [P, NC, 2 * P], F32R)
        m["cL"] = sb("cL", [P, NC, 2 * P], F32R)
        m["st"] = sb("st", [P, NT, 6])
        m["mv"] = sb("mv", [P, NT, 2])
        m["rv"] = sb("rv", [P, 3, NT])
        m["mx"] = sb("mx", [P, NT, HH, 2])
        m["re"] = sb("re", [P, B * NT, E_])
        m["flag"] = sb("flag", [1, 1], I32)
        m["least"] = sb("least", [P, 2])
        m["top"] = sb("top", [P, B * NT, E_])
        m["idx"] = sb("idx", [P, B * NT, E_], U32)
        m["idxf"] = sb("idxf", [P, B * NT, E_])
        m["wsum"] = sb("wsum", [P, B * NT, 1])
        m["hot"] = sb("hot", [P, NT, E_])
        m["rd"] = sb("rd", [P, 2, H])
        m["comb"] = sb("comb", [P, B * NT, E_])
        banks = [stack.enter_context(nc.psum_tensor(f"bank{i}", [P, 512], F32)) for i in range(8)]

        sems = {}
        for name in ("consts", "small", "w_split", "filled", "act_emptied", "dve_emptied",
                     "xn_ready", "xt_split", "k_exp", "q_exp", "ks_ready", "w_high", "x1_biased", "x1_ready",
                     "mb_ready", "ctx_high", "ctx_split", "xt_high", "x2_copied", "k_stacked", "q_stacked", "max_ready",
                     "pv_done", "pv_emptied", "ox_split", "x2_ready", "h_high", "h_split",
                     "y_step", "y_emptied", "out_ready", "stored", "dve_step", "act_step", "pool_step",
                     "biases", "rw_loaded", "mask_loaded", "mask_least", "least_turned", "flag_ready"):
            sems[name] = sem(name)
        for name, n in (("x_loaded", B * NT), ("w_loaded", NRAW), ("mu_loaded", 2), ("cx_loaded", 2)):
            sems[name] = [sem(f"{name}{i}") for i in range(n)]

        io = dict(x=x, ctx=ctx, mask=mask, gamma=gamma, beta=beta, Wqkv=Wqkv, Wout=Wout, Wq=Wq, bq=bq,
                  Wk=Wk, bk=bk, Wv=Wv, bv=bv, Wp=Wp, bp=bp, router_w=router_w, w1=w1, w2=w2, out=out)
        emit(nc, io, m, banks, sems)


def emit(nc, io, m, banks, s):
    kts = K = KG = NS = SN = tiles = readers = before_y = None

    def attend_to(key_tiles):
        nonlocal kts, K, KG, NS, SN, tiles, readers, before_y
        kts = key_tiles
        K = len(kts)
        KG = K // 2
        NS = -(-K // 4)
        SN = min(K, 4) * P
        tiles, readers, before_y = ring_plan(kts)

    attend_to(ALL_KEYS)

    def either(eng, rest, *counters):
        eng.wait_ge(s["flag_ready"], 1)
        flag = eng.value_load(m["flag"][0:1, 0:1], min_val=0, max_val=1)
        start = [c[0] for c in counters]
        with eng.If(flag == 1):
            attend_to(LAST_KEYS)
            rest()
        for c, v in zip(counters, start):
            c[0] = v
        with eng.Else():
            attend_to(ALL_KEYS)
            rest()

    def bank(*key):
        return banks[tiles[key][0]]

    def filled(eng, *key):
        eng.wait_ge(s["filled"], tiles[key][1])

    def emptied(eng, *key):
        who, count = readers[key]
        eng.wait_ge(s[who], count)

    pieces = ["wqkv1", "wqkv2", "wqkv0", "wkv0", "wkv1", "wout", "wq", "wp"]
    PIECE = {name: n + 1 for n, name in enumerate(pieces)}
    NSM = len(pieces)
    raw_jobs = pieces + [("unit", u) for u in range(NU)]

    def raw_slot(n):
        slot = n % NRAW
        return slot, 16 * sum(1 + (isinstance(job, tuple) or job.startswith("wkv"))
                              for job in raw_jobs[slot:n + 1:NRAW])

    def piece(part, name):
        if name.startswith("wqkv"):
            q = int(name[4])
            return m["wqkv" + part][:, :, q * D:(q + 1) * D]
        if name.startswith("wkv"):
            return m["wkv" + part][:, int(name[3]), :, :, :].rearrange("p f a n -> p f (a n)")
        return m[name + part][:, :, :]

    share = m["share"]
    KA = share[:, 0:NT * D].rearrange("p (i d) -> p i d", i=NT)
    V1 = share[:, 1024:1024 + NT * NC * 130].rearrange("p (i c v) -> p i c v", i=NT, c=NC)
    QA = share[:, 2064:2064 + NC * S].rearrange("p (c t) -> p c t", c=NC)
    MALL = share[:, 0:SKIPPED * B * S // P // 4].bitcast(U8)
    prf = m["pr"][:, :, :].rearrange("p a b -> p (a b)")
    probs_at = [m["pr"][:, n, :] for n in range(NP // 2)] + [
        share[:, 2048 + n * S:2048 + (n + 1) * S] for n in range(NP // 2)]
    XN = prf[:, 0:2048].rearrange("p (t d) -> p t d", t=B * NT)
    KVS = share[:, 3088:3088 + NC * 136].rearrange("p (c v) -> p c v", c=NC)
    qtf = m["qt"][0].rearrange("p a b -> p (a b)")
    HHI = qtf[:, 0:1024].rearrange("p (r t) -> p r t", r=2)
    HLO = qtf[:, 1024:2048].rearrange("p (r t) -> p r t", r=2)
    HLOW = m["mterm"][:, 0:2 * S].rearrange("p (r t) -> p r t", r=2)
    HID = m["xtf"][:, 0, :, :]
    RAW = m["tmp"]
    ON = m["tmp"][:, 2:4, :].rearrange("p a (i d) -> p (a i) d", i=2)

    def mask_term(b, i):
        if K > 2:
            return share[:, 0:2048].bitcast(BF16)[:, i * K * P:(i + 1) * K * P]
        return m["mterm"][:, 0:1024].bitcast(BF16)[:, (NT * b + i) * K * P:(NT * b + i + 1) * K * P]

    def mask_term_t(b, k):
        if K > 2:
            return m["mterm"][:, :].bitcast(BF16)[:, k * S:(k + 1) * S]
        return m["mterm"][:, 1024:2048].bitcast(BF16)[:, (K * b + k) * S:(K * b + k + 1) * S]

    def score_parts(n):
        if K == 2:
            return [(4 * (n // 2) + n % 2 + 2 * a, 0, slice(a * SN, (a + 1) * SN)) for a in range(2)]
        return [(n // NS, n % NS, slice(0, SN))]

    def key_cols(j, k0, n=P):
        first = (j * K * P if K == 2 else 0) + k0 * P
        return slice(first, first + n)

    def value_tile(j, k):
        return (j * K if K == 2 else 0) + k

    def qslot(j):
        return j % 2 if K == 2 else 0

    def flat(part, name):
        return {"wkv": lambda a: a.rearrange("p c f a n -> p (c f a n)"),
                "wq": lambda a: a.rearrange("p c n -> p (c n)"),
                "c": lambda a: a.rearrange("p c k -> p (c k)")}[name](
                    m[name + part][:, :, :, :, :] if name == "wkv" else m[name + part][:, :, :])

    def expert_weights(part, u):
        slot = u % NW
        if slot < 5:
            return m["we" + part][:, slot, :]
        if slot == 5:
            return flat(part, "wq")
        if slot == 6:
            return flat(part, "c")
        if slot < 9:
            return flat(part, "wkv")[:, (slot - 7) * 2 * D:(slot - 6) * 2 * D]
        n = 2 * (slot - 9) + "HL".index(part)
        return m["mq"][0].rearrange("p i h k -> p (i h k)")[:, n * 2 * D:(n + 1) * 2 * D]

    def last_use(eng, slot):
        q = B if K == 2 else 2 * B
        if slot in (6, 7, 8):
            filled(eng, "kv", q - 1, K - 1)
        elif slot == 5:
            filled(eng, "q", 2 * B - 1)
        elif slot > 8:
            filled(eng, "qT2", 2 if K == 2 else 2 * B - 1, NT - 1)

    def xt(part, b, c):
        return m["xt" + part][:, b, c, :]

    block = nc.Block()
    with block:
        @block.sync
        def _(sp):
            def load_raw(n):
                job = raw_jobs[n]
                slot, _ = raw_slot(n)
                done = s["w_loaded"][slot]
                if n >= NRAW:
                    sp.wait_ge(s["w_split"], n - NRAW + 1)
                dst = m["raw"][:, slot, :]
                if isinstance(job, tuple):
                    u = job[1]
                    sp.dma_start(dst[:, 0:D].rearrange("p (c n) -> p c n", c=NC),
                                 io["w1"][:, u * P:(u + 1) * P].rearrange("(c p) n -> p c n", p=P)).then_inc(done, 16)
                    sp.dma_start(dst[:, D:2 * D], io["w2"][u * P:(u + 1) * P, :]).then_inc(done, 16)
                elif job.startswith("wqkv"):
                    q = int(job[4])
                    sp.dma_start(dst.rearrange("p (c n) -> p c n", c=NC),
                                 io["Wqkv"][:, q * D:(q + 1) * D].rearrange("(c p) n -> p c n", p=P)).then_inc(done, 16)
                elif job in ("wout", "wq", "wp"):
                    w = {"wout": io["Wout"], "wq": io["Wq"], "wp": io["Wp"]}[job]
                    sp.dma_start(dst.rearrange("p (c n) -> p c n", c=NC),
                                 w.rearrange("(c p) n -> p c n", p=P)).then_inc(done, 16)
                else:
                    c = int(job[3])
                    for a, w in enumerate((io["Wk"], io["Wv"])):
                        sp.dma_start(dst.rearrange("p (f a n) -> p f a n", f=2, a=2)[:, :, a, :],
                                     w[c * P:(c + 1) * P, :].rearrange("p (f n) -> p f n", f=2)).then_inc(done, 16)

            for t in range(NT):
                sp.dma_start(m["xr"][:, t, :], io["x"][0, t * P:(t + 1) * P, :]).then_inc(s["x_loaded"][t], 16)
            sp.dma_start(MALL.rearrange("p (r k) -> p r k", k=SKIPPED),
                         io["mask"].rearrange("b o (p r) k -> (b o p) r k", r=B * S // P)[:, :, 0:SKIPPED]
                         ).then_inc(s["mask_loaded"], 16)
            with nc.allow_non_contiguous_dma("256 elements each, once"):
                for name in ("gamma", "beta"):
                    sp.dma_start(m[name[:3]][:, :], io[name].rearrange("(c p) -> p c", p=P)).then_inc(s["small"], 16)
            for n in range(2):
                load_raw(n)
            for t in range(NT, B * NT):
                sp.dma_start(m["xr"][:, t, :],
                             io["x"][1, (t - NT) * P:(t - NT + 1) * P, :]).then_inc(s["x_loaded"][t], 16)
            for n in range(2, NRAW):
                load_raw(n)
            for name in ("bq", "bk", "bv", "bp"):
                sp.dma_start(m[name][:, :], io[name].rearrange("(a d) -> a d", a=1).broadcast_to([P, D])
                             ).then_inc(s["biases"], 16)
            for n in range(NRAW, NSM):
                load_raw(n)
            with nc.allow_non_contiguous_dma("2048 elements, once"):
                for c in range(NC):
                    sp.dma_start(m["rw"][:, c, :], io["router_w"][:, c * P:(c + 1) * P].rearrange("e p -> p e")
                                 ).then_inc(s["rw_loaded"], 16)

            def load_ctx(n):
                q, g = n // KG, n % KG
                if n >= 2:
                    filled(sp, "cT", (n - 2) // KG, (n - 2) % KG)
                k0 = kts[2 * g]
                sp.dma_start(m["cx"][:, n % 2, :, :],
                             io["ctx"][passes(kts, q)[0] // 2, k0 * P:(k0 + 2) * P, :].rearrange(
                                 "(k p) d -> p k d", p=P)).then_inc(s["cx_loaded"][n % 2], 16)

            def load_mask(n):
                b, i = n // NT, n % NT
                if n >= 2:
                    sp.wait_ge(s["mb_ready"], n - 1)
                sp.dma_start(m["mu"][:, n % 2, 0:K * P],
                             io["mask"][b, 0, i * P:(i + 1) * P, kts[0] * P:(kts[-1] + 1) * P]
                             ).then_inc(s["mu_loaded"][n % 2], 16)

            def rest():
                if K == 2:
                    for n in range(B):
                        load_ctx(n)
                for b in range(B):
                    for i in range(NT):
                        load_mask(NT * b + i)
                    for n in range(2 * KG if K > 2 else 0):
                        load_ctx(2 * KG * b + n)
                for n in range(NSM, NSM + NU):
                    load_raw(n)
                for t in range(B * NT):
                    sp.wait_ge(s["out_ready"], t + 1)
                    sp.dma_start(io["out"][t // NT, (t % NT) * P:(t % NT + 1) * P, :],
                                 m["xr"][:, t, :]).then_inc(s["stored"], 16)
                sp.wait_ge(s["stored"], 16 * B * NT)

            either(sp, rest)

        @block.gpsimd
        def _(pool):
            pool.memset(m["ident"][:, :], 0.0).then_inc(s["pool_step"], 1)
            pool.memset(m["blocks"][:, :], 1.0).then_inc(s["pool_step"], 1)
            pool.wait_ge(s["pool_step"], 2)
            pool.affine_select(out=m["ident"][:, :], in_=m["ident"][:, :], compare_op=ALU.not_equal, fill=1.0,
                               base=0, pattern=[[-1, P]], channel_multiplier=1).then_inc(s["pool_step"], 1)
            v = m["blocks"][:, :].rearrange("p (a e) -> p a e", e=HD)
            pool.affine_select(out=v, in_=v, compare_op=ALU.is_ge, fill=0.0, base=0,
                               pattern=[[-HD, P // HD], [0, HD]], channel_multiplier=1).then_inc(s["pool_step"], 1)
            pool.wait_ge(s["pool_step"], 4)
            v = m["blocks"][:, :].rearrange("p (a e) -> p a e", e=HD)
            pool.affine_select(out=v, in_=v, compare_op=ALU.is_ge, fill=0.0, base=HD - 1,
                               pattern=[[HD, P // HD], [0, HD]], channel_multiplier=-1).then_inc(s["consts"], 1)
            pool.tensor_copy(m["identb"][:, :], m["ident"][:, :]).then_inc(s["consts"], 1)
            pool.tensor_copy(m["identr"][:, :], m["ident"][:, :]).then_inc(s["consts"], 1)
            pool.iota(m["iota8"][:, :], pattern=[[1, E_]], base=0, channel_multiplier=0,
                      allow_small_or_imprecise_dtypes=True).then_inc(s["consts"], 1)
            pool.memset(m["vx"][:, :, :, HD:32], 0.0).then_inc(s["pool_step"], 1)
            pool.wait_ge(s["pool_step"], 5)
            pool.memset(m["vx"][:, :, :, HD:HD + 1], 1.0).then_inc(s["consts"], 1)

            for n, name in enumerate(pieces):
                pool.wait_ge(s["w_high"], n + 1)
                src = m["raw"][:, raw_slot(n)[0], :].rearrange("p (c n) -> p c n", c=2)
                pool.tensor_tensor(piece("L", name), src, piece("H", name).bitcast(F32),
                                   ALU.subtract).then_inc(s["w_split"], 1)

            def split_unit(u):
                slot, count = raw_slot(NSM + u)
                pool.wait_ge(s["w_loaded"][slot], count)
                if u >= NW:
                    pool.wait_ge(s["y_step"], TASKS.index((u - NW, 1)) + 1)
                else:
                    last_use(pool, u)
                src, high = m["raw"][:, slot, :], expert_weights("H", u)
                pool.tensor_copy(high, src).then_inc(s["pool_step"], 1)
                pool.wait_ge(s["pool_step"], 5 + u + 1)
                pool.tensor_tensor(expert_weights("L", u), src, high.bitcast(F32),
                                   ALU.subtract).then_inc(s["w_split"], 1)

            def mask_terms(n):
                b, i = n // NT, n % NT
                if n == 0 and K > 2:
                    filled(pool, "nd", B - 1, NT - 1)
                if n == NT and K > 2:
                    pool.wait_ge(s["max_ready"], 2 * NT)
                pool.wait_ge(s["mu_loaded"][n % 2], 16 * (n // 2 + 1))
                pool.tensor_scalar(mask_term(b, i), m["mu"][:, n % 2, 0:K * P], MASKED, None,
                                   ALU.mult).then_inc(s["mb_ready"], 1)

            def rest():
                for b in range(B):
                    for i in range(NT):
                        mask_terms(NT * b + i)
                    if b == (1 if K == 2 else 0):
                        pool.wait_ge(s["biases"], 64)
                        for t in range(B * NT):
                            filled(pool, "x1T", t // NT, NC - 1)
                            pool.tensor_tensor(m["xr"][:, t, :], m["xr"][:, t, :], m["bp"][:, :],
                                               ALU.add).then_inc(s["x1_biased"], 1)
                for u in range(NU):
                    split_unit(u)

            either(pool, rest)

        @block.scalar
        def _(act):
            steps = [0]

            def step(ins):
                ins.then_inc(s["act_step"], 1)
                steps[0] += 1
                return steps[0]

            def evacuate(name, b):
                for c in range(NC):
                    filled(act, name, b, c)
                    pt = bank(name, b, c)[:, :]
                    if name == "xnT":
                        for part in "Hf":
                            ins = act.activation(xt(part, b, c), pt, ACT.Identity, bias=m["bet"][:, c:c + 1],
                                                 scale=m["gam"][:, c:c + 1])
                        ins.then_inc(s["act_emptied"], 1)
                        continue
                    if name == "x2T":
                        act.activation(xt("f", b, c), pt, ACT.Copy).then_inc(s["x2_copied"], 1)
                    high = xt("H", b, c)
                    if name in ("aoT", "oxT"):
                        high = m["oxH"][:, c, :]
                        before = {("aoT", 1): ("ao", 0), ("oxT", 0): ("ao", 1), ("oxT", 1): ("p", 0)}
                        if (name, b) in before and c == 0:
                            filled(act, *before[name, b], NT - 1)
                    act.activation(high, pt, ACT.Copy).then_inc(s["xt_high"], 1)

            def linear_kv(b):
                for i in range(NT):
                    filled(act, "akv", b, i)
                    n = NT * b + i
                    if b and i == 0:
                        filled(act, "sum", 0, NC - 1)
                    if n == 0:
                        act.wait_ge(s["ks_ready"], 1)
                    pt = bank("akv", b, i)
                    ins = act.activation(KA[:, i, :], pt[:, 0:D], ACT.Relu, scale=-1.0)
                    wait = step(ins)
                    act.activation(V1[:, i, :, 0:P], pt[:, D:2 * D].rearrange("p (c v) -> p c v", c=NC), ACT.Copy)
                    act.wait_ge(s["act_step"], wait)
                    act.activation(KA[:, i, :], KA[:, i, :], ACT.Exp, scale=-1.0).then_inc(s["k_exp"], 1)

            def linear_q(b):
                for c in range(NC):
                    filled(act, "aq", b, c)
                    if b:
                        filled(act, "nd", 0, NT - 1)
                    act.wait_ge(s["act_step"], step(
                        act.activation(QA[:, c, :], bank("aq", b, c)[:, :], ACT.Relu, scale=-1.0)))
                    act.activation(QA[:, c, :], QA[:, c, :], ACT.Exp, scale=-1.0).then_inc(s["q_exp"], 1)

            def round_piece(n):
                slot, count = raw_slot(n)
                act.wait_ge(s["w_loaded"][slot], count)
                act.activation(piece("H", pieces[n]), m["raw"][:, slot, :].rearrange("p (c n) -> p c n", c=2),
                               ACT.Copy).then_inc(s["w_high"], 1)

            for n in range(2):
                round_piece(n)
            act.wait_ge(s["small"], 32)
            evacuate("xnT", 0)
            round_piece(2)

            def rest():
                units = [0]
                gathered = [0]

                def context(q, g):
                    filled(act, "cT", q, g)
                    n = KG * q + g
                    if n:
                        filled(act, "kv", (n - 1) // KG, 2 * ((n - 1) % KG) + 1)
                    act.activation(flat("H", "c"), bank("cT", q, g)[:, :], ACT.Copy).then_inc(s["ctx_high"], 1)

                def key_stacks(q, k):
                    for j in passes(kts, q):
                        filled(act, "kT", j, k)
                        act.activation(m["kt"][:, :, key_cols(j, k)],
                                       bank("kT", j, k)[:, :].rearrange("p (r k) -> p r k", r=NPR),
                                       ACT.Copy).then_inc(s["act_emptied"], 1)

                def mask_transposed(b):
                    for k in range(KG):
                        filled(act, "mT", b, k)
                        for a in range(2):
                            ins = act.activation(mask_term_t(b, 2 * k + a),
                                                 bank("mT", b, k)[:, :].bitcast(BF16)[:, a * S:(a + 1) * S],
                                                 ACT.Copy, scale=EASED)
                        ins.then_inc(s["act_emptied"], 1)

                def query_stacks(name, j, i):
                    filled(act, name, j, i)
                    act.activation(m["qt"][qslot(j)][:, :, i * P:(i + 1) * P],
                                   bank(name, j, i)[:, :].rearrange("p (r k) -> p r k", r=NPR),
                                   ACT.Copy).then_inc(s["act_emptied"], 1)

                def probs(j, g, k):
                    for h in range(4):
                        filled(act, "st", j, g, k, h)
                        u = units[0]
                        if u >= NP:
                            act.wait_ge(s["pv_done"], u - NP + 1)
                        elif u == NP // 2:
                            filled(act, "nd", B - 1, NT - 1)
                        act.activation(probs_at[u % NP], bank("st", j, g, k, h)[:, :], ACT.Exp,
                                       scale=SCALE).then_inc(s["act_emptied"], 1)
                        units[0] += 1

                def norm(j, g):
                    n = gathered[0]
                    act.wait_ge(s["pv_done"], 4 * K * (n + 1))
                    if n >= 2:
                        filled(act, "oN", (n - 2) // 2, (n - 2) % 2)
                    act.activation(RAW[:, n % 2, :], banks[6 + g][:, :], ACT.Copy).then_inc(s["pv_emptied"], 1)
                    gathered[0] += 1

                def round_hidden(n):
                    filled(act, "h", n)
                    if n >= 2:
                        act.wait_ge(s["h_split"], n - 1)
                    act.activation(HID[:, n % 2, :], bank("h", n)[:, :], ACT.Relu).then_inc(s["act_emptied"], 1)
                    emptied(act, "h", n)
                    if n >= 2:
                        act.wait_ge(s["y_step"], n - 1)
                    else:
                        filled(act, "st", 2 if K == 2 else 2 * B - 1, 1, K - 1, 3)
                    act.activation(HHI[:, n % 2, :], HID[:, n % 2, :], ACT.Square).then_inc(s["h_high"], 1)

                def route(b):
                    filled(act, "route", b)
                    act.activation(m["re"][:, NT * b:NT * (b + 1), :].rearrange("p t e -> p (t e)"),
                                   bank("route", b)[:, 0:NT * E_], ACT.Exp, scale=-1.0).then_inc(s["act_emptied"], 1)

                for stage, *at in schedule(kts):
                    if stage == "kv":
                        linear_kv(*at)
                    elif stage == "q":
                        linear_q(*at)
                    elif stage == "turn":
                        evacuate(*at)
                    elif stage == "round":
                        round_piece(*at)
                    elif stage == "mask":
                        mask_transposed(*at)
                    elif stage == "context":
                        context(*at)
                    elif stage == "kturn":
                        key_stacks(*at)
                    elif stage == "qturn":
                        query_stacks("qT", *at)
                    elif stage == "qturn2":
                        query_stacks("qT2", *at)
                    elif stage == "probs":
                        probs(*at)
                    elif stage == "norm":
                        norm(*at)
                    elif stage == "route":
                        route(*at)
                    elif stage == "in":
                        round_hidden(*at)

            either(act, rest, steps)

        @block.vector
        def _(dve):
            steps = [0]
            turns = [0]

            def chain(ins):
                steps[0] += 1
                ins.then_inc(s["dve_step"], 1)
                dve.wait_ge(s["dve_step"], steps[0])

            def statistics(b, rows=None):
                counts = []
                for i in range(NT + 1):
                    if i < NT:
                        counts.append(rows(i) if rows else (s["x_loaded"][NT * b + i], 16))
                    if i:
                        dve.wait_ge(*counts[i - 1])
                        ins = dve.bn_stats(m["st"][:, i - 1, :], m["xr"][:, NT * b + i - 1, :])
                chain(ins)
                for i in range(NT):
                    ins = dve.bn_aggr(m["mv"][:, i, :], m["st"][:, i, :])
                chain(ins)

            def normalise_rows(src, dst, b, ready):
                v, y, a = m["rv"][:, 0, :], m["rv"][:, 1, :], m["rv"][:, 2, :]
                chain(dve.tensor_scalar(v, m["mv"][:, :, 1], LN_EPS, None, ALU.add))
                chain(dve.tensor_scalar(y.bitcast(I32), v.bitcast(I32), -0.5, ROOT_SEED, ALU.mult, ALU.add))
                for _ in range(3):
                    chain(dve.tensor_tensor(a, y, y, ALU.mult))
                    chain(dve.scalar_tensor_tensor(out=a, in0=a, scalar=-0.5, in1=v, op0=ALU.mult, op1=ALU.mult))
                    chain(dve.scalar_tensor_tensor(out=y, in0=a, scalar=1.5, in1=y, op0=ALU.add, op1=ALU.mult))
                for i in range(NT):
                    t = NT * b + i
                    dve.tensor_scalar(dst[:, t, :], src[:, t, :], m["mv"][:, i, 0:1], m["rv"][:, 1, i:i + 1],
                                      ALU.subtract, ALU.mult).then_inc(ready, 1)

            def split_rows(name, b):
                for c in range(NC):
                    if name == "xnT":
                        emptied(dve, name, b, c)
                        dve.tensor_tensor(xt("L", b, c), xt("f", b, c), xt("H", b, c).bitcast(F32),
                                          ALU.subtract).then_inc(s["xt_split"], 1)
                        continue
                    turns[0] += 1
                    dve.wait_ge(s["xt_high"], turns[0])
                    if name in ("aoT", "oxT"):
                        high, low, done = m["oxH"][:, c, :], m["oxL"][:, c, :], s["ox_split"]
                    else:
                        high, low, done = xt("H", b, c), xt("L", b, c), s["xt_split"]
                    dve.tensor_tensor(low, bank(name, b, c)[:, :], high.bitcast(F32), ALU.subtract).then_inc(done, 1)

            def linear_kv(b):
                for i in range(NT):
                    dve.wait_ge(s["k_exp"], NT * b + i + 1)
                    dve.scalar_tensor_tensor(out=KA[:, i, :], in0=bank("akv", b, i)[:, 0:D], scalar=0.0,
                                             in1=KA[:, i, :], op0=ALU.max, op1=ALU.add
                                             ).then_inc(s["dve_emptied"], 1)

            def linear_sums(b):
                if b:
                    filled(dve, "nd", 0, NT - 1)
                for c in range(NC):
                    filled(dve, "sum", b, c)
                    pt = bank("sum", b, c)
                    dve.tensor_tensor(KVS[:, c, 0:P], pt[:, 0:P], m["blocks"][:, :], ALU.mult)
                    dve.tensor_scalar(KVS[:, c, P:P + HH],
                                      m["blocks"][:, :].rearrange("p (h e) -> p h e", e=HD)[:, :, 0],
                                      pt[:, P:P + 1], None, ALU.mult).then_inc(s["dve_emptied"], 1)

            def linear_q(b):
                for c in range(NC):
                    dve.wait_ge(s["q_exp"], NC * b + c + 1)
                    dve.scalar_tensor_tensor(out=QA[:, c, :], in0=bank("aq", b, c)[:, :], scalar=0.0,
                                             in1=QA[:, c, :], op0=ALU.max, op1=ALU.add
                                             ).then_inc(s["dve_emptied"], 1)

            def linear_out(b):
                if b:
                    filled(dve, "aoT", 0, NC - 1)
                for i in range(NT):
                    filled(dve, "nd", b, i)
                    pt = bank("nd", b, i)[:, 0:NC * 136].rearrange("p (c v) -> p c v", c=NC)
                    rd = m["rd"][:, i % 2, :].rearrange("p (c h) -> p c h", c=NC)
                    chain(dve.tensor_scalar(rd, pt[:, :, P:P + HH], DEN_EPS, None, ALU.add))
                    chain(dve.reciprocal(rd, rd))
                    dve.tensor_tensor(ON[:, i, :].rearrange("p (c h e) -> p c h e", c=NC, e=HD),
                                      pt[:, :, 0:P].rearrange("p c (h e) -> p c h e", e=HD),
                                      rd.unsqueeze(3).broadcast_to([P, NC, HH, HD]),
                                      ALU.mult).then_inc(s["dve_emptied"], 1)

            chain(dve.memset(m["mk"][:, :, :, 3 * HD:STK].bitcast(F32), 0.0))
            dve.memset(m["mq"][0][:, :, :, 3 * HD:STK].bitcast(F32), 0.0)
            chain(dve.memset(m["mk"][:, :, :, 3 * HD:3 * HD + 2].bitcast(F32), 1.0))

            def enter(b):
                statistics(b)
                normalise_rows(m["xr"], XN, b, s["xn_ready"])

            enter(0)
            dve.wait_ge(s["mask_loaded"], 16)
            dve.tensor_reduce(m["least"][:, 0:1], MALL.bitcast(U16), AX.X, ALU.min).then_inc(s["mask_least"], 1)
            split_rows("xnT", 0)
            dve.wait_ge(s["least_turned"], 1)
            chain(dve.tensor_reduce(m["least"][0:1, 0:1], banks[7][0:1, 0:P], AX.X, ALU.min))
            dve.tensor_scalar(m["flag"][0:1, 0:1], m["least"][0:1, 0:1], 257.0, None,
                              ALU.is_equal).then_inc(s["flag_ready"], 1)
            dve.memset(V1[:, :, :, P:P + 1], 1.0).then_inc(s["ks_ready"], 1)
            dve.wait_ge(s["consts"], 5)

            def attended(b):
                def rows(i):
                    t = NT * b + i
                    filled(dve, "ao", b, i)
                    dve.scalar_tensor_tensor(out=m["xr"][:, t, :], in0=m["xr"][:, t, :], scalar=2.0,
                                             in1=bank("ao", b, i)[:, 0:D], op0=ALU.mult, op1=ALU.add
                                             ).then_inc(s["dve_emptied"], 1)
                    return s["dve_emptied"], readers["ao", b, i][1]

                statistics(b, rows)
                normalise_rows(m["xr"], m["xr"], b, s["x1_ready"])

            def rest():
                kvs = [0]
                stacks = [(j, x[2]) for x in schedule(kts) if x[0] == "keys" for j in passes(kts, x[1])]

                def context(q, g):
                    dve.wait_ge(s["ctx_high"], KG * q + g + 1)
                    dve.tensor_tensor(flat("L", "c"), bank("cT", q, g)[:, :], flat("H", "c").bitcast(F32),
                                      ALU.subtract).then_inc(s["ctx_split"], 1)

                def keys(q, k):
                    if q == 0 and k == 0:
                        dve.wait_ge(s["biases"], 64)
                    filled(dve, "kv", q, k)
                    for n, j in enumerate(passes(kts, q)):
                        key_stack(j, k, bank("kv", q, k)[:, n * 2 * P:(n + 1) * 2 * P],
                                  j == passes(kts, q)[-1], ("kv", q, k))

                def key_stack(j, k, pt, last, tile):
                    cols = slice((j % 2) * P, (j % 2 + 1) * P)
                    kf = m["kf"][:, kvs[0] % 2, :]
                    if kvs[0] >= 2:
                        dve.wait_ge(s["k_stacked"], kvs[0] - 1)
                    dve.tensor_tensor(kf, pt[:, 0:P], m["bk"][:, cols], ALU.add)
                    values = dve.tensor_tensor(m["vx"][:, value_tile(j, k), :, 0:HD],
                                               pt[:, P:2 * P].rearrange("p (h e) -> p h e", e=HD),
                                               m["bv"][:, cols].rearrange("p (h e) -> p h e", e=HD), ALU.add)
                    if last:
                        values.then_inc(s["dve_emptied"], 1)
                        emptied(dve, *tile)
                    else:
                        chain(values)
                    mk = m["mk"][:, kvs[0] % 2, :, :]
                    if kvs[0] >= 2:
                        filled(dve, "kT", *stacks[kvs[0] - 2])
                    kv3 = kf.rearrange("p (h e) -> p h e", e=HD)
                    both = mk.rearrange("p h (r a e) -> p h r a e", r=2, a=2)[:, :, :, 0, :]
                    chain(dve.tensor_copy(both, kv3.unsqueeze(2).broadcast_to([P, HH, 2, HD])))
                    dve.tensor_tensor(mk[:, :, HD:2 * HD], kv3, mk[:, :, 0:HD].bitcast(F32),
                                      ALU.subtract).then_inc(s["k_stacked"], 1)
                    kvs[0] += 1

                def query(j):
                    cols = slice((j % 2) * P, (j % 2 + 1) * P)
                    if j == 1 and K == 2:
                        filled(dve, "ao", B - 1, NT - 1)
                        chain(dve.memset(m["mq"][1][:, :, :, 3 * HD:STK].bitcast(F32), 0.0))
                    filled(dve, "q", j)
                    if j:
                        dve.wait_ge(s["q_stacked"], j)
                    chain(dve.tensor_tensor(m["qf"][:, :, :], bank("q", j)[:, :].rearrange("p (i n) -> p i n", i=NT),
                                            m["bq"][:, cols].unsqueeze(1).broadcast_to([P, NT, P]), ALU.add))
                    back = 2 if K == 2 else 1
                    if j >= back:
                        filled(dve, "qT2", j - back, NT - 1)
                    q3 = m["qf"][:, :, :].rearrange("p i (h e) -> p (i h) e", e=HD)
                    mq = m["mq"][qslot(j)].rearrange("p i h k -> p (i h) k")
                    both = mq[:, :, 0:2 * HD].rearrange("p h (r e) -> p h r e", r=2)
                    chain(dve.tensor_copy(both, q3.unsqueeze(2).broadcast_to([P, NT * HH, 2, HD])))
                    dve.tensor_tensor(mq[:, :, 2 * HD:3 * HD], q3, mq[:, :, 0:HD].bitcast(F32),
                                      ALU.subtract).then_inc(s["q_stacked"], 1)

                def maxima(j, i):
                    dve.wait_ge(s["mb_ready"], NT * (j // 2 + 1))
                    for n in range(HH * K // 4):
                        filled(dve, "smax", j, i, n)
                        for h, c, cols in score_parts(n):
                            pt = bank("smax", j, i, n)[:, cols]
                            ins = dve.tensor_tensor_reduce(pt, pt, mask_term(j // 2, i)[:, c * SN:(c + 1) * SN],
                                                           1.0, -3e38, ALU.add, ALU.max,
                                                           m["mx"][:, i, h, c:c + 1])
                        ins.then_inc(s["dve_emptied"], 1)
                    emptied(dve, "smax", j, i, HH * K // 4 - 1)
                    mx = m["mx"][:, i, :, 0]
                    if NS > 1:
                        chain(dve.tensor_tensor(mx, mx, m["mx"][:, i, :, 1], ALU.max))
                    mq = m["mq"][qslot(j)][:, i, :, :]
                    chain(dve.tensor_scalar(mq[:, :, 3 * HD], mx, -1.0, None, ALU.mult))
                    dve.scalar_tensor_tensor(out=mq[:, :, 3 * HD + 1], in0=mx, scalar=-1.0,
                                             in1=mq[:, :, 3 * HD].bitcast(F32), op0=ALU.mult,
                                             op1=ALU.subtract).then_inc(s["max_ready"], 1)

                def norm(j, g):
                    filled(dve, "oN", j, g)
                    if g == 0 and j % 2 == 0:
                        filled(dve, *(("oxT", 0) if j else ("aoT", 1)), NC - 1)
                    pt = bank("oN", j, g)[:, :].rearrange("p (i h v) -> p i h v", i=NT, h=4)
                    rd = m["rd"][:, g, :].rearrange("p (i h) -> p i h", i=NT)
                    chain(dve.reciprocal(rd, pt[:, :, :, HD]))
                    q = 2 * (j % 2) + g
                    dve.tensor_tensor(ON[:, :, q * 4 * HD:(q + 1) * 4 * HD].rearrange("p i (h e) -> p i h e", e=HD),
                                      pt[:, :, :, 0:HD], rd.unsqueeze(3).broadcast_to([P, NT, 4, HD]),
                                      ALU.mult).then_inc(s["dve_emptied"], 1)

                def project(b):
                    def rows(i):
                        t = NT * b + i
                        filled(dve, "p", b, i)
                        dve.wait_ge(s["x1_biased"], t + 1)
                        dve.tensor_tensor(m["xr"][:, t, :], m["xr"][:, t, :], bank("p", b, i)[:, 0:D],
                                          ALU.add).then_inc(s["dve_emptied"], 1)
                        return s["dve_emptied"], readers["p", b, i][1]

                    statistics(b, rows)

                def shares(b):
                    rows = slice(NT * b, NT * (b + 1))
                    emptied(dve, "route", b)
                    re, top, idxf, wsum, comb = (m[x][:, rows, :] for x in ("re", "top", "idxf", "wsum", "comb"))
                    chain(dve.tensor_scalar(re, re, 1.0, None, ALU.add))
                    chain(dve.reciprocal(re, re))
                    for t in range(NT * b, NT * (b + 1)):
                        ins = dve.max(m["top"][:, t, :], m["re"][:, t, :])
                    chain(ins)
                    for t in range(NT * b, NT * (b + 1)):
                        ins = dve.max_index(m["idx"][:, t, :], m["top"][:, t, :], m["re"][:, t, :])
                    chain(ins)
                    chain(dve.tensor_copy(idxf, m["idx"][:, rows, :]))
                    chain(dve.tensor_tensor(wsum, top[:, :, 0:1], top[:, :, 1:2], ALU.add))
                    chain(dve.tensor_scalar(wsum, wsum, 1e-20, None, ALU.add))
                    chain(dve.reciprocal(wsum, wsum))
                    chain(dve.tensor_tensor(top[:, :, 0:2], top[:, :, 0:2], wsum.broadcast_to([P, NT, 2]), ALU.mult))
                    places = m["iota8"][:, :].unsqueeze(1).broadcast_to([P, NT, E_])
                    hot = m["hot"][:, :, :]
                    for k, dst in ((0, hot), (1, comb)):
                        chain(dve.tensor_tensor(dst, places, idxf[:, :, k:k + 1].broadcast_to([P, NT, E_]),
                                                ALU.is_equal))
                        chain(dve.tensor_tensor(dst, dst, top[:, :, k:k + 1].broadcast_to([P, NT, E_]), ALU.mult))
                    chain(dve.tensor_tensor(comb, comb, hot, ALU.add))

                def hidden_low(n):
                    emptied(dve, "h", n)
                    chain(dve.tensor_tensor(HLOW[:, n % 2, :], HID[:, n % 2, :], HID[:, n % 2, :], ALU.mult))
                    dve.wait_ge(s["h_high"], n + 1)
                    if n >= 2:
                        dve.wait_ge(s["y_step"], n - 1)
                    dve.tensor_tensor(HLO[:, n % 2, :], HLOW[:, n % 2, :], HHI[:, n % 2, :].bitcast(F32),
                                      ALU.subtract).then_inc(s["h_split"], 1)

                def gather(e, b):
                    dve.wait_ge(s["y_step"], TASKS.index((UNITS.index((e, LAST[e])), b)) + 1)
                    for i in range(NT):
                        t = NT * b + i
                        if gathers[0] >= NT:
                            dve.wait_ge(s["y_emptied"], gathers[0] - NT + 1)
                        gathers[0] += 1
                        y_read[e, t] = gathers[0]
                        dve.scalar_tensor_tensor(out=m["xr"][:, t, :],
                                                 in0=banks[4 + t // 2][:, (t % 2) * D:(t % 2 + 1) * D],
                                                 scalar=m["comb"][:, t, e:e + 1], in1=m["xr"][:, t, :],
                                                 op0=ALU.mult, op1=ALU.add).then_inc(s["y_emptied"], 1)

                def finish(b, part):
                    if part == 0:
                        statistics(b, lambda i: (s["y_emptied"], y_read[E_ - 1, NT * b + i]))
                    else:
                        normalise_rows(m["xr"], m["xr"], b, s["out_ready"])

                gathers, y_read = [0], {}
                for stage, *at in schedule(kts):
                    if stage == "kv":
                        linear_kv(*at)
                    elif stage == "sum":
                        linear_sums(*at)
                    elif stage == "q":
                        linear_q(*at)
                    elif stage == "linear":
                        linear_out(*at)
                    elif stage == "turn":
                        split_rows(*at)
                    elif stage == "attended":
                        attended(*at)
                    elif stage == "enter":
                        enter(*at)
                    elif stage == "context":
                        context(*at)
                    elif stage == "keys":
                        keys(*at)
                    elif stage == "query":
                        query(*at)
                    elif stage == "maxima":
                        maxima(*at)
                    elif stage == "norm":
                        norm(*at)
                    elif stage == "project":
                        project(*at)
                    elif stage == "settle":
                        normalise_rows(m["xr"], m["xr"], at[0], s["x2_ready"])
                    elif stage == "shares":
                        shares(*at)
                    elif stage == "in":
                        hidden_low(*at)
                    elif stage == "add":
                        gather(*at)
                    elif stage == "finish":
                        finish(*at)

            either(dve, rest, steps, turns)

        @block.tensor
        def _(pe):
            order = [0]

            def claim(*key):
                bk, n, before = tiles[key]
                order[0] += 1
                assert n == order[0], key
                if before is not None:
                    emptied(pe, *before)
                return banks[bk]

            def three(out, pairs, stop=True, start=True):
                todo = [(a, b, x, y) for a, b in pairs for x, y in (("H", "H"), ("H", "L"), ("L", "H"))]
                for n, (a, b, x, y) in enumerate(todo):
                    ins = pe.matmul(out, a(x), b(y), start=start and n == 0, stop=stop and n == len(todo) - 1)
                return ins

            def transposed(name, b):
                src, ready, count = {"xnT": (XN, "xn_ready", NT * (b + 1)),
                                     "aoT": (ON, None, 0), "x1T": (m["xr"], "x1_ready", NT * (b + 1)),
                                     "oxT": (ON, None, 0), "x2T": (m["xr"], "x2_ready", NT * (b + 1))}[name]
                if ready:
                    pe.wait_ge(s[ready], count)
                elif name == "aoT":
                    emptied(pe, "nd", b, NT - 1)
                else:
                    emptied(pe, "oN", 2 * b + 1, 1)
                for c in range(NC):
                    pt = claim(name, b, c)
                    for i in range(NT):
                        t = i if ready is None else NT * b + i
                        ins = pe.transpose(pt[:, i * P:(i + 1) * P], src[:, t, c * P:(c + 1) * P],
                                           m["ident"][:, :])
                    ins.then_inc(s["filled"], 1)

            def xtile(b, c, i):
                return lambda part: m["xt" + part][:, b, c, i * P:(i + 1) * P]

            def linear_kv(b):
                pe.wait_ge(s["w_split"], PIECE["wqkv2"])
                pe.wait_ge(s["xt_split"], NC * (b + 1))
                for i in range(NT):
                    pt = claim("akv", b, i)
                    three(pt[:, :], [(xtile(b, c, i), lambda p, c=c: m["wqkv" + p][:, c, D:3 * D])
                                     for c in range(NC)]).then_inc(s["filled"], 1)

            def linear_sums(b):
                for i in range(NT):
                    emptied(pe, "akv", b, i)
                pe.wait_ge(s["ks_ready"], 1)
                for c in range(NC):
                    pt = claim("sum", b, c)
                    for i in range(NT):
                        ins = pe.matmul(pt[:, 0:P + 1], KA[:, i, c * P:(c + 1) * P], V1[:, i, c, 0:P + 1],
                                        start=(i == 0), stop=(i == NT - 1))
                    ins.then_inc(s["filled"], 1)

            def linear_q(b):
                pe.wait_ge(s["w_split"], PIECE["wqkv0"])
                for c in range(NC):
                    pt = claim("aq", b, c)
                    three(pt[:, :], [(lambda p, a=a, c=c: m["wqkv" + p][:, a, c * P:(c + 1) * P],
                                      lambda p, a=a: xt(p, b, a)) for a in range(NC)]).then_inc(s["filled"], 1)

            def linear_out(b):
                emptied(pe, "sum", b, NC - 1)
                emptied(pe, "aq", b, NC - 1)
                for i in range(NT):
                    pt = claim("nd", b, i)
                    for c in range(NC):
                        ins = pe.matmul(pt[:, c * 136:(c + 1) * 136], QA[:, c, i * P:(i + 1) * P], KVS[:, c, :],
                                        start=True, stop=True)
                    ins.then_inc(s["filled"], 1)

            def attended(b):
                pe.wait_ge(s["w_split"], PIECE["wout"])
                emptied(pe, "aoT", b, NC - 1)
                for i in range(NT):
                    pt = claim("ao", b, i)
                    three(pt[:, 0:D], [(lambda p, c=c: m["ox" + p][:, c, i * P:(i + 1) * P],
                                        lambda p, c=c: m["wout" + p][:, c, :]) for c in range(NC)]
                          ).then_inc(s["filled"], 1)

            def mask_transposed(b):
                pe.wait_ge(s["mb_ready"], NT * (b + 1))
                for k in range(KG):
                    pt = claim("mT", b, k)[:, :].bitcast(BF16)
                    for a in range(2):
                        for i in range(NT):
                            ins = pe.transpose(pt[:, a * S + i * P:a * S + (i + 1) * P],
                                               mask_term(b, i)[:, (2 * k + a) * P:(2 * k + a + 1) * P],
                                               m["identb"][:, :])
                    ins.then_inc(s["filled"], 1)

            pe.wait_ge(s["consts"], 5)
            def keep_warm(steps):
                for _ in range(steps):
                    pe.matmul(banks[6][:, 0:P], m["identb"][:, :], m["identb"][:, :], start=True, stop=True)

            keep_warm(WARM_UP[0])
            transposed("xnT", 0)
            keep_warm(WARM_UP[1])
            pe.wait_ge(s["mask_least"], 1)
            pe.transpose(banks[7][0:1, 0:P], m["least"][:, 0:1], m["ident"][:, :]).then_inc(s["least_turned"], 1)
            keep_warm(WARM_UP[2])

            def rest():
                units = [0, 0]
                kvs = [0]
                ctxs = [0]

                def turn_stack(key, stack):
                    pt = claim(*key)
                    for r in range(NPR):
                        ins = pe.transpose(pt[:, r * P:(r + 1) * P].bitcast(F32R),
                                           stack[:, 2 * r:2 * r + 2, :].rearrange("p a b -> p (a b)"),
                                           m["identr"][:, :])
                    ins.then_inc(s["filled"], 1)

                def turn_context(j, g):
                    n = ctxs[0]
                    pe.wait_ge(s["cx_loaded"][n % 2], 16 * (n // 2 + 1))
                    ctxs[0] += 1
                    pt = claim("cT", j, g)
                    for c in range(NC):
                        for k in range(2):
                            ins = pe.transpose(pt[:, (2 * c + k) * P:(2 * c + k + 1) * P],
                                               m["cx"][:, n % 2, k, c * P:(c + 1) * P], m["ident"][:, :])
                    ins.then_inc(s["filled"], 1)

                def turn_keys(q, k):
                    for j in passes(kts, q):
                        pe.wait_ge(s["k_stacked"], kvs[0] + 1)
                        turn_stack(("kT", j, k), m["mk"][:, kvs[0] % 2, :, :])
                        kvs[0] += 1

                def keys(q, k):
                    pe.wait_ge(s["w_split"], PIECE["wkv1"])
                    emptied(pe, "cT", q, k // 2)
                    f, n = passes(kts, q)[0] % 2, len(passes(kts, q))
                    pt = claim("kv", q, k)
                    three(pt[:, 0:2 * P * n], [(lambda p, c=c: m["c" + p][:, c, (k % 2) * P:(k % 2 + 1) * P],
                                                lambda p, c=c: m["wkv" + p][:, c, f:f + n, :, :].rearrange(
                                                    "p f a n -> p (f a n)")) for c in range(NC)]
                          ).then_inc(s["filled"], 1)

                def query(j):
                    b, f = j // 2, j % 2
                    pe.wait_ge(s["w_split"], PIECE["wq"])
                    emptied(pe, "x1T", b, NC - 1)
                    pt = claim("q", j)
                    for i in range(NT):
                        ins = three(pt[:, i * P:(i + 1) * P],
                                    [(xtile(b, c, i), lambda p, c=c: m["wq" + p][:, c, f * P:(f + 1) * P])
                                     for c in range(NC)])
                    ins.then_inc(s["filled"], 1)

                def turn_queries(j, i):
                    emptied(pe, "q", j)
                    turn_stack(("qT", j, i), m["mq"][qslot(j)][:, i, :, :])

                def maxima(j, i):
                    emptied(pe, "kT", j, K - 1)
                    emptied(pe, "qT", j, i)
                    for n in range(HH * K // 4):
                        pt = claim("smax", j, i, n)
                        for h, c, cols in score_parts(n):
                            rows = slice(STK * (h % 2), STK * (h % 2) + 3 * HD)
                            ins = pe.matmul(pt[:, cols], m["qt"][qslot(j)][rows, h // 2, i * P:(i + 1) * P],
                                            m["kt"][rows, h // 2, key_cols(j, c * SN // P, SN)], start=True,
                                            stop=True)
                        ins.then_inc(s["filled"], 1)

                def turn_queries_again(j, i):
                    pe.wait_ge(s["max_ready"], NT * j + i + 1)
                    turn_stack(("qT2", j, i), m["mq"][qslot(j)][:, i, :, :])

                def probs(j, g, k):
                    emptied(pe, "qT2", j, NT - 1)
                    emptied(pe, "mT", j // 2, KG - 1)
                    for h in range(4):
                        head = 4 * g + h
                        rows = slice(STK * (head % 2), STK * (head % 2) + STK)
                        pt = claim("st", j, g, k, h)
                        pe.matmul(pt[:, :], m["kt"][rows, head // 2, key_cols(j, k)],
                                  m["qt"][qslot(j)][rows, head // 2, :], start=True, stop=False)
                        pe.matmul(pt[:, :], m["identb"][:, :], mask_term_t(j // 2, k), start=False,
                                  stop=True).then_inc(s["filled"], 1)

                def values(j, g, k):
                    if k == 0 and 2 * j + g >= 2:
                        pe.wait_ge(s["pv_emptied"], 2 * j + g - 1)
                    for h in range(4):
                        emptied(pe, "st", j, g, k, h)
                        pe.matmul(banks[6 + g][32 * h:32 * h + 32, :], m["vx"][:, value_tile(j, k), 4 * g + h, :],
                                  probs_at[units[0] % NP], start=(k == 0),
                                  stop=(k == K - 1)).then_inc(s["pv_done"], 1)
                        units[0] += 1

                def norm(j, g):
                    n = 2 * j + g
                    pe.wait_ge(s["pv_emptied"], n + 1)
                    pt = claim("oN", j, g)
                    for i in range(NT):
                        ins = pe.transpose(pt[:, i * P:(i + 1) * P], RAW[:, n % 2, i * P:(i + 1) * P],
                                           m["ident"][:, :])
                    ins.then_inc(s["filled"], 1)

                def project(b):
                    pe.wait_ge(s["w_split"], PIECE["wp"])
                    emptied(pe, "oxT", b, NC - 1)
                    for i in range(NT):
                        pt = claim("p", b, i)
                        three(pt[:, 0:D], [(lambda p, c=c: m["ox" + p][:, c, i * P:(i + 1) * P],
                                            lambda p, c=c: m["wp" + p][:, c, :]) for c in range(NC)]
                              ).then_inc(s["filled"], 1)

                def route(b):
                    pe.wait_ge(s["rw_loaded"], 32)
                    pe.wait_ge(s["x2_copied"], NC * (b + 1))
                    pt = claim("route", b)
                    for i in range(NT):
                        for c in range(NC):
                            ins = pe.matmul(pt[:, i * E_:(i + 1) * E_], m["xtf"][:, b, c, i * P:(i + 1) * P],
                                            m["rw"][:, c, :], start=(c == 0), stop=(c == NC - 1))
                    ins.then_inc(s["filled"], 1)

                def expert_in(n):
                    u, b = TASKS[n]
                    pe.wait_ge(s["w_split"], NSM + u + 1)
                    emptied(pe, "x2T", b, NC - 1)
                    pt = claim("h", n)
                    three(pt[:, :], [(lambda p, c=c: expert_weights(p, u)[:, c * P:(c + 1) * P],
                                      lambda p, c=c: xt(p, b, c)) for c in range(NC)]).then_inc(s["filled"], 1)

                def expert_out(n):
                    u, b = TASKS[n]
                    e, k = UNITS[u]
                    pe.wait_ge(s["h_split"], n + 1)
                    if u == 0:
                        if b == 0:
                            for kk in (4, 5):
                                emptied(pe, *before_y[kk])
                        else:
                            pe.wait_ge(s["pv_emptied"], 8)
                    for i in range(NT):
                        t = NT * b + i
                        y = banks[4 + t // 2][:, (t % 2) * D:(t % 2 + 1) * D]
                        if k == 0 and e:
                            pe.wait_ge(s["y_emptied"], y_read[e - 1, b] + 2 * (i // 2) + 2)
                        for p, (x_, y_) in enumerate((("H", "H"), ("H", "L"), ("L", "H"))):
                            ins = pe.matmul(y, {"H": HHI, "L": HLO}[x_][:, n % 2, i * P:(i + 1) * P],
                                            expert_weights(y_, u)[:, D:2 * D],
                                            start=(k == 0 and p == 0 and t % 2 == 0),
                                            stop=(k == LAST[e] and p == 2), skip_group_check=True)
                    ins.then_inc(s["y_step"], 1)

                adds = [tuple(x[1:]) for x in schedule(kts) if x[0] == "add"]
                y_read = {x: NT * n for n, x in enumerate(adds)}
                for stage, *at in schedule(kts):
                    if stage == "kv":
                        linear_kv(*at)
                    elif stage == "sum":
                        linear_sums(*at)
                    elif stage == "q":
                        linear_q(*at)
                    elif stage == "linear":
                        linear_out(*at)
                    elif stage == "turn":
                        transposed(*at)
                    elif stage == "attended":
                        attended(*at)
                    elif stage == "mask":
                        mask_transposed(*at)
                    elif stage == "context":
                        turn_context(*at)
                    elif stage == "keys":
                        keys(*at)
                    elif stage == "kturn":
                        turn_keys(*at)
                    elif stage == "query":
                        query(*at)
                    elif stage == "qturn":
                        turn_queries(*at)
                    elif stage == "maxima":
                        maxima(*at)
                    elif stage == "qturn2":
                        turn_queries_again(*at)
                    elif stage == "probs":
                        probs(*at)
                    elif stage == "values":
                        values(*at)
                    elif stage == "norm":
                        norm(*at)
                    elif stage == "project":
                        project(*at)
                    elif stage == "route":
                        route(*at)
                    elif stage == "in":
                        expert_in(*at)
                    elif stage == "out":
                        expert_out(*at)

            either(pe, rest, order)


_INS = ["x", "ctx_1024", "mask_Bx1xSxS2_bk1", "L0_attn_gamma", "L0_attn_beta", "L0_attn_Wqkv", "L0_attn_Wout",
        "L0_xattn_Wq", "L0_xattn_bq", "L0_xattn_Wk", "L0_xattn_bk", "L0_xattn_Wv", "L0_xattn_bv",
        "L0_xattn_Wp", "L0_xattn_bp", "L0_ffn_router_w", "L0_ffn_w1", "L0_ffn_w2"]


def kernel(**inputs):
    import concourse.bacc as _bacc
    from concourse.bass_utils import run_bass_kernel_spmd as _run

    nc = _bacc.Bacc("TRN2", target_bir_lowering=False, num_devices=1)
    arrays, args = {}, []
    for name in _INS:
        a = np.ascontiguousarray(inputs[name])
        arrays[f"in_{name}"] = a
        args.append(nc.dram_tensor(f"in_{name}", a.shape, mybir.dt.from_np(a.dtype), kind="ExternalInput").ap())
    args.append(nc.dram_tensor("out", (B, S, D), F32, kind="ExternalOutput").ap())
    decoder_layer(nc, *args)
    r = _run(nc, [arrays], core_ids=[0])
    return r.results[0]["out"]
```
